# Optimizing a Trainium2 kernel written in Bass

```python
import numpy as np
import jax
import jax.numpy as jnp

def _softmax(x, axis=-1):
    return jax.nn.softmax(x, axis=axis)

def _gelu(x):
    return jax.nn.gelu(x, approximate=True)

def _silu(x):
    return jax.nn.silu(x)

def _sigmoid(x):
    return jax.nn.sigmoid(x)

def _layernorm(x, axis=-1, eps=1e-05):
    m = jnp.mean(x, axis=axis, keepdims=True)
    v = jnp.var(x, axis=axis, keepdims=True)
    return (x - m) / jnp.sqrt(v + eps)

def _scatter_add(tgt, idx, src, axis=0):
    return tgt.at[idx].add(src)

def _segment_sum(src, seg, n):
    return jax.ops.segment_sum(src, seg, n)
kernel_name = 'mk_recurrent_d2_jaxref_r8_3b1c8c'

def setup_inputs(seed: int=0):
    np.random.seed(seed)
    _w = jnp.asarray

    def _L0_attn_setup():
        import jax, jax.numpy as jnp
        import numpy as np
        D_MODEL = 128
        D_STATE = 16
        D_CONV = 4
        EXPAND = 2
        D_INNER = D_MODEL * EXPAND

        def soft_clamp(x, lo, hi, sharp):
            c = (hi + lo) / 2.0
            r = (hi - lo) / 2.0
            return jnp.tanh((x - c) / (r + 1e-08) * sharp) / sharp * r + c
        key = jax.random.key(seed)
        ks = jax.random.split(key, 9)
        B, L = (2, 128)
        x = jax.random.normal(ks[0], (B, L, D_MODEL), jnp.float32)
        norm_w = jnp.ones((D_MODEL,), jnp.float32)
        W_in = jax.random.normal(ks[1], (2 * D_INNER, D_MODEL), jnp.float32) * 0.02
        conv_w = jax.random.normal(ks[2], (D_INNER, 1, D_CONV), jnp.float32) * 0.02
        conv_b = jnp.zeros((D_INNER,), jnp.float32)
        W_dt = jax.random.normal(ks[3], (D_INNER, D_INNER), jnp.float32) * 0.02
        b_dt = jnp.full((D_INNER,), -2.0, jnp.float32)
        W_B = jax.random.normal(ks[4], (D_STATE, D_INNER), jnp.float32) * 0.02
        W_C = jax.random.normal(ks[5], (D_STATE, D_INNER), jnp.float32) * 0.02
        A_log = jax.random.normal(ks[6], (D_INNER, D_STATE), jnp.float32) * 0.1
        D_param = jnp.full((D_INNER,), 0.1, jnp.float32)
        W_out = jax.random.normal(ks[7], (D_MODEL, D_INNER), jnp.float32) * 0.02
        residual_scale = jnp.asarray(0.3, jnp.float32)
        return dict(x=x, norm_w=norm_w, W_in=W_in, conv_w=conv_w, conv_b=conv_b, W_dt=W_dt, b_dt=b_dt, W_B=W_B, W_C=W_C, A_log=A_log, D_param=D_param, W_out=W_out, residual_scale=residual_scale)
    _L0_attn_in = _L0_attn_setup()

    def _L0_ffn_setup():
        import jax, jax.numpy as jnp
        import numpy as np
        B, S, H = (1, 256, 128)
        E, K = (16, 4)
        G, TG = (4, 2)
        I_MOE = 64
        N_SH = 2
        SCALE = 2.5

        def _mlp(x, gw, uw, dw):
            return jax.nn.silu(x @ gw.T) * (x @ uw.T) @ dw.T

        def _route(x2d, router_weight, e_bias):
            T = x2d.shape[0]
            scores = jax.nn.sigmoid(x2d @ router_weight.T)
            sc = scores + e_bias[None, :]
            group_scores = jnp.sum(jax.lax.top_k(sc.reshape(T, G, E // G), 2)[0], axis=-1)
            _, gidx = jax.lax.top_k(group_scores, TG)
            gmask = jnp.zeros((T, G), sc.dtype).at[jnp.arange(T)[:, None], gidx].set(1.0)
            smask = jnp.repeat(gmask, E // G, axis=1)
            masked = jnp.where(smask > 0, sc, 0.0)
            _, tidx = jax.lax.top_k(masked, K)
            tw = jnp.take_along_axis(scores, tidx, axis=1)
            tw = tw / (jnp.sum(tw, axis=-1, keepdims=True) + 1e-20)
            tw = tw * SCALE
            return (tidx, tw)

        def _moe_forward(hidden_states, router_weight, e_bias, gate_w, up_w, down_w, sh_gate_w, sh_up_w, sh_down_w):
            orig_shape = hidden_states.shape
            x = hidden_states.reshape(-1, H)
            T = x.shape[0]
            tidx, tw = _route(x, router_weight, e_bias)
            g = jnp.einsum('th,eih->tei', x, gate_w)
            u = jnp.einsum('th,eih->tei', x, up_w)
            h = jax.nn.silu(g) * u
            yo = jnp.einsum('tei,ehi->teh', h, down_w)
            combine = jnp.zeros((T, E), tw.dtype).at[jnp.arange(T)[:, None], tidx].add(tw)
            routed = jnp.einsum('te,teh->th', combine, yo)
            shared = _mlp(hidden_states.reshape(-1, H), sh_gate_w, sh_up_w, sh_down_w)
            return (routed + shared).reshape(orig_shape)
        key = jax.random.key(seed)
        ks = jax.random.split(key, 9)
        s = 0.02
        return {'hidden_states': jax.random.normal(ks[0], (B, S, H), jnp.float32), 'router_weight': jax.random.normal(ks[1], (E, H), jnp.float32) * s, 'e_bias': jnp.zeros((E,), jnp.float32), 'gate_w': jax.random.normal(ks[2], (E, I_MOE, H), jnp.float32) * s, 'up_w': jax.random.normal(ks[3], (E, I_MOE, H), jnp.float32) * s, 'down_w': jax.random.normal(ks[4], (E, H, I_MOE), jnp.float32) * s, 'sh_gate_w': jax.random.normal(ks[5], (N_SH * I_MOE, H), jnp.float32) * s, 'sh_up_w': jax.random.normal(ks[6], (N_SH * I_MOE, H), jnp.float32) * s, 'sh_down_w': jax.random.normal(ks[7], (H, N_SH * I_MOE), jnp.float32) * s}
    _L0_ffn_in = _L0_ffn_setup()

    def _L1_attn_setup():
        import jax, jax.numpy as jnp
        import numpy as np
        EMBED_DIM = 128
        NUM_HEADS = 16
        CHUNK = 32

        def _mha_residual(x, Wq, Wk, Wv, Wo, num_heads):
            *lead, S, D = x.shape
            hd = D // num_heads
            scale = 1.0 / jnp.sqrt(jnp.asarray(hd, x.dtype))
            q = (x @ Wq).reshape(*lead, S, num_heads, hd)
            k = (x @ Wk).reshape(*lead, S, num_heads, hd)
            v = (x @ Wv).reshape(*lead, S, num_heads, hd)
            scores = jnp.einsum('...qhe,...khe->...hqk', q, k) * scale
            attn = jax.nn.softmax(scores, axis=-1)
            ctx = jnp.einsum('...hqk,...khe->...qhe', attn, v)
            ctx = ctx.reshape(*lead, S, D)
            return x + ctx @ Wo
        key = jax.random.key(seed)
        ks = jax.random.split(key, 9)
        B, S, D = (4, 1024, EMBED_DIM)
        w = lambda k: jax.random.normal(k, (D, D), dtype=jnp.float32) * (1.0 / np.sqrt(D))
        return {'x': jax.random.normal(ks[0], (B, S, D), dtype=jnp.float32), 'Wq_l': w(ks[1]), 'Wk_l': w(ks[2]), 'Wv_l': w(ks[3]), 'Wo_l': w(ks[4]), 'Wq_g': w(ks[5]), 'Wk_g': w(ks[6]), 'Wv_g': w(ks[7]), 'Wo_g': w(ks[8])}
    _L1_attn_in = _L1_attn_setup()

    def _L1_ffn_setup():
        import jax, jax.numpy as jnp
        import numpy as np
        EPS = 1e-05

        @jax.custom_vjp
        def ste_quantize(w):
            scale = jnp.maximum(jnp.mean(jnp.abs(w)), EPS)
            return jnp.clip(jnp.round(w / scale), -1.0, 1.0)

        def _ste_fwd(w):
            return (ste_quantize(w), None)

        def _ste_bwd(_, g):
            return (g,)
        ste_quantize.defvjp(_ste_fwd, _ste_bwd)
        key = jax.random.key(seed)
        k1, k2 = jax.random.split(key)
        x = jax.random.normal(k1, (8, 1024, 128), dtype=jnp.float32)
        weight = jax.random.normal(k2, (128, 128), dtype=jnp.float32) * 0.02
        return {'x': x, 'weight': weight}
    _L1_ffn_in = _L1_ffn_setup()
    _d = {'L0_attn_x': _L0_attn_in['x'], 'L0_attn_norm_w': _L0_attn_in['norm_w'], 'L0_attn_W_in': _L0_attn_in['W_in'], 'L0_attn_conv_w': _L0_attn_in['conv_w'], 'L0_attn_conv_b': _L0_attn_in['conv_b'], 'L0_attn_W_dt': _L0_attn_in['W_dt'], 'L0_attn_b_dt': _L0_attn_in['b_dt'], 'L0_attn_W_B': _L0_attn_in['W_B'], 'L0_attn_W_C': _L0_attn_in['W_C'], 'L0_attn_A_log': _L0_attn_in['A_log'], 'L0_attn_D_param': _L0_attn_in['D_param'], 'L0_attn_W_out': _L0_attn_in['W_out'], 'L0_attn_residual_scale': _L0_attn_in['residual_scale'], 'L0_ffn_router_weight': _L0_ffn_in['router_weight'], 'L0_ffn_e_bias': _L0_ffn_in['e_bias'], 'L0_ffn_gate_w': _L0_ffn_in['gate_w'], 'L0_ffn_up_w': _L0_ffn_in['up_w'], 'L0_ffn_down_w': _L0_ffn_in['down_w'], 'L0_ffn_sh_gate_w': _L0_ffn_in['sh_gate_w'], 'L0_ffn_sh_up_w': _L0_ffn_in['sh_up_w'], 'L0_ffn_sh_down_w': _L0_ffn_in['sh_down_w'], 'L1_attn_Wq_l': _L1_attn_in['Wq_l'], 'L1_attn_Wk_l': _L1_attn_in['Wk_l'], 'L1_attn_Wv_l': _L1_attn_in['Wv_l'], 'L1_attn_Wo_l': _L1_attn_in['Wo_l'], 'L1_attn_Wq_g': _L1_attn_in['Wq_g'], 'L1_attn_Wk_g': _L1_attn_in['Wk_g'], 'L1_attn_Wv_g': _L1_attn_in['Wv_g'], 'L1_attn_Wo_g': _L1_attn_in['Wo_g'], 'L1_ffn_weight': _L1_ffn_in['weight']}
    _x0 = _d['L0_attn_x']
    _d['L0_attn_x'] = jax.random.normal(jax.random.fold_in(jax.random.key(seed), 1), (32, 256, 128), dtype=_x0.dtype)
    del _x0
    return _d

def reference(L0_attn_x, L0_attn_norm_w, L0_attn_W_in, L0_attn_conv_w, L0_attn_conv_b, L0_attn_W_dt, L0_attn_b_dt, L0_attn_W_B, L0_attn_W_C, L0_attn_A_log, L0_attn_D_param, L0_attn_W_out, L0_attn_residual_scale, L0_ffn_router_weight, L0_ffn_e_bias, L0_ffn_gate_w, L0_ffn_up_w, L0_ffn_down_w, L0_ffn_sh_gate_w, L0_ffn_sh_up_w, L0_ffn_sh_down_w, L1_attn_Wq_l, L1_attn_Wk_l, L1_attn_Wv_l, L1_attn_Wo_l, L1_attn_Wq_g, L1_attn_Wk_g, L1_attn_Wv_g, L1_attn_Wo_g, L1_ffn_weight):

    def _L0_attn_ref(x, norm_w, W_in, conv_w, conv_b, W_dt, b_dt, W_B, W_C, A_log, D_param, W_out, residual_scale):
        import jax, jax.numpy as jnp
        import numpy as np
        D_MODEL = 128
        D_STATE = 16
        D_CONV = 4
        EXPAND = 2
        D_INNER = D_MODEL * EXPAND

        def soft_clamp(x, lo, hi, sharp):
            c = (hi + lo) / 2.0
            r = (hi - lo) / 2.0
            return jnp.tanh((x - c) / (r + 1e-08) * sharp) / sharp * r + c
        B, L, _ = x.shape
        var = jnp.mean(x * x, axis=-1, keepdims=True)
        xn = x * jax.lax.rsqrt(var + 1e-06) * norm_w
        proj = xn @ W_in.T
        x_branch, gate = (proj[..., :D_INNER], proj[..., D_INNER:])
        xc = jax.lax.conv_general_dilated(jnp.swapaxes(x_branch, 1, 2), conv_w, (1,), [(D_CONV - 1, 0)], dimension_numbers=('NCH', 'OIH', 'NCH'), feature_group_count=D_INNER)
        xc = xc + conv_b[None, :, None]
        xc = jnp.swapaxes(xc, 1, 2)
        xc = xc * jax.nn.sigmoid(xc)
        dt = soft_clamp(jax.nn.softplus(xc @ W_dt.T + b_dt), 0.001, 0.1, 0.5)
        Bp = xc @ W_B.T
        Cp = xc @ W_C.T
        A = -jnp.exp(soft_clamp(A_log, -5.0, 5.0, 0.5))
        dt_A = soft_clamp(dt[..., None] * A[None, None], -8.0, 8.0, 0.5)
        dA = jnp.exp(dt_A)
        dB = dt[..., None] * Bp[:, :, None, :]
        h0 = jnp.zeros((B, D_INNER, D_STATE), jnp.float32)

        def step(h, inp):
            dA_t, dB_t, x_t, C_t, t = inp
            h = h * dA_t + dB_t * x_t[:, :, None]
            nrm = jnp.sqrt(jnp.sum(h * h, axis=(1, 2), keepdims=True))
            fac = jnp.minimum(20.0 / (nrm + 1e-08), 1.0)
            h = jnp.where(t % 10 == 0, h * fac, h)
            y = jnp.einsum('bdn,bn->bd', h, C_t) + D_param * x_t
            return (h, y)
        xs = (jnp.swapaxes(dA, 0, 1), jnp.swapaxes(dB, 0, 1), jnp.swapaxes(xc, 0, 1), jnp.swapaxes(Cp, 0, 1), jnp.arange(L))
        _, ys = jax.lax.scan(step, h0, xs)
        x_ssm = jnp.swapaxes(ys, 0, 1)
        x_out = x_ssm * (gate * jax.nn.sigmoid(gate)) @ W_out.T
        scale = jax.nn.sigmoid(residual_scale) * 0.5
        return x + scale * x_out

    def _L0_ffn_ref(hidden_states, router_weight, e_bias, gate_w, up_w, down_w, sh_gate_w, sh_up_w, sh_down_w):
        import jax, jax.numpy as jnp
        import numpy as np
        B, S, H = (1, 256, 128)
        E, K = (16, 4)
        G, TG = (4, 2)
        I_MOE = 64
        N_SH = 2
        SCALE = 2.5

        def _mlp(x, gw, uw, dw):
            return jax.nn.silu(x @ gw.T) * (x @ uw.T) @ dw.T

        def _route(x2d, router_weight, e_bias):
            T = x2d.shape[0]
            scores = jax.nn.sigmoid(x2d @ router_weight.T)
            sc = scores + e_bias[None, :]
            group_scores = jnp.sum(jax.lax.top_k(sc.reshape(T, G, E // G), 2)[0], axis=-1)
            _, gidx = jax.lax.top_k(group_scores, TG)
            gmask = jnp.zeros((T, G), sc.dtype).at[jnp.arange(T)[:, None], gidx].set(1.0)
            smask = jnp.repeat(gmask, E // G, axis=1)
            masked = jnp.where(smask > 0, sc, 0.0)
            _, tidx = jax.lax.top_k(masked, K)
            tw = jnp.take_along_axis(scores, tidx, axis=1)
            tw = tw / (jnp.sum(tw, axis=-1, keepdims=True) + 1e-20)
            tw = tw * SCALE
            return (tidx, tw)

        def _moe_forward(hidden_states, router_weight, e_bias, gate_w, up_w, down_w, sh_gate_w, sh_up_w, sh_down_w):
            orig_shape = hidden_states.shape
            x = hidden_states.reshape(-1, H)
            T = x.shape[0]
            tidx, tw = _route(x, router_weight, e_bias)
            g = jnp.einsum('th,eih->tei', x, gate_w)
            u = jnp.einsum('th,eih->tei', x, up_w)
            h = jax.nn.silu(g) * u
            yo = jnp.einsum('tei,ehi->teh', h, down_w)
            combine = jnp.zeros((T, E), tw.dtype).at[jnp.arange(T)[:, None], tidx].add(tw)
            routed = jnp.einsum('te,teh->th', combine, yo)
            shared = _mlp(hidden_states.reshape(-1, H), sh_gate_w, sh_up_w, sh_down_w)
            return (routed + shared).reshape(orig_shape)
        return _moe_forward(hidden_states, router_weight, e_bias, gate_w, up_w, down_w, sh_gate_w, sh_up_w, sh_down_w)

    def _L1_attn_ref(x, Wq_l, Wk_l, Wv_l, Wo_l, Wq_g, Wk_g, Wv_g, Wo_g):
        import jax, jax.numpy as jnp
        import numpy as np
        EMBED_DIM = 128
        NUM_HEADS = 16
        CHUNK = 32

        def _mha_residual(x, Wq, Wk, Wv, Wo, num_heads):
            *lead, S, D = x.shape
            hd = D // num_heads
            scale = 1.0 / jnp.sqrt(jnp.asarray(hd, x.dtype))
            q = (x @ Wq).reshape(*lead, S, num_heads, hd)
            k = (x @ Wk).reshape(*lead, S, num_heads, hd)
            v = (x @ Wv).reshape(*lead, S, num_heads, hd)
            scores = jnp.einsum('...qhe,...khe->...hqk', q, k) * scale
            attn = jax.nn.softmax(scores, axis=-1)
            ctx = jnp.einsum('...hqk,...khe->...qhe', attn, v)
            ctx = ctx.reshape(*lead, S, D)
            return x + ctx @ Wo
        B, S, D = x.shape
        nC = S // CHUNK
        chunks = x.reshape(B, nC, CHUNK, D)
        chunks = _mha_residual(chunks, Wq_l, Wk_l, Wv_l, Wo_l, NUM_HEADS)
        summaries = chunks.mean(axis=2)
        global_ctx = _mha_residual(summaries, Wq_g, Wk_g, Wv_g, Wo_g, NUM_HEADS)
        enhanced = chunks + global_ctx[:, :, None, :]
        return enhanced.reshape(B, S, D)

    def _L1_ffn_ref(x, weight):
        import jax, jax.numpy as jnp
        import numpy as np
        EPS = 1e-05

        @jax.custom_vjp
        def ste_quantize(w):
            scale = jnp.maximum(jnp.mean(jnp.abs(w)), EPS)
            return jnp.clip(jnp.round(w / scale), -1.0, 1.0)

        def _ste_fwd(w):
            return (ste_quantize(w), None)

        def _ste_bwd(_, g):
            return (g,)
        ste_quantize.defvjp(_ste_fwd, _ste_bwd)
        w_ternary = ste_quantize(weight)
        scale = jnp.maximum(jnp.mean(jnp.abs(weight)), EPS)
        return jnp.einsum('bsi,oi->bso', x, w_ternary * scale)
    x = L0_attn_x
    xn = _layernorm(x, axis=-1)
    s = _L0_attn_ref(xn, L0_attn_norm_w, L0_attn_W_in, L0_attn_conv_w, L0_attn_conv_b, L0_attn_W_dt, L0_attn_b_dt, L0_attn_W_B, L0_attn_W_C, L0_attn_A_log, L0_attn_D_param, L0_attn_W_out, L0_attn_residual_scale)
    g = _silu(_L0_ffn_ref(xn, L0_ffn_router_weight, L0_ffn_e_bias, L0_ffn_gate_w, L0_ffn_up_w, L0_ffn_down_w, L0_ffn_sh_gate_w, L0_ffn_sh_up_w, L0_ffn_sh_down_w))
    x = x + s * g
    xn = _layernorm(x, axis=-1)
    s = _L1_attn_ref(xn, L1_attn_Wq_l, L1_attn_Wk_l, L1_attn_Wv_l, L1_attn_Wo_l, L1_attn_Wq_g, L1_attn_Wk_g, L1_attn_Wv_g, L1_attn_Wo_g)
    g = _silu(_L1_ffn_ref(xn, L1_ffn_weight))
    x = x + s * g
    return x

_drawn_inputs = setup_inputs


def setup_inputs(seed=0):
    import zlib

    import numpy as np

    out = dict(_drawn_inputs(seed))
    spreads = {'L0_attn_norm_w': (1.0, 0.6),
     'L0_attn_conv_b': (0.0, 0.8),
     'L0_attn_b_dt': (-2.0, 0.6),
     'L0_attn_D_param': (0.10000000149011612, 0.6),
     'L0_ffn_e_bias': (0.0, 0.8)}
    factors = {'L0_attn_W_in': 8.0,
     'L0_attn_conv_w': 8.0,
     'L0_attn_W_dt': 8.0,
     'L0_attn_W_B': 8.0,
     'L0_attn_W_C': 8.0,
     'L0_attn_A_log': 8.0,
     'L0_attn_W_out': 8.0,
     'L0_ffn_router_weight': 8.0,
     'L0_ffn_gate_w': 8.0,
     'L0_ffn_up_w': 8.0,
     'L0_ffn_down_w': 8.0,
     'L0_ffn_sh_gate_w': 8.0,
     'L0_ffn_sh_up_w': 8.0,
     'L0_ffn_sh_down_w': 8.0,
     'L1_attn_Wq_l': 3.249,
     'L1_attn_Wk_l': 3.051,
     'L1_attn_Wq_g': 8.0,
     'L1_attn_Wk_g': 8.0,
     'L1_attn_Wv_g': 8.0,
     'L1_attn_Wo_g': 8.0}
    for name, (base, spread) in spreads.items():
        noise = np.random.default_rng([zlib.crc32(name.encode()), seed]).standard_normal(out[name].shape)
        drawn = base * np.exp(spread * noise) if base else spread * noise
        out[name] = jnp.asarray(drawn.astype(out[name].dtype))
    for name, factor in factors.items():
        out[name] = (out[name] * factor).astype(out[name].dtype)
    return out
```

```python
import numpy as np
from contextlib import ExitStack

import concourse.bass as bass
from concourse import mybir

F32 = mybir.dt.float32
BF16 = mybir.dt.bfloat16
ALU = mybir.AluOpType
ACT = mybir.ActivationFunctionType
AX = mybir.AxisListType

P = 128
B, L, D = 32, 256, 128
T = B * L
DI = 256
NS = 16
E_ALL, TOPK = 16, 4
GROUPS, TOPG = 4, 2
MOE_SCALE = 2.5

MT = 512
MCH = T // MT
MQ = MT // P
NJ = 9
STEPS = 10
NC = -(-L // STEPS)
ST = STEPS * B
TP = NC * ST
HALO = 3 * B


class Count:

    def __init__(self, ctx, nc, name, per, credit=0, by=1):
        self.sem, self.per, self.credit, self.by = ctx.enter_context(nc.semaphore(name)), per, credit, by

    def at(self, k, n=1):
        return k * (self.per * self.by) + (self.credit + n * self.by)

    def give(self, eng):
        eng.sem_inc(self.sem, self.credit)


class Alternate:

    def __init__(self, ctx, nc, name, per, credit=0):
        self.sems = [ctx.enter_context(nc.semaphore(f"{name}_{p}")) for p in range(2)]
        self.half, self.credit = per * 8, credit

    def at(self, k, p, n=1):
        return k * self.half + (self.credit - p * self.half + n * 16)

    def give(self, eng):
        for s in self.sems:
            eng.sem_inc(s, self.credit)


def in_pairs(eng, n, first, body):
    for k in range(first, 0):
        body(k, k % 2, k)
    loops = (n + first - 1) // 2 if first < 0 else (n - 2) // 2
    with eng.Fori(0, loops) as i:
        body(i * 2, 0, None)
        body(i * 2 + 1, 1, None)
    for k in range(2 * loops, n):
        body(k, k % 2, k)


def expert_phase(nc, io, scratch):
    with ExitStack() as ctx:
        def sb(name, shape, dt=F32):
            return ctx.enter_context(nc.sbuf_tensor("m_" + name, shape, dt))

        def ps(name, shape, dt=F32):
            return ctx.enter_context(nc.psum_tensor("m_" + name, shape, dt))

        def cnt(name, per, credit=0, by=1):
            return Count(ctx, nc, "m_" + name, per, credit, by)

        gate_w = sb("gate_w", [P, NJ * P])
        up_w = sb("up_w", [P, NJ * P])
        down_w = sb("down_w", [P, NJ, D])
        router_w = sb("router_w", [P, E_ALL])
        e_bias = sb("e_bias", [P, E_ALL])
        sel = sb("sel", [96, 8 * P], BF16)
        ident = sb("ident", [P, P])
        ahead = sb("ahead", [P, E_ALL])
        restart = sb("restart", [P, MQ * E_ALL])
        mhalf = sb("mhalf", [P, MQ])
        x_in = sb("x_in", [P, 2, MQ, D])
        xn = sb("xn", [P, MQ, D])
        xr = sb("xr", [P, MQ, D])
        stats = sb("stats", [P, MQ, 6])
        mv = sb("mv", [P, MQ, 2])
        pt = sb("pt", [P, 4, MQ])
        rstd = sb("rstd", [P, 2, MQ])
        xnT = sb("xnT", [P, 2, MT])
        xrT = sb("xrT", [P, MT])
        th = sb("th", [P, MQ, E_ALL])
        r = {n: sb("r_" + n, [P, MQ, E_ALL]) for n in
             ("sig", "sc", "msk", "gt", "eq", "cum", "sel", "tw", "c", "r1")}
        pairs = sb("pairs", [P, MQ * GROUPS, 6])
        gs = sb("gs", [P, MQ, GROUPS])
        wins = sb("wins", [P, MQ, GROUPS])
        cmp = sb("cmp", [P, MQ, GROUPS])
        top8 = sb("top8", [P, MQ, 8])
        room = sb("room", [P, MQ])
        den = sb("den", [P, MQ])
        hi = sb("hi", [P, MQ, E_ALL], BF16)
        c3 = sb("c3", [P, MQ, 96])
        cT = sb("cT", [96, 2, MT], BF16)
        sl = sb("sl", [P, 2, MT])
        hb = sb("hb", [P, 2, MT])
        hid = sb("hid", [P, 2, MT])
        g_out = sb("g_out", [P, 2, MT])
        zero = sb("zero", [P, P])

        pg = ps("pg", [P, 2, MT])
        pu = ps("pu", [P, 2, MT])
        pc = ps("pc", [P, MT])
        py = ps("py", [P, MT])
        pf = ps("pf", [P, 2, MT])

        w_load = ctx.enter_context(nc.semaphore("m_w_load"))
        consts = ctx.enter_context(nc.semaphore("m_consts"))
        spare = ctx.enter_context(nc.semaphore("m_spare"))
        zeroed = ctx.enter_context(nc.semaphore("m_zeroed"))
        pads = ctx.enter_context(nc.semaphore("m_pads"))
        x_load = cnt("x_load", 1, by=16)
        x_used = cnt("x_used", 1, 2)
        moments = cnt("moments", 1)
        rstd_ok = cnt("rstd_ok", 1)
        pchain = cnt("pchain", 7)
        xn_ok = cnt("xn_ok", 1)
        tp_n = cnt("tp_n", 1)
        tp_r = cnt("tp_r", 1)
        xnT_ok = cnt("xnT_ok", 1)
        xrT_ok = cnt("xrT_ok", 1)
        logits = cnt("logits", 1)
        th_ok = cnt("th_ok", 1)
        c3_ok = cnt("c3_ok", 1, 1)
        c_tp = cnt("c_tp", 1)
        cT_ok = cnt("cT_ok", 1, 1)
        xn_st = cnt("xn_st", 1, 32, by=16)
        xr_st = cnt("xr_st", 1, 16, by=16)
        gu_ok = cnt("gu_ok", NJ)
        sl_ok = cnt("sl_ok", NJ)
        hb_ok = cnt("hb_ok", NJ, 2)
        cb_ok = cnt("cb_ok", NJ - 1)
        hid_ok = cnt("hid_ok", NJ, 2)
        down_ok = cnt("down_ok", NJ, 2)
        g_ok = cnt("g_ok", 1, 1)
        g_st = cnt("g_st", 1, 32, by=16)
        dch = ctx.enter_context(nc.semaphore("m_dve_chain"))
        DCH = 57
        NW = 7

        block = ctx.enter_context(nc.Block())

        @block.sync
        def _(sp):
            for dst, src in ((gate_w, "gate_w"), (up_w, "up_w"), (down_w, "down_w"), (router_w, "router_w"),
                             (e_bias, "e_bias"), (sel, "moe_sel"), (ident, "ident")):
                sp.dma_start(dst[:], io[src]).then_inc(w_load, 16)
            xn_st.give(sp)
            xr_st.give(sp)
            g_st.give(sp)
            sp.wait_ge(zeroed, 1)
            sp.dma_start(scratch["xrT"][:, 0:HALO], zero[:, 0:HALO]).then_inc(pads, 16)
            for name, at in (("xrT", HALO + T), ("xnT", T), ("gT", T)):
                sp.dma_start(scratch[name][:, at:at + TP - T], zero[:, 0:TP - T]).then_inc(pads, 16)

            def body(k, p, kk):
                if kk is None or kk + 1 < MCH:
                    sp.wait_ge(x_used.sem, x_used.at(k + 1, -1))
                    sp.sem_inc(spare, 1)
                    sp.dma_start(x_in[:, 1 - p], io["x_tm"][bass.ds((k + 1) * MT, MT), :].rearrange(
                        "(q p) d -> p q d", p=P)).then_inc(x_load.sem, 16)
                    sp.wait_ge(xnT_ok.sem, xnT_ok.at(k + 1))
                    sp.sem_inc(spare, 1)
                    sp.dma_start(scratch["xnT"][:, bass.ds((k + 1) * MT, MT)], xnT[:, 1 - p]).then_inc(xn_st.sem, 16)
                    sp.wait_ge(xrT_ok.sem, xrT_ok.at(k + 1))
                    sp.sem_inc(spare, 1)
                    sp.dma_start(scratch["xrT"][:, bass.ds((k + 1) * MT + HALO, MT)], xrT[:]).then_inc(xr_st.sem, 16)
                if kk is None or kk >= 0:
                    sp.wait_ge(g_ok.sem, g_ok.at(k))
                    sp.sem_inc(spare, 1)
                    sp.dma_start(scratch["gT"][:, bass.ds(k * MT, MT)], g_out[:, p]).then_inc(g_st.sem, 16)

            in_pairs(sp, MCH, -1, body)
            sp.wait_ge(pads, 64)
            sp.wait_ge(xn_st.sem, xn_st.at(MCH - 1))
            sp.sem_inc(spare, 1)
            sp.wait_ge(xr_st.sem, xr_st.at(MCH - 1))
            sp.sem_inc(spare, 1)
            sp.wait_ge(g_st.sem, g_st.at(MCH - 1))
            sp.sem_inc(spare, 1)

        @block.gpsimd
        def _(pool):
            pool.memset(mhalf[:], -0.5).then_inc(consts, 1)
            pool.wait_ge(consts, 4)

            def body(k, p, kk):
                if kk is not None and kk + 1 >= MCH:
                    return
                k1 = k + 1
                step = [0]

                def link(ins):
                    step[0] += 1
                    ins.then_inc(pchain.sem, 1)
                    pool.wait_ge(pchain.sem, pchain.at(k1, step[0]))
                    if step[0] == 4:
                        pool.sem_inc(spare, 1)

                pool.wait_ge(moments.sem, moments.at(k1))
                pool.sem_inc(spare, 1)
                link(pool.tensor_scalar(pt[:, 0], mv[:, :, 1], 1e-5, None, ALU.add))
                link(pool.tensor_tensor(rstd[:, 0], pt[:, 0], mhalf[:], ALU.pow))
                link(pool.tensor_tensor(pt[:, 1], rstd[:, 0], rstd[:, 0], ALU.mult))
                link(pool.tensor_tensor(pt[:, 2], pt[:, 1], mv[:, :, 1], ALU.mult))
                link(pool.tensor_scalar(pt[:, 3], pt[:, 2], 1e-6, None, ALU.add))
                link(pool.tensor_tensor(pt[:, 1], pt[:, 3], mhalf[:], ALU.pow))
                link(pool.tensor_tensor(rstd[:, 1], pt[:, 1], rstd[:, 0], ALU.mult))
                pool.sem_inc(rstd_ok.sem, 1)

            in_pairs(pool, MCH, -1, body)

        @block.tensor
        def _(pe):
            pe.wait_ge(w_load, 16 * NW)
            pe.wait_ge(consts, 4)

            def gate_up(k, p, j):
                s = (p + j) % 2
                pe.wait_ge(hb_ok.sem, hb_ok.at(k, j - 1))
                pe.matmul(pg[:, s], gate_w[:, j * P:(j + 1) * P], xnT[:, p], start=True, stop=True)
                pe.matmul(pu[:, s], up_w[:, j * P:(j + 1) * P], xnT[:, p], start=True,
                          stop=True).then_inc(gu_ok.sem, 1)

            def spread(k, p, j):
                if j == 0:
                    pe.wait_ge(cT_ok.sem, cT_ok.at(k))
                pe.wait_ge(hid_ok.sem, hid_ok.at(k, j if j else -1))
                pe.matmul(pc[:], sel[:, j * P:(j + 1) * P], cT[:, p], start=True, stop=True).then_inc(cb_ok.sem, 1)

            def down(k, p, j):
                s = (p + j) % 2
                pe.wait_ge(hid_ok.sem, hid_ok.at(k, j + 1))
                if j == 0:
                    pe.wait_ge(g_ok.sem, g_ok.at(k, 0))
                pe.matmul(py[:], down_w[:, j], hid[:, s], start=(j == 0), stop=(j == NJ - 1)).then_inc(down_ok.sem, 1)

            def front(k, p, part):
                if part == 0:
                    pe.wait_ge(xn_ok.sem, xn_ok.at(k))
                    for q in range(MQ):
                        mm = pe.transpose(pf[:, 0, q * P:(q + 1) * P], xn[:, q], ident[:])
                    mm.then_inc(tp_n.sem, 1)
                    pe.wait_ge(cT_ok.sem, cT_ok.at(k, 0))
                    for q in range(MQ):
                        mm = pe.transpose(pf[:, 1, q * P:(q + 1) * P], xr[:, q], ident[:])
                    mm.then_inc(tp_r.sem, 1)
                elif part == 1:
                    pe.wait_ge(xnT_ok.sem, xnT_ok.at(k))
                    for q in range(MQ):
                        mm = pe.matmul(pf[:, 0, q * E_ALL:(q + 1) * E_ALL], xnT[:, p, q * P:(q + 1) * P],
                                       router_w[:], start=True, stop=True)
                    mm.then_inc(logits.sem, 1)
                else:
                    pe.wait_ge(c3_ok.sem, c3_ok.at(k))
                    pe.wait_ge(xrT_ok.sem, xrT_ok.at(k))
                    for q in range(MQ):
                        mm = pe.transpose(pf[0:96, 1, q * P:(q + 1) * P], c3[:, q], ident[:])
                    mm.then_inc(c_tp.sem, 1)

            def body(k, p, kk):
                has_front = kk is None or kk + 1 < MCH
                if kk is not None and kk < 0:
                    for part in range(3):
                        front(k + 1, 1 - p, part)
                    return
                gate_up(k, p, 0)
                for j in range(NJ):
                    if j < NJ - 1:
                        gate_up(k, p, j + 1)
                        spread(k, p, j)
                    if has_front and j == 2:
                        front(k + 1, 1 - p, 0)
                    if has_front and j == 4:
                        front(k + 1, 1 - p, 1)
                    down(k, p, j)
                if has_front:
                    front(k + 1, 1 - p, 2)

            in_pairs(pe, MCH, -1, body)

        @block.scalar
        def _(act):
            g_ok.give(act)
            cT_ok.give(act)

            def main(k, p, j):
                s = (p + j) % 2
                act.wait_ge(gu_ok.sem, gu_ok.at(k, j + 1))
                act.activation(sl[:, s], pg[:, s], ACT.Silu).then_inc(sl_ok.sem, 1)

            def front(k, p, part):
                if part == 0:
                    act.wait_ge(tp_n.sem, tp_n.at(k))
                    act.wait_ge(xn_st.sem, xn_st.at(k, -1))
                    act.activation(xnT[:, p], pf[:, 0], ACT.Copy).then_inc(xnT_ok.sem, 1)
                    act.wait_ge(tp_r.sem, tp_r.at(k))
                    act.wait_ge(xr_st.sem, xr_st.at(k, 0))
                    act.activation(xrT[:], pf[:, 1], ACT.Copy).then_inc(xrT_ok.sem, 1)
                elif part == 1:
                    act.wait_ge(logits.sem, logits.at(k))
                    act.wait_ge(c3_ok.sem, c3_ok.at(k, 0))
                    act.activation(th[:], pf[:, 0, 0:MQ * E_ALL], ACT.Tanh, scale=0.5).then_inc(th_ok.sem, 1)
                else:
                    act.wait_ge(c_tp.sem, c_tp.at(k))
                    act.activation(cT[:, p], pf[0:96, 1], ACT.Copy).then_inc(cT_ok.sem, 1)

            def body(k, p, kk):
                has_front = kk is None or kk + 1 < MCH
                if kk is not None and kk < 0:
                    for part in range(3):
                        front(k + 1, 1 - p, part)
                    return
                for j in range(NJ):
                    main(k, p, j)
                    if has_front and j == 3:
                        front(k + 1, 1 - p, 0)
                    if has_front and j == 5:
                        front(k + 1, 1 - p, 1)
                if has_front:
                    front(k + 1, 1 - p, 2)
                act.wait_ge(down_ok.sem, down_ok.at(k, NJ))
                act.wait_ge(g_st.sem, g_st.at(k, -1))
                act.activation(g_out[:, p], py[:], ACT.Silu).then_inc(g_ok.sem, 1)

            in_pairs(act, MCH, -1, body)

        @block.vector
        def _(v):
            x_used.give(v)
            c3_ok.give(v)
            hb_ok.give(v)
            hid_ok.give(v)
            v.sem_inc(down_ok.sem, 2)
            v.memset(c3[:], 0.0).then_inc(consts, 1)
            v.memset(restart[:], 1.0).then_inc(dch, 1)
            for i in range(GROUPS):
                v.memset(ahead[:].rearrange("p (q g) -> p q g", g=GROUPS)[:, :, i], float(i)).then_inc(dch, 1)
            v.wait_ge(dch, 5)
            v.memset(restart[:].rearrange("p (q e) -> p q e", e=E_ALL)[:, :, 0], 0.0).then_inc(consts, 1)
            v.memset(zero[:], 0.0).then_inc(zeroed, 1)
            v.wait_ge(zeroed, 1)
            v.memset(cmp[:], 0.0).then_inc(consts, 1)
            v.wait_ge(consts, 4)
            v.wait_ge(w_load, 16 * NW)
            link_base = 5

            def main(k, p, j):
                s = (p + j) % 2
                v.wait_ge(sl_ok.sem, sl_ok.at(k, j + 1))
                if j < NJ - 1:
                    v.tensor_tensor(hb[:, s], sl[:, s], pu[:, s], ALU.mult).then_inc(hb_ok.sem, 1)
                    v.wait_ge(hb_ok.sem, hb_ok.at(k, j + 1))
                    v.wait_ge(cb_ok.sem, cb_ok.at(k, j + 1))
                    v.wait_ge(down_ok.sem, down_ok.at(k, j - 1))
                    v.tensor_tensor(hid[:, s], hb[:, s], pc[:], ALU.mult).then_inc(hid_ok.sem, 1)
                else:
                    v.wait_ge(down_ok.sem, down_ok.at(k, j - 1))
                    v.tensor_tensor(hid[:, s], sl[:, s], pu[:, s], ALU.mult).then_inc(hb_ok.sem, 1)
                    v.wait_ge(hb_ok.sem, hb_ok.at(k, NJ))
                    v.sem_inc(hid_ok.sem, 1)

            def front(k, p, parts, step):
                def link(ins):
                    step[0] += 1
                    ins.then_inc(dch, 1)
                    v.wait_ge(dch, k * DCH + (link_base + step[0]))

                def todo():
                    v.wait_ge(x_load.sem, x_load.at(k))
                    for q in range(MQ):
                        ins = v.bn_stats(stats[:, q], x_in[:, p, q])
                        if q < MQ - 1:
                            ins.then_inc(dch, 1)
                            step[0] += 1
                    link(ins)
                    v.sem_inc(spare, 1)
                    for q in range(MQ):
                        ins = v.bn_aggr(mv[:, q], stats[:, q])
                        if q < MQ - 1:
                            ins.then_inc(dch, 1)
                            step[0] += 1
                    link(ins)
                    v.sem_inc(moments.sem, 1)
                    yield
                    v.wait_ge(rstd_ok.sem, rstd_ok.at(k))
                    for q in range(MQ):
                        v.tensor_scalar(xn[:, q], x_in[:, p, q], mv[:, q, 0:1], rstd[:, 0, q:q + 1],
                                        ALU.subtract, ALU.mult).then_inc(dch, 1)
                        step[0] += 1
                        ins = v.tensor_scalar(xr[:, q], x_in[:, p, q], mv[:, q, 0:1], rstd[:, 1, q:q + 1],
                                              ALU.subtract, ALU.mult)
                        if q < MQ - 1:
                            ins.then_inc(dch, 1)
                            step[0] += 1
                    link(ins)
                    v.sem_inc(xn_ok.sem, 1)
                    v.sem_inc(x_used.sem, 1)
                    yield
                    v.wait_ge(th_ok.sem, th_ok.at(k))
                    link(v.tensor_scalar(r["sig"][:], th[:], 0.5, 0.5, ALU.mult, ALU.add))
                    link(v.tensor_tensor(r["sc"][:], r["sig"][:],
                                         e_bias[:].unsqueeze(1).broadcast_to([P, MQ, E_ALL]), ALU.add))
                    sc4 = r["sc"][:].rearrange("p q (g e) -> p (q g) e", e=4)
                    at = 0
                    for s in (1, 2, 3):
                        ins = v.tensor_tensor(pairs[:, :, at:at + 4 - s], sc4[:, :, 0:4 - s], sc4[:, :, s:4], ALU.add)
                        at += 4 - s
                        if s < 3:
                            ins.then_inc(dch, 1)
                            step[0] += 1
                    link(ins)
                    link(v.tensor_reduce(gs[:].rearrange("p q g -> p (q g)"), pairs[:], AX.X, ALU.max))
                    yield
                    wn = wins[:]
                    link(v.tensor_copy(wn, ahead[:].rearrange("p (q g) -> p q g", g=GROUPS)))
                    for s in (1, 2, 3):
                        n = GROUPS - s
                        link(v.tensor_tensor(cmp[:, :, 0:n], gs[:, :, 0:n], gs[:, :, s:GROUPS], ALU.is_ge))
                        link(v.tensor_tensor(wn[:, :, 0:n], wn[:, :, 0:n], cmp[:, :, 0:n], ALU.add))
                        link(v.tensor_tensor(wn[:, :, s:GROUPS], wn[:, :, s:GROUPS], cmp[:, :, 0:n], ALU.subtract))
                    link(v.tensor_scalar(wn, wn, float(GROUPS - TOPG) - 0.5, None, ALU.is_gt))
                    yield
                    link(v.tensor_tensor(r["msk"][:].rearrange("p q (g e) -> p (q g) e", e=4), sc4,
                                         wins[:].rearrange("p q g -> p (q g)").unsqueeze(2).broadcast_to(
                                             [P, MQ * GROUPS, 4]), ALU.mult))
                    v.sem_inc(spare, 1)
                    for q in range(MQ):
                        ins = v.max(top8[:, q], r["msk"][:, q])
                        if q < MQ - 1:
                            ins.then_inc(dch, 1)
                            step[0] += 1
                    link(ins)
                    fourth = top8[:, :, TOPK - 1:TOPK].broadcast_to([P, MQ, E_ALL])
                    link(v.tensor_tensor(r["gt"][:], r["msk"][:], fourth, ALU.is_gt))
                    link(v.tensor_tensor(r["eq"][:], r["msk"][:], fourth, ALU.is_equal))
                    link(v.tensor_reduce(room[:], r["gt"][:], AX.X, ALU.add))
                    link(v.tensor_scalar(room[:], room[:], -1.0, float(TOPK), ALU.mult, ALU.add))
                    link(v.tensor_tensor_scan(r["cum"][:].rearrange("p q e -> p (q e)"), restart[:],
                                              r["eq"][:].rearrange("p q e -> p (q e)"), 0.0, ALU.mult, ALU.add))
                    yield
                    link(v.tensor_tensor(r["cum"][:], r["cum"][:],
                                         room[:].unsqueeze(2).broadcast_to([P, MQ, E_ALL]), ALU.is_le))
                    link(v.tensor_tensor(r["sel"][:], r["cum"][:], r["eq"][:], ALU.mult))
                    link(v.tensor_tensor(r["sel"][:], r["sel"][:], r["gt"][:], ALU.add))
                    link(v.tensor_tensor(r["tw"][:], r["sel"][:], r["sig"][:], ALU.mult))
                    link(v.tensor_reduce(den[:], r["tw"][:], AX.X, ALU.add))
                    link(v.tensor_scalar(den[:], den[:], 1e-20, None, ALU.add))
                    link(v.reciprocal(den[:], den[:]))
                    link(v.scalar_tensor_tensor(r["c"][:], r["tw"][:], MOE_SCALE,
                                                den[:].unsqueeze(2).broadcast_to([P, MQ, E_ALL]), ALU.mult, ALU.mult))
                    yield
                    v.wait_ge(cT_ok.sem, cT_ok.at(k, 0))
                    link(v.tensor_copy(hi[:], r["c"][:]))
                    link(v.tensor_copy(c3[:, :, 0:16], hi[:]))
                    link(v.tensor_tensor(r["r1"][:], r["c"][:], c3[:, :, 0:16], ALU.subtract))
                    link(v.tensor_copy(hi[:], r["r1"][:]))
                    link(v.tensor_copy(c3[:, :, 32:48], hi[:]))
                    link(v.tensor_tensor(c3[:, :, 64:80], r["r1"][:], c3[:, :, 32:48], ALU.subtract))
                    v.sem_inc(c3_ok.sem, 1)
                    yield

                gen = todo()
                return gen

            def body(k, p, kk):
                has_front = kk is None or kk + 1 < MCH
                step = [0]
                gen = front(k + 1, 1 - p, None, step) if has_front else None
                if kk is not None and kk < 0:
                    for _ in gen:
                        pass
                    assert step[0] == DCH, step[0]
                    return
                for j in range(NJ):
                    main(k, p, j)
                    if has_front and j in (0, 1, 5, 6, 7, 8):
                        next(gen)
                if has_front:
                    for _ in gen:
                        pass
                    assert step[0] == DCH, step[0]

            in_pairs(v, MCH, -1, body)


def scan_phase(nc, io, scratch):
    R_DT, C_DT = (0.1 - 0.001) / 2, (0.1 + 0.001) / 2
    A_DT = 0.5 / (R_DT + 1e-8)
    NP = NS // 2
    NQ = ST // 64
    with ExitStack() as ctx:
        def sb(name, shape, dt=F32):
            return ctx.enter_context(nc.sbuf_tensor("s_" + name, shape, dt))

        def ps(name, shape, dt=F32):
            return ctx.enter_context(nc.psum_tensor("s_" + name, shape, dt))

        def cnt(name, per, credit=0, by=1):
            return Count(ctx, nc, "s_" + name, per, credit, by)

        def sem(name):
            return ctx.enter_context(nc.semaphore("s_" + name))

        h = sb("h", [P, 2, 2 * NS, ST])
        dA = sb("dA", [P, 2, 2 * NS, ST])
        conv_w = sb("conv_w", [P, 4, DI])
        gate_w = sb("gate_w", [P, DI])
        dt_w = sb("dt_w", [P, 2, DI])
        bc_w = sb("bc_w", [P, 2, 2 * NS])
        out_w = sb("out_w", [P, 2, D])
        pick = sb("pick", [96, NS], BF16)
        ident = sb("ident", [P, P])
        ident_b = sb("ident_b", [64, 64], BF16)
        ones = sb("ones", [P, P])
        cols = sb("cols", [P, 8])
        col2 = sb("col2", [P, 4])
        a16 = sb("a16", [P, 2 * NS])
        cst = sb("cst", [P, 2, B])
        xr = sb("xr", [P, HALO + ST])
        xg = sb("xg", [P, 4, ST])
        zg = sb("zg", [P, 4, ST])
        th = sb("th", [P, 2, ST])
        z = sb("z", [P, 2, ST])
        dt = sb("dt", [P, 2, ST])
        dtx = sb("dtx", [P, 2, ST])
        s3 = sb("s3", [64, NQ, 2, 96], BF16)
        rest = sb("rest", [64, NQ, 2, NS])
        bcT = sb("bcT", [96, 2, 2, ST], BF16)
        prod = sb("prod", [P, 2, 2, ST])
        xn = sb("xn", [P, ST])
        g = sb("g", [P, ST])
        tok = sb("tok", [P, 3, D])
        nrm = sb("nrm", [P, B])
        n2 = sb("n2", [P, 4, B])

        F = ps("F", [P, 2, 512])
        X = ps("X", [P, 2, 2, 512])
        Y = ps("Y", [P, 2, 512])
        Fb = F[:, 1, :].bitcast(BF16)
        NORM = F[:, 0, 480:512]

        w_load, consts, aset, vset, setup = (sem(n) for n in ("w_load", "consts", "aset", "vset", "setup"))
        xr_ld = cnt("xr_ld", 1, by=16)
        f_conv = cnt("f_conv", 1)
        a_conv = cnt("a_conv", 1)
        xc_ok = cnt("xc_ok", 1)
        f_gate = cnt("f_gate", 1, 1)
        a_gate = cnt("a_gate", 1)
        gs_ok = cnt("gs_ok", 1)
        f_dt = cnt("f_dt", 1)
        a_ln = cnt("a_ln", 1)
        v_ok = cnt("v_ok", 1)
        sp_ok = cnt("sp_ok", 1)
        a_dt = cnt("a_dt", 1)
        dt_ok = cnt("dt_ok", 1, 1)
        f_bc = cnt("f_bc", 1)
        s3_ok = cnt("s3_ok", 1)
        f_t = cnt("f_t", 1, 1)
        bcT_ok = cnt("bcT_ok", 1, 1)
        xg_st = cnt("xg_st", 1, 16, by=16)
        zg_ld = cnt("zg_ld", 3, by=16)
        b_ok = cnt("b_ok", NP)
        b_rd = cnt("b_rd", NP)
        c_ok = cnt("c_ok", NP)
        dA_ok = cnt("dA_ok", 4, 1)
        a_th = cnt("a_th", 2 * NS)
        st0_ok = cnt("st0_ok", 1)
        sq_ok = cnt("sq_ok", 1)
        nr_ok = cnt("nr_ok", 1)
        n2_ps = cnt("n2_ps", 1)
        n2_ok = cnt("n2_ok", 1)
        PCH = 7 + 2 * (STEPS - 1)
        pch = cnt("pch", PCH)
        h_ok = cnt("h_ok", 1, 1)
        prod_ok = cnt("prod_ok", 2 * NP, 2 * NP)
        prod_rd = cnt("prod_rd", 2 * NP, 2)
        yy_ok = cnt("yy_ok", 1)
        o_ok = cnt("o_ok", 1, 1)
        sg_ok = cnt("sg_ok", 1, 1)
        o_tp = cnt("o_tp", 1)
        tok_ok = cnt("tok_ok", 1, 1)
        tok_st = cnt("tok_st", 3, 48, by=16)
        vch = cnt("vch", 8)
        a_exp = cnt("a_exp", 2)
        NW = 15

        spare = sem("spare")

        stage = dA[:, 1].rearrange("p a b -> p (a b)")
        w_in, taps, a_log = stage[:, 0:2 * DI], stage[:, 512:1536], stage[:, 1536:1568]

        def has_inner(kk):
            return kk is None or kk + 2 < NC

        def has_drive(kk):
            return kk is None or 0 <= kk + 1 < NC

        def has_output(kk):
            return kk is None or kk >= 0

        block = ctx.enter_context(nc.Block())

        @block.sync
        def _(sp):
            loads = [(w_in, "w_in"), (taps, "taps"), (a_log, "a_log"), (dt_w[:], "dt_w"), (bc_w[:], "bc_w"),
                     (out_w[:], "out_w"), (pick[:], "pick"), (ident[:], "ident"), (ident_b[:], "ident_b"),
                     (cols[:, 0:2], "conv_b"), (cols[:, 2:4], "b_dt"), (cols[:, 4:6], "d_param"),
                     (cols[:, 6:7], "residual"), (cols[:, 7:8], "norm_w"), (ones[:], "ones")]
            assert len(loads) == NW
            for dst, src in loads:
                sp.dma_start(dst, io[src]).then_inc(w_load, 16)
            xg_st.give(sp)
            tok_st.give(sp)

            def body(k, p, kk):
                if has_inner(kk):
                    k2 = k + 2
                    sp.wait_ge(f_gate.sem, f_gate.at(k2, 0))
                    sp.sem_inc(spare, 1)
                    sp.dma_start(xr[:], scratch["xrT"][:, bass.ds(k2 * ST, HALO + ST)]).then_inc(xr_ld.sem, 16)
                if has_output(kk):
                    sp.wait_ge(xg_st.sem, xg_st.at(k))
                    sp.sem_inc(spare, 1)
                    sp.wait_ge(o_ok.sem, o_ok.at(k, 0))
                    sp.sem_inc(spare, 1)
                    sp.dma_start(zg[:].rearrange("p a b -> p (a b)"),
                                 scratch["xg"][bass.ds(k * P, P), :]).then_inc(zg_ld.sem, 16)
                    sp.wait_ge(sg_ok.sem, sg_ok.at(k, 0))
                    sp.sem_inc(spare, 1)
                    sp.dma_start(xn[:], scratch["xnT"][:, bass.ds(k * ST, ST)]).then_inc(zg_ld.sem, 16)
                    sp.dma_start(g[:], scratch["gT"][:, bass.ds(k * ST, ST)]).then_inc(zg_ld.sem, 16)
                if has_inner(kk):
                    sp.wait_ge(gs_ok.sem, gs_ok.at(k2))
                    sp.sem_inc(spare, 1)
                    sp.dma_start(scratch["xg"][bass.ds(k2 * P, P), :],
                                 xg[:].rearrange("p a b -> p (a b)")).then_inc(xg_st.sem, 16)
                if has_output(kk):
                    sp.wait_ge(tok_ok.sem, tok_ok.at(k))
                    sp.sem_inc(spare, 1)
                    for q in range(3):
                        n = min(P, ST - q * P)
                        sp.dma_start(scratch["sg"][bass.ds(k * ST + q * P, n), :],
                                     tok[0:n, q]).then_inc(tok_st.sem, 16)

            in_pairs(sp, NC, -2, body)
            sp.wait_ge(tok_st.sem, tok_st.at(NC - 1, 3))
            sp.sem_inc(spare, 1)

        @block.gpsimd
        def _(pool):
            pool.memset(cst[:, 0], 0.5).then_inc(consts, 1)
            pool.memset(cst[:, 1], -1.0).then_inc(consts, 1)
            h_ok.give(pool)
            pool.wait_ge(consts, 5)

            def body(k, p, kk):
                if not has_drive(kk):
                    return
                k1, q = k + 1, 1 - p
                step = [0]

                def link(ins):
                    step[0] += 1
                    ins.then_inc(pch.sem, 1)
                    pool.wait_ge(pch.sem, pch.at(k1, step[0]))
                    if step[0] in (3, 5):
                        pool.sem_inc(spare, 1)

                def at(buf, par, s):
                    return buf[:, par, :, s * B:(s + 1) * B]

                pool.wait_ge(dA_ok.sem, dA_ok.at(k1, 4))
                pool.wait_ge(b_rd.sem, b_rd.at(k1, NP))
                link(pool.tensor_tensor(at(dA, q, 0), at(dA, q, 0), at(h, 1 - q, STEPS - 1), ALU.mult))
                link(pool.tensor_tensor(at(h, q, 0), at(h, q, 0), at(dA, q, 0), ALU.add))
                pool.sem_inc(st0_ok.sem, 1)
                pool.wait_ge(n2_ok.sem, n2_ok.at(k1))
                link(pool.tensor_tensor(n2[:, 1], n2[:, 0], cst[:, 0], ALU.pow))
                link(pool.tensor_scalar(n2[:, 2], n2[:, 1], 1e-8, None, ALU.add))
                link(pool.tensor_tensor(n2[:, 1], n2[:, 2], cst[:, 1], ALU.pow))
                link(pool.tensor_scalar(n2[:, 3], n2[:, 1], 20.0, 1.0, ALU.mult, ALU.min))
                pool.tensor_tensor(at(h, q, 0), at(h, q, 0),
                                   n2[:, 3].unsqueeze(1).broadcast_to([P, 2 * NS, B]), ALU.mult).then_inc(pch.sem, 1)
                step[0] += 1
                pool.wait_ge(pch.sem, pch.at(k1, step[0]))
                for s in range(1, STEPS):
                    link(pool.tensor_tensor(at(dA, q, s), at(dA, q, s), at(h, q, s - 1), ALU.mult))
                    link(pool.tensor_tensor(at(h, q, s), at(h, q, s), at(dA, q, s), ALU.add))
                pool.sem_inc(h_ok.sem, 1)
                assert step[0] == PCH, step[0]

            in_pairs(pool, NC, -2, body)

        @block.tensor
        def _(pe):
            f_gate.give(pe)
            f_t.give(pe)
            prod_rd.give(pe)
            o_ok.give(pe)
            pe.wait_ge(w_load, 16 * NW)
            pe.wait_ge(consts, 5)
            pe.wait_ge(setup, 5)

            def spread(k, bc, par, m):
                for e in range(2):
                    n = 2 * m + e
                    mm = pe.matmul(X[:, m % 2, e, 0:ST], pick[:, n:n + 1].broadcast_to([96, P]),
                                   bcT[:, par, bc, :], start=True, stop=True)
                return mm

            def body(k, p, kk):
                if has_drive(kk):
                    k1 = k + 1
                    pe.wait_ge(bcT_ok.sem, bcT_ok.at(k1))
                    for m in range(NP):
                        if m >= 2:
                            pe.wait_ge(b_rd.sem, b_rd.at(k1, m - 1))
                        elif kk is None or kk > 0:
                            pe.wait_ge(prod_ok.sem, prod_ok.at(k - 1, 2 * (m + NP - 1)))
                        spread(k1, 0, 1 - p, m).then_inc(b_ok.sem, 1)
                    pe.wait_ge(nr_ok.sem, nr_ok.at(k1))
                    pe.matmul(NORM, ones[:], nrm[:], start=True, stop=True).then_inc(n2_ps.sem, 1)

                def inner(part):
                    k2 = k + 2
                    if part == 0:
                        pe.wait_ge(xr_ld.sem, xr_ld.at(k2))
                        pe.wait_ge(bcT_ok.sem, bcT_ok.at(k2, 0))
                        if has_drive(kk):
                            pe.wait_ge(n2_ok.sem, n2_ok.at(k + 1))
                        for c in range(2):
                            for t in range(4):
                                mm = pe.matmul(F[:, c, 0:ST], conv_w[:, t, c * P:(c + 1) * P],
                                               xr[:, t * B:t * B + ST], start=(t == 0), stop=(t == 3))
                        mm.then_inc(f_conv.sem, 1)
                    elif part == 1:
                        pe.wait_ge(a_conv.sem, a_conv.at(k2))
                        for c in range(2):
                            mm = pe.matmul(F[:, c, 0:ST], gate_w[:, c * P:(c + 1) * P], xr[:, HALO:HALO + ST],
                                           start=True, stop=True)
                        mm.then_inc(f_gate.sem, 1)
                    elif part == 2:
                        pe.wait_ge(gs_ok.sem, gs_ok.at(k2))
                        for c in range(2):
                            for i in range(2):
                                mm = pe.matmul(F[:, c, 0:ST], dt_w[:, i, c * P:(c + 1) * P], xg[:, i],
                                               start=(i == 0), stop=(i == 1))
                        mm.then_inc(f_dt.sem, 1)
                    elif part == 3:
                        pe.wait_ge(v_ok.sem, v_ok.at(k2))
                        for q in range(NQ):
                            for i in range(2):
                                mm = pe.matmul(F[0:64, 0, q * 32:(q + 1) * 32], xg[:, i, q * 64:(q + 1) * 64],
                                               bc_w[:, i], start=(i == 0), stop=(i == 1))
                        mm.then_inc(f_bc.sem, 1)
                    else:
                        pe.wait_ge(s3_ok.sem, s3_ok.at(k2))
                        pe.sem_inc(spare, 1)
                        for q in range(NQ):
                            for bc in range(2):
                                mm = pe.transpose(Fb[0:96, bc * ST + q * 64:bc * ST + (q + 1) * 64], s3[:, q, bc],
                                                  ident_b[:])
                        mm.then_inc(f_t.sem, 1)

                def spread_c(m):
                    if m >= 2:
                        pe.wait_ge(prod_ok.sem, prod_ok.at(k, 2 * (m - 1)))
                    elif has_drive(kk):
                        pe.wait_ge(b_rd.sem, b_rd.at(k + 1, m + NP - 1))
                    else:
                        pe.wait_ge(prod_ok.sem, prod_ok.at(k - 1, 2 * (m + NP - 1)))
                    spread(k, 1, p, m).then_inc(c_ok.sem, 1)

                def sum_states(m):
                    if m == 0:
                        pe.wait_ge(tok_ok.sem, tok_ok.at(k, 0))
                    for c in range(2):
                        pe.wait_ge(prod_ok.sem, prod_ok.at(k, 2 * m + c + 1))
                        for e in range(2):
                            mm = pe.matmul(Y[:, c, 0:ST], ident[:], prod[:, c, e], start=(m == 0 and e == 0),
                                           stop=(m == NP - 1 and e == 1))
                        mm.then_inc(prod_rd.sem, 1)

                if has_inner(kk):
                    inner(0)
                if has_output(kk):
                    spread_c(0)
                for m in range(NP):
                    if has_output(kk):
                        if m + 1 < NP:
                            spread_c(m + 1)
                        sum_states(m)
                    if has_inner(kk) and m in (1, 2, 4):
                        inner({1: 1, 2: 2, 4: 3}[m])
                if has_inner(kk):
                    inner(4)
                if has_output(kk):
                    pe.wait_ge(yy_ok.sem, yy_ok.at(k))
                    for i in range(2):
                        mm = pe.matmul(Y[:, 0, 0:ST], out_w[:, i], zg[:, i], start=(i == 0), stop=(i == 1))
                    mm.then_inc(o_ok.sem, 1)
                    pe.wait_ge(sg_ok.sem, sg_ok.at(k))
                    for q in range(3):
                        n = min(P, ST - q * P)
                        mm = pe.transpose(Y[0:n, 1, q * P:(q + 1) * P], xn[:, q * P:q * P + n], ident[:])
                    mm.then_inc(o_tp.sem, 1)

            in_pairs(pe, NC, -2, body)

        @block.scalar
        def _(act):
            bcT_ok.give(act)
            dA_ok.give(act)
            tok_ok.give(act)
            act.wait_ge(w_load, 16 * NW)
            act.activation(a16[:], a_log, ACT.Tanh, scale=0.5 / (5.0 + 1e-8)).then_inc(aset, 1)
            act.activation(col2[:, 3:4], cols[:, 6:7], ACT.Tanh, scale=0.5).then_inc(aset, 1)
            act.wait_ge(aset, 2)
            act.activation(a16[:], a16[:], ACT.Exp, scale=10.0).then_inc(aset, 1)
            act.wait_ge(setup, 5)
            act.wait_ge(consts, 5)

            def body(k, p, kk):
                if has_drive(kk):
                    k1, q = k + 1, 1 - p
                    act.wait_ge(dt_ok.sem, dt_ok.at(k1))
                    if kk is None or kk >= 1:
                        act.wait_ge(h_ok.sem, h_ok.at(k - 1))
                    for j in range(2 * NS):
                        act.activation(dA[:, q, j], dt[:, j // NS], ACT.Tanh, scale=a16[:, j:j + 1]).then_inc(a_th.sem, 1)
                    act.wait_ge(a_th.sem, a_th.at(k1, 2 * NS))
                    for j in range(4):
                        act.activation(dA[:, q, 8 * j:8 * j + 8], dA[:, q, 8 * j:8 * j + 8], ACT.Exp,
                                       scale=16.0).then_inc(dA_ok.sem, 1)
                    act.wait_ge(st0_ok.sem, st0_ok.at(k1))
                    act.activation(dA[:, q, :, 0:B], h[:, q, :, 0:B], ACT.Square).then_inc(sq_ok.sem, 1)
                    act.wait_ge(n2_ps.sem, n2_ps.at(k1))
                    act.activation(n2[:, 0], NORM, ACT.Copy).then_inc(n2_ok.sem, 1)
                if has_inner(kk):
                    k2 = k + 2
                    act.wait_ge(f_conv.sem, f_conv.at(k2))
                    act.wait_ge(dt_ok.sem, dt_ok.at(k2, 0))
                    for c in range(2):
                        act.activation(th[:, c], F[:, c, 0:ST], ACT.Tanh, bias=col2[:, c:c + 1], scale=0.5)
                    act.activation(z[:, 0], F[:, 0, 0:ST], ACT.Identity, bias=col2[:, 0:1], scale=0.5)
                    act.activation(z[:, 1], F[:, 1, 0:ST], ACT.Identity, bias=col2[:, 1:2],
                                   scale=0.5).then_inc(a_conv.sem, 1)
                    act.wait_ge(f_gate.sem, f_gate.at(k2))
                    act.wait_ge(xc_ok.sem, xc_ok.at(k2))
                    act.activation(th[:], F[:, :, 0:ST], ACT.Tanh, scale=0.5).then_inc(a_gate.sem, 1)
                    act.wait_ge(v_ok.sem, v_ok.at(k2))
                    act.activation(th[:], z[:], ACT.Abs).then_inc(a_exp.sem, 1)
                    act.wait_ge(a_exp.sem, a_exp.at(k2, 1))
                    act.activation(th[:], th[:], ACT.Exp, scale=-1.0).then_inc(a_exp.sem, 1)
                    act.wait_ge(a_exp.sem, a_exp.at(k2, 2))
                    act.activation(th[:], th[:], ACT.Ln, bias=1.0).then_inc(a_ln.sem, 1)
                    act.wait_ge(sp_ok.sem, sp_ok.at(k2))
                    act.activation(th[:], z[:], ACT.Tanh, bias=col2[:, 2:3], scale=A_DT).then_inc(a_dt.sem, 1)
                    act.wait_ge(f_t.sem, f_t.at(k2))
                    act.activation(bcT[:, p].rearrange("p a b -> p (a b)"), Fb[0:96, 0:2 * ST],
                                   ACT.Copy).then_inc(bcT_ok.sem, 1)
                if has_output(kk):
                    act.wait_ge(o_tp.sem, o_tp.at(k))
                    act.wait_ge(tok_st.sem, tok_st.at(k, 0))
                    act.activation(tok[:, 0:2], Y[:, 1, 0:2 * D], ACT.Copy)
                    act.activation(tok[0:64, 2], Y[0:64, 1, 2 * D:3 * D], ACT.Copy).then_inc(tok_ok.sem, 1)

            in_pairs(act, NC, -2, body)

        @block.vector
        def _(v):
            dt_ok.give(v)
            prod_ok.give(v)
            sg_ok.give(v)
            v.memset(s3[:], 0.0).then_inc(consts, 1)
            v.memset(h[:, 1, :, (STEPS - 1) * B:], 0.0).then_inc(consts, 1)
            v.memset(col2[:, 2:3], -C_DT * A_DT).then_inc(consts, 1)
            v.wait_ge(w_load, 16 * NW)
            v.tensor_scalar(col2[:, 0:2], cols[:, 0:2], 0.5, None, ALU.mult).then_inc(setup, 1)
            v.tensor_scalar(w_in, w_in, cols[:, 7:8], None, ALU.mult).then_inc(vset, 1)
            v.wait_ge(vset, 1)
            v.tensor_tensor(conv_w[:], taps.rearrange("p (t c) -> p t c", t=4),
                            w_in[:, 0:DI].unsqueeze(1).broadcast_to([P, 4, DI]), ALU.mult).then_inc(setup, 1)
            v.tensor_copy(gate_w[:], w_in[:, DI:2 * DI]).then_inc(setup, 1)
            v.wait_ge(aset, 3)
            v.tensor_scalar(a16[:], a16[:], -1.0 / 16, None, ALU.mult).then_inc(setup, 1)
            v.tensor_scalar(col2[:, 3:4], col2[:, 3:4], 0.125, 0.125, ALU.mult, ALU.add).then_inc(setup, 1)
            v.wait_ge(setup, 5)
            v.wait_ge(consts, 5)

            def body(k, p, kk):
                step = [0]

                def link(ins):
                    step[0] += 1
                    ins.then_inc(vch.sem, 1)
                    v.wait_ge(vch.sem, vch.at(k + 2, step[0]))

                if has_drive(kk):
                    k1, q = k + 1, 1 - p
                    for m in range(NP):
                        v.wait_ge(b_ok.sem, b_ok.at(k1, m + 1))
                        v.tensor_tensor(h[:, q, 2 * m:2 * m + 2], X[:, m % 2, :, 0:ST],
                                        dtx[:, 0].unsqueeze(1).broadcast_to([P, 2, ST]), ALU.mult)
                        v.tensor_tensor(h[:, q, NS + 2 * m:NS + 2 * m + 2], X[:, m % 2, :, 0:ST],
                                        dtx[:, 1].unsqueeze(1).broadcast_to([P, 2, ST]), ALU.mult).then_inc(b_rd.sem, 1)
                    v.wait_ge(sq_ok.sem, sq_ok.at(k1))
                    v.tensor_reduce(nrm[:], dA[:, q, :, 0:B].rearrange("p j b -> p b j"), AX.X,
                                    ALU.add).then_inc(nr_ok.sem, 1)

                def inner(part):
                    k2 = k + 2
                    if part == 0:
                        v.wait_ge(a_conv.sem, a_conv.at(k2))
                        v.wait_ge(xg_st.sem, xg_st.at(k2, 0))
                        v.scalar_tensor_tensor(xg[:, 0:2], th[:], 1.0, z[:], ALU.add, ALU.mult).then_inc(xc_ok.sem, 1)
                    elif part == 1:
                        v.wait_ge(a_gate.sem, a_gate.at(k2))
                        v.scalar_tensor_tensor(xg[:, 2:4], th[:], 1.0, F[:, :, 0:ST], ALU.add,
                                               ALU.mult).then_inc(gs_ok.sem, 1)
                    elif part == 2:
                        v.wait_ge(f_dt.sem, f_dt.at(k2))
                        v.tensor_scalar(z[:, 0], F[:, 0, 0:ST], cols[:, 2:3], None, ALU.add)
                        v.tensor_scalar(z[:, 1], F[:, 1, 0:ST], cols[:, 3:4], None, ALU.add).then_inc(v_ok.sem, 1)
                    elif part == 3:
                        v.wait_ge(a_ln.sem, a_ln.at(k2))
                        v.scalar_tensor_tensor(z[:], z[:], 0.0, th[:], ALU.max, ALU.add).then_inc(sp_ok.sem, 1)
                    elif part == 4:
                        v.wait_ge(a_dt.sem, a_dt.at(k2))
                        v.wait_ge(dA_ok.sem, dA_ok.at(k2, 0))
                        link(v.tensor_scalar(dt[:], th[:], 2 * R_DT, C_DT, ALU.mult, ALU.add))
                        v.tensor_tensor(dtx[:], dt[:], xg[:, 0:2], ALU.mult).then_inc(dt_ok.sem, 1)
                    else:
                        src = F[0:64, 0, 0:NQ * 2 * NS].rearrange("p (q c n) -> p q c n", q=NQ, c=2)
                        v.wait_ge(f_bc.sem, f_bc.at(k2))
                        v.wait_ge(f_t.sem, f_t.at(k2, 0))
                        link(v.tensor_copy(s3[:, :, :, 0:NS], src))
                        link(v.tensor_tensor(rest[:], src, s3[:, :, :, 0:NS], ALU.subtract))
                        link(v.tensor_copy(s3[:, :, :, 32:32 + NS], rest[:]))
                        link(v.tensor_tensor(rest[:], rest[:], s3[:, :, :, 32:32 + NS], ALU.subtract))
                        v.tensor_copy(s3[:, :, :, 64:64 + NS], rest[:]).then_inc(s3_ok.sem, 1)

                for m in range(NP):
                    if has_output(kk):
                        if m == 0:
                            v.wait_ge(h_ok.sem, h_ok.at(k))
                        v.wait_ge(c_ok.sem, c_ok.at(k, m + 1))
                        for c in range(2):
                            v.wait_ge(prod_rd.sem, prod_rd.at(k, 2 * m + c - 1))
                            v.tensor_tensor(prod[:, c], h[:, p, c * NS + 2 * m:c * NS + 2 * m + 2],
                                            X[:, m % 2, :, 0:ST], ALU.mult).then_inc(prod_ok.sem, 1)
                    if has_inner(kk) and m in (0, 2, 3, 4, 5, 6):
                        inner((0, None, 1, 2, 3, 4, 5)[m])
                if has_output(kk):
                    v.wait_ge(zg_ld.sem, zg_ld.at(k, 3))
                    v.wait_ge(prod_rd.sem, prod_rd.at(k, 2 * NP))
                    link(v.scalar_tensor_tensor(zg[:, 0], zg[:, 0], cols[:, 4:5], Y[:, 0, 0:ST], ALU.mult, ALU.add))
                    link(v.scalar_tensor_tensor(zg[:, 1], zg[:, 1], cols[:, 5:6], Y[:, 1, 0:ST], ALU.mult, ALU.add))
                    v.tensor_tensor(zg[:, 0:2], zg[:, 0:2], zg[:, 2:4], ALU.mult).then_inc(yy_ok.sem, 1)
                    v.wait_ge(o_ok.sem, o_ok.at(k))
                    link(v.scalar_tensor_tensor(xn[:], Y[:, 0, 0:ST], col2[:, 3:4], xn[:], ALU.mult, ALU.add))
                    v.tensor_tensor(xn[:], xn[:], g[:], ALU.mult).then_inc(sg_ok.sem, 1)
                for _ in range(8 - step[0]):
                    v.sem_inc(vch.sem, 1)

            in_pairs(v, NC, -2, body)


def attention_phase(nc, io, scratch, out):
    SC = float(np.float32(1.0) / np.sqrt(np.float32(8.0)))
    CH = 32
    HC = 8
    HT = HC * CH
    G = 4
    with ExitStack() as ctx:
        def sb(name, shape, dt=F32):
            return ctx.enter_context(nc.sbuf_tensor("a_" + name, shape, dt))

        def ps(name, shape, dt=F32):
            return ctx.enter_context(nc.psum_tensor("a_" + name, shape, dt))

        def cnt(name, per, credit=0, by=1):
            return Count(ctx, nc, "a_" + name, per, credit, by)

        def sem(name):
            return ctx.enter_context(nc.semaphore("a_" + name))

        w = sb("w", [P, 8, D])
        wt = sb("wt", [P, D])
        tern = sb("tern", [P, 4])
        ident = sb("ident", [P, P])
        ones = sb("ones", [P, P])
        jmask = sb("jmask", [P, 4])
        vmask = sb("vmask", [P, 4])
        osum = sb("osum", [P, CH])
        bmask = sb("bmask", [P, CH])
        mhalf = sb("mhalf", [P, MQ])
        x_in = sb("x_in", [P, 2, MQ, D])
        sg_in = sb("sg_in", [P, 2, MQ, D])
        x1 = sb("x1", [P, 2, MQ, D])
        xn = sb("xn", [P, MQ, D])
        stats = sb("stats", [P, MQ, 6])
        mv = sb("mv", [P, MQ, 2])
        rstd = sb("rstd", [P, 2, MQ])
        xnT = sb("xnT", [P, 2, MT])
        qm = sb("qm", [P, 2 * HC, 4, CH])
        kT = sb("kT", [P, MT])
        x4 = sb("x4", [P, 2 * HC, 4, CH])
        vb = sb("vb", [P, 2, HC * G, CH])
        mx = sb("mx", [P, G * HC])
        e = sb("e", [P, 2, G, HC, CH])
        eT = sb("eT", [P, 2, G, HC, CH])
        rden = sb("rden", [P, HT])
        ctxT = sb("ctxT", [P, 2, HT])
        ch = sb("ch", [P, 2, 2, HT])
        means = sb("means", [P, B * HC])
        gT = sb("gT", [P, B * HC])

        S = ps("S", [P, G, 512])
        V = ps("V", [P, HC, D])
        C = ps("C", [P, 2, HT])
        TB = ps("TB", [P, MT])

        w_load, power_ok, consts, wsum, wchain, spare = (
            sem(n) for n in ("w_load", "power_ok", "consts", "wsum", "wchain", "spare"))
        x_ld = cnt("x_ld", 3, by=16)
        x_rd = cnt("x_rd", 1, 2)
        x1_ok = cnt("x1_ok", 1)
        x1_st = cnt("x1_st", 1, 32, by=16)
        moments = cnt("moments", 1)
        rstd_ok = cnt("rstd_ok", 1)
        pchain = cnt("pchain", 1)
        xn_ok = cnt("xn_ok", 1)
        tp = cnt("tp", 1, 1)
        xnT_ok = cnt("xnT_ok", 1)
        xnT_st = cnt("xnT_st", 1, 32, by=16)
        x4_ok = cnt("x4_ok", 1)
        q_ps = cnt("q_ps", 1)
        qm_ok = cnt("qm_ok", 1)
        k_ps = cnt("k_ps", 1)
        kT_ok = cnt("kT_ok", 1)
        v_ps = cnt("v_ps", 2)
        vb_ok = cnt("vb_ok", 2, 1)
        s_ps = cnt("s_ps", 2)
        mx_ok = cnt("mx_ok", 2)
        sub_ok = cnt("sub_ok", 2, 1)
        ex_ok = cnt("ex_ok", 2)
        eT_ok = cnt("eT_ok", 2)
        av_ps = cnt("av_ps", 2, 2)
        rd_ok = cnt("rd_ok", 2)
        ctx_ok = cnt("ctx_ok", 2, 1)
        o_ps = cnt("o_ps", 2)
        ch_ok = cnt("ch_ok", 2, 1)
        sum_ok = sem("sum_ok")
        ch_st = cnt("ch_st", 1, 32, by=16)
        dch = cnt("dch", 1)
        means_ok, g_ok = sem("means_ok"), sem("g_ok")
        f_ld = Alternate(ctx, nc, "a_f_ld", 3)
        f_ps = cnt("f_ps", 1)
        f_sl = cnt("f_sl", 1)
        f_en = cnt("f_en", 1)
        f_pr = cnt("f_pr", 1)
        f_tp = cnt("f_tp", 1, 2)
        f_out = cnt("f_out", 1, 2)
        f_st = Alternate(ctx, nc, "a_f_st", 1, 16)

        loads = [(w[:], "attn_w"), (wt[:], "tern_w"), (ident[:], "ident"), (ones[:], "ones"), (jmask[:], "jmask"),
                 (vmask[:], "vmask"), (osum[:], "osum"), (bmask[:], "bmask")]
        NW = len(loads)
        x_bt = io["x_bt"]
        sg_bt = scratch["sg"].rearrange("(t b) d -> b t d", b=B)

        def has_front(kk):
            return kk is None or kk + 1 < MCH

        def has_main(kk):
            return kk is None or kk >= 0

        block = ctx.enter_context(nc.Block())

        @block.sync
        def _(sp):
            for dst, src in loads:
                sp.dma_start(dst, io[src]).then_inc(w_load, 16)
            for c in (x1_st, xnT_st, ch_st, f_st):
                c.give(sp)

            def wait(c, value):
                sp.wait_ge(c.sem, value)
                sp.sem_inc(spare, 1)

            def body(k, p, kk):
                k1, n = k + 1, 1 - p
                if has_front(kk):
                    wait(x_rd, x_rd.at(k1, -1))
                    sp.dma_start(x_in[:, n], x_bt[bass.ds(k1 * MT, MT), :].rearrange(
                        "(q p) d -> p q d", p=P)).then_inc(x_ld.sem, 16)
                    for b in range(2):
                        sp.dma_start(sg_in[:, n, 2 * b:2 * b + 2], sg_bt[bass.ds(k1 * 2 + b, 1), 0:L, :].rearrange(
                            "o (q p) d -> p (o q) d", p=P)).then_inc(x_ld.sem, 16)
                    wait(x1_ok, x1_ok.at(k1))
                    sp.dma_start(scratch["x1"][:, bass.ds(k1 * MT, MT)],
                                 x1[:, n].rearrange("p q d -> p (q d)")).then_inc(x1_st.sem, 16)
                    wait(xnT_ok, xnT_ok.at(k1))
                    sp.dma_start(scratch["xnT1"][:, bass.ds(k1 * MT, MT)], xnT[:, n]).then_inc(xnT_st.sem, 16)
                if has_main(kk):
                    wait(ch_ok, ch_ok.at(k, 2))
                    sp.dma_start(scratch["ch"][:, bass.ds(k * MT, MT)],
                                 ch[:, p].rearrange("p a b -> p (a b)")).then_inc(ch_st.sem, 16)

            in_pairs(sp, MCH, -1, body)
            for c in (x1_st, xnT_st, ch_st):
                sp.wait_ge(c.sem, c.at(MCH - 1))
            sp.wait_ge(means_ok, 1)

            def load(k, p):
                wait(f_out, f_out.at(k, -1))
                for dst, src in ((x_in[:, p].rearrange("p q d -> p (q d)"), "x1"), (xnT[:, p], "xnT1"),
                                 (ch[:, p].rearrange("p a b -> p (a b)"), "ch")):
                    sp.dma_start(dst, scratch[src][:, bass.ds(k * MT, MT)]).then_inc(f_ld.sems[p], 16)

            def last(k, p, kk):
                if kk is None or kk + 1 < MCH:
                    load(k + 1, 1 - p)
                wait(f_out, f_out.at(k))
                sp.dma_start(out[bass.ds(k * MT, MT), :].rearrange("(q p) d -> p q d", p=P),
                             x1[:, p]).then_inc(f_st.sems[p], 16)

            load(0, 0)
            in_pairs(sp, MCH, 0, last)
            for p in range(2):
                sp.wait_ge(f_st.sems[p], f_st.at(MCH - 2 + p, p))

        @block.gpsimd
        def _(pool):
            pool.memset(mhalf[:], -0.5).then_inc(power_ok, 1)
            pool.wait_ge(power_ok, 1)

            def body(k, p, kk):
                if has_front(kk):
                    k1 = k + 1
                    pool.wait_ge(moments.sem, moments.at(k1))
                    pool.sem_inc(spare, 1)
                    pool.tensor_scalar(rstd[:, 1], mv[:, :, 1], 1e-5, None, ALU.add).then_inc(pchain.sem, 1)
                    pool.wait_ge(pchain.sem, pchain.at(k1))
                    pool.tensor_tensor(rstd[:, 0], rstd[:, 1], mhalf[:], ALU.pow).then_inc(rstd_ok.sem, 1)
                    pool.wait_ge(xnT_ok.sem, xnT_ok.at(k1))
                    pool.sem_inc(spare, 1)
                    pool.tensor_copy(x4[:], xnT[:, 1 - p].rearrange("p (c q) -> p c q", q=CH).unsqueeze(2).broadcast_to(
                        [P, 2 * HC, 4, CH])).then_inc(x4_ok.sem, 1)

            in_pairs(pool, MCH, -1, body)
            pool.wait_ge(means_ok, 1)
            pool.tensor_copy(x4[:, 0:HC], means[:].rearrange("p (c q) -> p c q", q=CH).unsqueeze(2).broadcast_to(
                [P, HC, 4, CH])).then_inc(x4_ok.sem, 1)

        @block.tensor
        def _(pe):
            tp.give(pe)
            av_ps.give(pe)
            f_tp.give(pe)
            pe.wait_ge(w_load, 16 * NW)

            def values_scores(k, hf, wv):
                pe.wait_ge(vb_ok.sem, vb_ok.at(k, hf))
                pe.wait_ge(x4_ok.sem, x4_ok.at(k))
                for c in range(HC):
                    mm = pe.matmul(V[:, c], x4[:, hf * HC + c].rearrange("p j q -> p (j q)"), wv,
                                   start=True, stop=True)
                mm.then_inc(v_ps.sem, 1)
                pe.wait_ge(qm_ok.sem, qm_ok.at(k))
                pe.wait_ge(kT_ok.sem, kT_ok.at(k))
                pe.wait_ge(sub_ok.sem, sub_ok.at(k, hf))
                for c in range(HC):
                    for g in range(G):
                        a = slice(32 * g, 32 * g + 32)
                        mm = pe.matmul(S[:, g, c * CH:(c + 1) * CH],
                                       qm[a, hf * HC + c].rearrange("p j q -> p (j q)"),
                                       kT[a, hf * HT + c * CH:hf * HT + (c + 1) * CH], start=True, stop=True)
                mm.then_inc(s_ps.sem, 1)

            def contexts(k, hf):
                pe.wait_ge(eT_ok.sem, eT_ok.at(k, hf + 1))
                pe.wait_ge(vb_ok.sem, vb_ok.at(k, hf + 1))
                pe.wait_ge(ctx_ok.sem, ctx_ok.at(k, hf))
                for g in range(G):
                    a = slice(32 * g, 32 * g + 32)
                    pe.matmul(C[a, 1], osum[:], eT[:, hf, g].rearrange("p c q -> p (c q)"), start=True, stop=True)
                for c in range(HC):
                    for g in range(G):
                        a = slice(32 * g, 32 * g + 32)
                        mm = pe.matmul(C[a, 0, c * CH:(c + 1) * CH], vb[:, hf, c * G + g], eT[:, hf, g, c],
                                       start=True, stop=True)
                mm.then_inc(av_ps.sem, 1)

            def project(k, hf, wo):
                pe.wait_ge(ctx_ok.sem, ctx_ok.at(k, hf + 1))
                pe.matmul(TB[:, 0:HT], wo, ctxT[:, hf], start=True, stop=True).then_inc(o_ps.sem, 1)

            def front(k1, n, part):
                if part == 0:
                    pe.wait_ge(xn_ok.sem, xn_ok.at(k1))
                    for q in range(MQ):
                        mm = pe.transpose(TB[:, q * P:(q + 1) * P], xn[:, q], ident[:])
                    mm.then_inc(tp.sem, 1)
                elif part == 1:
                    pe.wait_ge(xnT_ok.sem, xnT_ok.at(k1))
                    pe.matmul(TB[:], w[:, 0], xnT[:, n], start=True, stop=True).then_inc(q_ps.sem, 1)
                    pe.wait_ge(qm_ok.sem, qm_ok.at(k1))
                    pe.matmul(TB[:], w[:, 1], xnT[:, n], start=True, stop=True).then_inc(k_ps.sem, 1)

            def body(k, p, kk):
                k1, n = k + 1, 1 - p
                if has_main(kk):
                    values_scores(k, 0, w[:, 2])
                    values_scores(k, 1, w[:, 2])
                    contexts(k, 0)
                    pe.wait_ge(ch_ok.sem, ch_ok.at(k, 0))
                    project(k, 0, w[:, 3])
                if has_front(kk):
                    if has_main(kk):
                        pe.wait_ge(ch_ok.sem, ch_ok.at(k, 1))
                    front(k1, n, 0)
                if has_main(kk):
                    contexts(k, 1)
                if has_front(kk):
                    front(k1, n, 1)
                if has_main(kk):
                    if has_front(kk):
                        pe.wait_ge(kT_ok.sem, kT_ok.at(k1))
                    else:
                        pe.wait_ge(ch_ok.sem, ch_ok.at(k, 1))
                    project(k, 1, w[:, 3])

            in_pairs(pe, MCH, -1, body)

            K = MCH
            pe.wait_ge(means_ok, 1)
            pe.matmul(TB[:, 0:HT], w[:, 4], means[:], start=True, stop=True).then_inc(q_ps.sem, 1)
            pe.wait_ge(qm_ok.sem, qm_ok.at(K))
            pe.matmul(TB[:, 0:HT], w[:, 5], means[:], start=True, stop=True).then_inc(k_ps.sem, 1)
            values_scores(K, 0, w[:, 6])
            contexts(K, 0)
            pe.wait_ge(kT_ok.sem, kT_ok.at(K))
            project(K, 0, w[:, 7])
            pe.wait_ge(consts, 1)
            pe.matmul(V[:, 0, 0:1], ones[:], tern[:, 0:1], start=True, stop=True).then_inc(wsum, 1)

            pe.wait_ge(consts, 2)

            def last(k, p, kk):
                pe.wait_ge(f_ld.sems[p], f_ld.at(k, p, 3))
                pe.matmul(S[:, p], wt[:], xnT[:, p], start=True, stop=True).then_inc(f_ps.sem, 1)
                pe.wait_ge(f_pr.sem, f_pr.at(k))
                for q in range(MQ):
                    mm = pe.transpose(S[:, 2 + p, q * P:(q + 1) * P],
                                      ch[:, p].rearrange("p a b -> p (a b)")[:, q * P:(q + 1) * P], ident[:])
                mm.then_inc(f_tp.sem, 1)

            in_pairs(pe, MCH, 0, last)

        @block.scalar
        def _(act):
            vb_ok.give(act)
            act.wait_ge(w_load, 16 * NW)

            def half(k, hf):
                act.wait_ge(v_ps.sem, v_ps.at(k, hf + 1))
                act.wait_ge(av_ps.sem, av_ps.at(k, hf - 1))
                for j in range(4):
                    ins = act.activation(vb[:, hf, :, 8 * j:8 * j + 8],
                                         V[:].rearrange("p c (g j e) -> p (c g) j e", g=G, j=4)[:, :, j],
                                         ACT.Copy, scale=vmask[:, j:j + 1])
                ins.then_inc(vb_ok.sem, 1)
                act.wait_ge(sub_ok.sem, sub_ok.at(k, hf + 1))
                act.activation(e[:, hf], e[:, hf], ACT.Exp, scale=SC).then_inc(ex_ok.sem, 1)

            def queries(k1, nc_):
                act.wait_ge(q_ps.sem, q_ps.at(k1))
                for j in range(4):
                    ins = act.activation(qm[:, 0:nc_, j], TB[:, 0:nc_ * CH].rearrange("p (c q) -> p c q", q=CH),
                                         ACT.Copy, scale=jmask[:, j:j + 1])
                ins.then_inc(qm_ok.sem, 1)
                act.wait_ge(k_ps.sem, k_ps.at(k1))
                act.activation(kT[:, 0:nc_ * CH], TB[:, 0:nc_ * CH], ACT.Copy).then_inc(kT_ok.sem, 1)

            def body(k, p, kk):
                if has_main(kk):
                    half(k, 0)
                    half(k, 1)
                if has_front(kk):
                    k1 = k + 1
                    act.wait_ge(tp.sem, tp.at(k1))
                    act.wait_ge(xnT_st.sem, xnT_st.at(k1, -1))
                    act.activation(xnT[:, 1 - p], TB[:], ACT.Copy).then_inc(xnT_ok.sem, 1)
                    queries(k1, 2 * HC)

            in_pairs(act, MCH, -1, body)
            queries(MCH, HC)
            half(MCH, 0)

            def last(k, p, kk):
                act.wait_ge(f_ps.sem, f_ps.at(k))
                act.activation(sg_in[:, p].rearrange("p q d -> p (q d)"), S[:, p], ACT.Silu).then_inc(f_sl.sem, 1)

            in_pairs(act, MCH, 0, last)

        @block.vector
        def _(v):
            for c in (x_rd, sub_ok, ctx_ok, ch_ok, f_out):
                c.give(v)
            v.wait_ge(w_load, 16 * NW)
            v.tensor_reduce(tern[:, 0:1], wt[:], AX.X, ALU.add, apply_absolute_value=True).then_inc(consts, 1)

            def softmax_in(k, hf, masked=False):
                src = S[:, :, 0:HT].rearrange("p g (c q) -> p g c q", q=CH)
                v.wait_ge(s_ps.sem, s_ps.at(k, hf + 1))
                if masked:
                    for g in range(G):
                        v.tensor_tensor(e[:, hf, g], src[:, g], bmask[:].unsqueeze(1).broadcast_to([P, HC, CH]),
                                        ALU.add).then_inc(wchain, 1)
                    v.wait_ge(wchain, 4)
                    src = e[:, hf]
                v.tensor_reduce(mx[:].rearrange("p (g c) -> p g c", g=G), src, AX.X, ALU.max).then_inc(mx_ok.sem, 1)
                v.wait_ge(mx_ok.sem, mx_ok.at(k, hf + 1))
                v.tensor_tensor(e[:, hf], src, mx[:].rearrange("p (g c) -> p g c", g=G).unsqueeze(3).broadcast_to(
                    [P, G, HC, CH]), ALU.subtract).then_inc(sub_ok.sem, 1)

            def turn(k, hf):
                v.wait_ge(ex_ok.sem, ex_ok.at(k, hf + 1))
                v.wait_ge(av_ps.sem, av_ps.at(k, hf - 1))
                v.transpose(eT[:, hf].rearrange("p g c q -> p (g c q)"),
                            e[:, hf].rearrange("p g c q -> p (g c q)")).then_inc(eT_ok.sem, 1)

            def normalise(k, hf):
                v.wait_ge(av_ps.sem, av_ps.at(k, hf + 1))
                v.reciprocal(rden[:], C[:, 1]).then_inc(rd_ok.sem, 1)
                v.wait_ge(rd_ok.sem, rd_ok.at(k, hf + 1))
                v.tensor_tensor(ctxT[:, hf], C[:, 0], rden[:], ALU.mult).then_inc(ctx_ok.sem, 1)

            def residual(k, p, hf):
                v.wait_ge(o_ps.sem, o_ps.at(k, hf + 1))
                v.wait_ge(ch_st.sem, ch_st.at(k, -1))
                v.tensor_tensor(ch[:, p, hf], TB[:, 0:HT], xnT[:, p, hf * HT:(hf + 1) * HT],
                                ALU.add).then_inc(ch_ok.sem, 1)
                v.wait_ge(ch_ok.sem, ch_ok.at(k, hf + 1))
                v.sem_inc(spare, 1)
                v.tensor_reduce(means[:, bass.ds(k * (2 * HC) + hf * HC, HC)],
                                ch[:, p, hf].rearrange("p (c q) -> p c q", q=CH), AX.X, ALU.add).then_inc(sum_ok, 1)

            def front_sum(k1, n):
                v.wait_ge(x_ld.sem, x_ld.at(k1, 3))
                v.wait_ge(x1_st.sem, x1_st.at(k1, -1))
                v.tensor_tensor(x1[:, n], x_in[:, n], sg_in[:, n], ALU.add).then_inc(x1_ok.sem, 1)
                v.wait_ge(x1_ok.sem, x1_ok.at(k1))
                v.sem_inc(x_rd.sem, 1)
                for q in range(MQ):
                    ins = v.bn_stats(stats[:, q], x1[:, n, q])
                ins.then_inc(dch.sem, 1)
                v.wait_ge(dch.sem, dch.at(k1, 1))
                v.sem_inc(spare, 1)
                for q in range(MQ):
                    ins = v.bn_aggr(mv[:, q], stats[:, q])
                ins.then_inc(moments.sem, 1)

            def front_norm(k1, n):
                v.wait_ge(rstd_ok.sem, rstd_ok.at(k1))
                v.wait_ge(tp.sem, tp.at(k1, 0))
                for q in range(MQ):
                    ins = v.tensor_scalar(xn[:, q], x1[:, n, q], mv[:, q, 0:1], rstd[:, 0, q:q + 1],
                                          ALU.subtract, ALU.mult)
                ins.then_inc(xn_ok.sem, 1)

            def body(k, p, kk):
                k1, n = k + 1, 1 - p
                if has_main(kk):
                    softmax_in(k, 0)
                if has_front(kk):
                    front_sum(k1, n)
                if has_main(kk):
                    softmax_in(k, 1)
                    turn(k, 0)
                if has_front(kk):
                    front_norm(k1, n)
                if has_main(kk):
                    normalise(k, 0)
                    turn(k, 1)
                    residual(k, p, 0)
                    normalise(k, 1)
                    residual(k, p, 1)

            in_pairs(v, MCH, -1, body)
            K = MCH
            v.wait_ge(sum_ok, 2 * MCH)
            v.tensor_scalar(means[:], means[:], 1.0 / CH, None, ALU.mult).then_inc(means_ok, 1)
            softmax_in(K, 0, masked=True)
            turn(K, 0)
            normalise(K, 0)
            v.wait_ge(o_ps.sem, o_ps.at(K, 1))
            v.tensor_tensor(gT[:], TB[:, 0:HT], means[:], ALU.add).then_inc(g_ok, 1)
            v.wait_ge(wsum, 1)
            v.tensor_scalar(tern[:, 1:2], V[:, 0, 0:1], 1.0 / (D * D), 1e-5, ALU.mult, ALU.max).then_inc(wchain, 1)
            v.wait_ge(wchain, 5)
            v.reciprocal(tern[:, 2:3], tern[:, 1:2]).then_inc(wchain, 1)
            v.wait_ge(wchain, 6)
            v.tensor_scalar(wt[:], wt[:], tern[:, 2:3], 1.0, ALU.mult, ALU.min).then_inc(wchain, 1)
            v.wait_ge(wchain, 7)
            v.tensor_scalar(wt[:], wt[:], -1.0, 12582912.0, ALU.max, ALU.add).then_inc(wchain, 1)
            v.wait_ge(wchain, 8)
            v.tensor_scalar(wt[:], wt[:], 12582912.0, tern[:, 1:2], ALU.subtract, ALU.mult).then_inc(consts, 1)
            v.wait_ge(g_ok, 1)

            def last(k, p, kk):
                chp = ch[:, p].rearrange("p a (c q) -> p (a c) q", q=CH)
                v.wait_ge(f_ld.sems[p], f_ld.at(k, p, 3))
                v.tensor_tensor(chp, chp, gT[:, bass.ds(k * 2 * HC, 2 * HC)].unsqueeze(2).broadcast_to(
                    [P, 2 * HC, CH]), ALU.add).then_inc(f_en.sem, 1)
                v.wait_ge(f_sl.sem, f_sl.at(k))
                v.wait_ge(f_en.sem, f_en.at(k))
                v.tensor_tensor(chp, chp, sg_in[:, p].rearrange("p q (c t) -> p (q c) t", t=CH),
                                ALU.mult).then_inc(f_pr.sem, 1)
                v.wait_ge(f_tp.sem, f_tp.at(k))
                v.wait_ge(f_st.sems[p], f_st.at(k, p, 0))
                v.tensor_tensor(x1[:, p].rearrange("p q d -> p (q d)"), S[:, 2 + p],
                                x_in[:, p].rearrange("p q d -> p (q d)"), ALU.add).then_inc(f_out.sem, 1)

            in_pairs(v, MCH, 0, last)


def host_arrays(i):
    c = np.ascontiguousarray
    x = i["L0_attn_x"]
    out = {"x_tm": c(x.transpose(1, 0, 2).reshape(T, D)), "ident": np.eye(P, dtype=np.float32)}
    for n, a, s in (("gate_w", "L0_ffn_gate_w", "L0_ffn_sh_gate_w"), ("up_w", "L0_ffn_up_w", "L0_ffn_sh_up_w")):
        out[n] = c(np.concatenate([i[a].reshape(-1, D), i[s]], 0).T)
    down = np.concatenate([i["L0_ffn_down_w"].transpose(0, 2, 1).reshape(-1, D), i["L0_ffn_sh_down_w"].T], 0)
    out["down_w"] = c(down.reshape(NJ, P, D).transpose(1, 0, 2))
    out["router_w"] = c(i["L0_ffn_router_weight"].T)
    out["e_bias"] = c(np.broadcast_to(i["L0_ffn_e_bias"], (P, E_ALL)))
    w = lambda n: i["L0_attn_" + n]
    halves = lambda a: c(a.reshape(2, P, -1).transpose(1, 0, 2))
    out["w_in"] = c(w("W_in").T)
    out["taps"] = c(np.broadcast_to(w("conv_w")[:, 0].T.reshape(1, -1), (P, 4 * DI)))
    out["a_log"] = c(halves(w("A_log")).reshape(P, -1))
    out["dt_w"], out["out_w"] = halves(w("W_dt").T), halves(w("W_out").T)
    out["bc_w"] = halves(np.concatenate([w("W_B"), w("W_C")], 0).T)
    for n, a in (("conv_b", "conv_b"), ("b_dt", "b_dt"), ("d_param", "D_param")):
        out[n] = c(w(a).reshape(2, P).T)
    out["residual"] = c(np.broadcast_to(w("residual_scale").reshape(1, 1), (P, 1)))
    out["x_bt"] = c(x.reshape(T, D))
    out["attn_w"] = c(np.stack([i["L1_attn_W" + n + s] for s in ("_l", "_g") for n in "qkvo"], 1))
    out["tern_w"] = c(i["L1_ffn_weight"].T)
    out["norm_w"] = c(w("norm_w").reshape(P, 1))
    return out


def constants():
    bf16 = mybir.dt.np(BF16)
    sel = np.zeros((96, 8 * P), bf16)
    for a in range(3):
        for e in range(E_ALL):
            sel[32 * a + e, (e // 2) * P + (e % 2) * 64:(e // 2) * P + (e % 2) * 64 + 64] = 1
    pick = np.zeros((96, NS), bf16)
    for a in range(3):
        pick[32 * a:32 * a + NS] = np.eye(NS)
    row, head = np.arange(P), np.arange(4)
    bmask = np.where(row[:, None] % 32 // 8 == np.arange(32) // 8, 0.0, -1e30)
    return {"jmask": (row[:, None] // 8 % 4 == head).astype(np.float32),
            "vmask": (row[:, None] // 32 == head).astype(np.float32),
            "osum": (row[:, None] // 32 == np.arange(32) // 8).astype(np.float32),
            "bmask": bmask.astype(np.float32), "moe_sel": sel, "pick": pick, "ident_b": np.eye(64).astype(bf16),
            "ones": np.ones((P, P), np.float32)}


def program(nc, io, scratch, out):
    expert_phase(nc, io, scratch)
    scan_phase(nc, io, scratch)
    attention_phase(nc, io, scratch, out)


SCRATCH = (("xnT", (P, TP)), ("xrT", (P, HALO + TP)), ("gT", (P, TP)), ("xg", (NC * P, 4 * ST)), ("sg", (TP, D)),
           ("x1", (P, T)), ("xnT1", (P, T)), ("ch", (P, T)))


def kernel(**inputs):
    import concourse.bacc as bacc
    from concourse.bass_utils import run_bass_kernel_spmd

    arrays = {**host_arrays({k: np.asarray(v) for k, v in inputs.items()}), **constants()}
    nc = bacc.Bacc("TRN2", target_bir_lowering=False, num_devices=1, dynamic_dma_scratch_size=1024)
    io = {n: nc.dram_tensor("in_" + n, a.shape, mybir.dt.from_np(a.dtype), kind="ExternalInput").ap()
          for n, a in arrays.items()}
    scratch = {n: nc.dram_tensor(n, s, F32, kind="Internal").ap() for n, s in SCRATCH}
    out = nc.dram_tensor("out", (T, D), F32, kind="ExternalOutput").ap()
    program(nc, io, scratch, out)
    r = run_bass_kernel_spmd(nc, [{"in_" + n: a for n, a in arrays.items()}], core_ids=[0])
    return r.results[0]["out"].reshape(B, L, D)
```

```python
import numpy as np
from contextlib import ExitStack

import concourse.bass as bass
from concourse import mybir

F32 = mybir.dt.float32
BF16 = mybir.dt.bfloat16
ALU = mybir.AluOpType
ACT = mybir.ActivationFunctionType
AX = mybir.AxisListType

P = 128
B, L, D = 32, 256, 128
T = B * L
DI = 256
NS = 16
E_ALL, TOPK = 16, 4
GROUPS, TOPG = 4, 2
MOE_SCALE = 2.5

MT = 512
MCH = T // MT
MQ = MT // P
NJ = 9
JP = 24
STEPS = 10
NC = -(-L // STEPS)
ST = STEPS * B
TP = NC * ST
HALO = 3 * B


class Count:

    def __init__(self, ctx, nc, name, per, credit=0, by=1):
        self.sem, self.per, self.credit, self.by = ctx.enter_context(nc.semaphore(name)), per, credit, by

    def at(self, k, n=1):
        return k * (self.per * self.by) + (self.credit + n * self.by)

    def give(self, eng):
        eng.sem_inc(self.sem, self.credit)


class Alternate:

    def __init__(self, ctx, nc, name, per, credit=0):
        self.sems = [ctx.enter_context(nc.semaphore(f"{name}_{p}")) for p in range(2)]
        self.half, self.credit = per * 8, credit

    def at(self, k, p, n=1):
        return k * self.half + (self.credit - p * self.half + n * 16)

    def give(self, eng):
        for s in self.sems:
            eng.sem_inc(s, self.credit)


def in_pairs(eng, n, first, body, loop_from=0, tail=2):
    for k in range(first, loop_from):
        body(k, k % 2, k)
    loops = (n - tail - loop_from) // 2
    with eng.Fori(0, loops) as i:
        body(i * 2 + loop_from, 0, None)
        body(i * 2 + (loop_from + 1), 1, None)
    for k in range(loop_from + 2 * loops, n):
        body(k, k % 2, k)


def expert_phase(nc, io, scratch):
    with ExitStack() as ctx:
        def sb(name, shape, dt=F32):
            return ctx.enter_context(nc.sbuf_tensor("m_" + name, shape, dt))

        def ps(name, shape, dt=F32):
            return ctx.enter_context(nc.psum_tensor("m_" + name, shape, dt))

        def cnt(name, per, credit=0, by=1):
            return Count(ctx, nc, "m_" + name, per, credit, by)

        gate_w = sb("gate_w", [P, NJ * P])
        up_w = sb("up_w", [P, NJ * P])
        down_w = sb("down_w", [P, NJ, D])
        router_w = sb("router_w", [P, E_ALL])
        e_bias = sb("e_bias", [P, E_ALL])
        sel = sb("sel", [96, 8 * P], BF16)
        ident = sb("ident", [P, P])
        ahead = sb("ahead", [P, E_ALL])
        restart = sb("restart", [P, MQ * E_ALL])
        mhalf = sb("mhalf", [P, MQ])
        x_in = sb("x_in", [P, 2, MQ, D])
        xn = sb("xn", [P, MQ, D])
        xr = sb("xr", [P, MQ, D])
        stats = sb("stats", [P, MQ, 6])
        mv = sb("mv", [P, MQ, 2])
        pt = sb("pt", [P, 4, MQ])
        rstd = sb("rstd", [P, 2, MQ])
        xnT = sb("xnT", [P, 2, MT])
        xrT = sb("xrT", [P, MT])
        th = sb("th", [P, MQ, E_ALL])
        r = {n: sb("r_" + n, [P, MQ, E_ALL]) for n in
             ("sig", "sc", "msk", "gt", "eq", "cum", "sel", "tw", "c", "r1")}
        pairs = sb("pairs", [P, MQ * GROUPS, 6])
        gs = sb("gs", [P, MQ, GROUPS])
        wins = sb("wins", [P, MQ, GROUPS])
        cmp = sb("cmp", [P, MQ, GROUPS])
        top8 = sb("top8", [P, MQ, 8])
        room = sb("room", [P, MQ])
        den = sb("den", [P, MQ])
        hi = sb("hi", [P, MQ, E_ALL], BF16)
        c3 = sb("c3", [P, MQ, 96])
        cT = sb("cT", [96, 2, MT], BF16)
        sl = sb("sl", [P, 2, MT])
        hb = sb("hb", [P, 2, MT])
        hid = sb("hid", [P, 2, MT])
        g_out = sb("g_out", [P, 2, MT])
        zero = sb("zero", [P, P])

        pg = ps("pg", [P, 2, MT])
        pu = ps("pu", [P, 2, MT])
        pc = ps("pc", [P, MT])
        py = ps("py", [P, MT])
        pf = ps("pf", [P, 2, MT])

        w_load = ctx.enter_context(nc.semaphore("m_w_load"))
        consts = ctx.enter_context(nc.semaphore("m_consts"))
        spare = ctx.enter_context(nc.semaphore("m_spare"))
        zeroed = ctx.enter_context(nc.semaphore("m_zeroed"))
        pads = ctx.enter_context(nc.semaphore("m_pads"))
        x_load = cnt("x_load", 1, by=16)
        x_used = cnt("x_used", 1, 2)
        moments = cnt("moments", 1)
        rstd_ok = cnt("rstd_ok", 1)
        pchain = cnt("pchain", 7)
        xn_ok = cnt("xn_ok", 1)
        tp_n = cnt("tp_n", 1)
        tp_r = cnt("tp_r", 1)
        xnT_ok = cnt("xnT_ok", 1)
        xrT_ok = cnt("xrT_ok", 1)
        logits = cnt("logits", 1)
        th_ok = cnt("th_ok", 1)
        c3_ok = cnt("c3_ok", 1, 1)
        c_tp = cnt("c_tp", 1)
        cT_ok = cnt("cT_ok", 1, 1)
        xn_st = cnt("xn_st", 1, 32, by=16)
        xr_st = cnt("xr_st", 1, 16, by=16)
        gu_ok = cnt("gu_ok", NJ)
        sl_ok = cnt("sl_ok", NJ)
        hb_ok = cnt("hb_ok", NJ, 2)
        cb_ok = cnt("cb_ok", NJ - 1)
        hid_ok = cnt("hid_ok", NJ, 2)
        down_ok = cnt("down_ok", NJ, 2)
        g_ok = cnt("g_ok", 1, 1)
        g_st = cnt("g_st", 1, 32, by=16)
        dch = ctx.enter_context(nc.semaphore("m_dve_chain"))
        DCH = 57
        NW = 7

        block = ctx.enter_context(nc.Block())

        @block.sync
        def _(sp):
            for dst, src in ((gate_w, "gate_w"), (up_w, "up_w"), (down_w, "down_w"), (router_w, "router_w"),
                             (e_bias, "e_bias"), (sel, "moe_sel"), (ident, "ident")):
                sp.dma_start(dst[:], io[src]).then_inc(w_load, 16)
            xn_st.give(sp)
            xr_st.give(sp)
            g_st.give(sp)
            sp.wait_ge(zeroed, 1)
            sp.dma_start(scratch["xrT"][:, 0:HALO], zero[:, 0:HALO]).then_inc(pads, 16)
            for name, at in (("xrT", HALO + T), ("xnT", T), ("gT", T)):
                sp.dma_start(scratch[name][:, at:at + TP - T], zero[:, 0:TP - T]).then_inc(pads, 16)

            def body(k, p, kk):
                if kk is None or kk + 1 < MCH:
                    sp.wait_ge(x_used.sem, x_used.at(k + 1, -1))
                    sp.sem_inc(spare, 1)
                    sp.dma_start(x_in[:, 1 - p], io["x_tm"][bass.ds((k + 1) * MT, MT), :].rearrange(
                        "(q p) d -> p q d", p=P)).then_inc(x_load.sem, 16)
                    sp.wait_ge(xnT_ok.sem, xnT_ok.at(k + 1))
                    sp.sem_inc(spare, 1)
                    sp.dma_start(scratch["xnT"][:, bass.ds((k + 1) * MT, MT)], xnT[:, 1 - p]).then_inc(xn_st.sem, 16)
                    sp.wait_ge(xrT_ok.sem, xrT_ok.at(k + 1))
                    sp.sem_inc(spare, 1)
                    sp.dma_start(scratch["xrT"][:, bass.ds((k + 1) * MT + HALO, MT)], xrT[:]).then_inc(xr_st.sem, 16)
                if kk is None or kk >= 0:
                    sp.wait_ge(g_ok.sem, g_ok.at(k))
                    sp.sem_inc(spare, 1)
                    sp.dma_start(scratch["gT"][:, bass.ds(k * MT, MT)], g_out[:, p]).then_inc(g_st.sem, 16)

            in_pairs(sp, MCH, -1, body)
            sp.wait_ge(pads, 64)
            sp.wait_ge(xn_st.sem, xn_st.at(MCH - 1))
            sp.sem_inc(spare, 1)
            sp.wait_ge(xr_st.sem, xr_st.at(MCH - 1))
            sp.sem_inc(spare, 1)
            sp.wait_ge(g_st.sem, g_st.at(MCH - 1))
            sp.sem_inc(spare, 1)

        @block.gpsimd
        def _(pool):
            pool.memset(mhalf[:], -0.5).then_inc(consts, 1)
            pool.wait_ge(consts, 4)

            def body(k, p, kk):
                if kk is not None and kk + 1 >= MCH:
                    return
                k1 = k + 1
                step = [0]

                def link(ins):
                    step[0] += 1
                    ins.then_inc(pchain.sem, 1)
                    pool.wait_ge(pchain.sem, pchain.at(k1, step[0]))
                    if step[0] == 4:
                        pool.sem_inc(spare, 1)

                pool.wait_ge(moments.sem, moments.at(k1))
                pool.sem_inc(spare, 1)
                link(pool.tensor_scalar(pt[:, 0], mv[:, :, 1], 1e-5, None, ALU.add))
                link(pool.tensor_tensor(rstd[:, 0], pt[:, 0], mhalf[:], ALU.pow))
                link(pool.tensor_tensor(pt[:, 1], rstd[:, 0], rstd[:, 0], ALU.mult))
                link(pool.tensor_tensor(pt[:, 2], pt[:, 1], mv[:, :, 1], ALU.mult))
                link(pool.tensor_scalar(pt[:, 3], pt[:, 2], 1e-6, None, ALU.add))
                link(pool.tensor_tensor(pt[:, 1], pt[:, 3], mhalf[:], ALU.pow))
                link(pool.tensor_tensor(rstd[:, 1], pt[:, 1], rstd[:, 0], ALU.mult))
                pool.sem_inc(rstd_ok.sem, 1)

            in_pairs(pool, MCH, -1, body)

        @block.tensor
        def _(pe):
            pe.wait_ge(w_load, 16 * NW)
            pe.wait_ge(consts, 4)

            def gate_up(k, p, j):
                s = (p + j) % 2
                pe.wait_ge(hb_ok.sem, hb_ok.at(k, j - 1))
                pe.matmul(pg[:, s], gate_w[:, j * P:(j + 1) * P], xnT[:, p], start=True, stop=True)
                pe.matmul(pu[:, s], up_w[:, j * P:(j + 1) * P], xnT[:, p], start=True,
                          stop=True).then_inc(gu_ok.sem, 1)

            def spread(k, p, j):
                if j == 0:
                    pe.wait_ge(cT_ok.sem, cT_ok.at(k))
                pe.wait_ge(hid_ok.sem, hid_ok.at(k, j if j else -1))
                pe.matmul(pc[:], sel[:, j * P:(j + 1) * P], cT[:, p], start=True, stop=True).then_inc(cb_ok.sem, 1)

            def down(k, p, j):
                s = (p + j) % 2
                pe.wait_ge(hid_ok.sem, hid_ok.at(k, j + 1))
                if j == 0:
                    pe.wait_ge(g_ok.sem, g_ok.at(k, 0))
                pe.matmul(py[:], down_w[:, j], hid[:, s], start=(j == 0), stop=(j == NJ - 1)).then_inc(down_ok.sem, 1)

            def front(k, p, part):
                if part == 0:
                    pe.wait_ge(xn_ok.sem, xn_ok.at(k))
                    for q in range(MQ):
                        mm = pe.transpose(pf[:, 0, q * P:(q + 1) * P], xn[:, q], ident[:])
                    mm.then_inc(tp_n.sem, 1)
                    pe.wait_ge(cT_ok.sem, cT_ok.at(k, 0))
                    for q in range(MQ):
                        mm = pe.transpose(pf[:, 1, q * P:(q + 1) * P], xr[:, q], ident[:])
                    mm.then_inc(tp_r.sem, 1)
                elif part == 1:
                    pe.wait_ge(xnT_ok.sem, xnT_ok.at(k))
                    for q in range(MQ):
                        mm = pe.matmul(pf[:, 0, q * E_ALL:(q + 1) * E_ALL], xnT[:, p, q * P:(q + 1) * P],
                                       router_w[:], start=True, stop=True)
                    mm.then_inc(logits.sem, 1)
                else:
                    pe.wait_ge(c3_ok.sem, c3_ok.at(k))
                    pe.wait_ge(xrT_ok.sem, xrT_ok.at(k))
                    for q in range(MQ):
                        mm = pe.transpose(pf[0:96, 1, q * P:(q + 1) * P], c3[:, q], ident[:])
                    mm.then_inc(c_tp.sem, 1)

            def body(k, p, kk):
                has_front = kk is None or kk + 1 < MCH
                if kk is not None and kk < 0:
                    for part in range(3):
                        front(k + 1, 1 - p, part)
                    return
                gate_up(k, p, 0)
                for j in range(NJ):
                    if j < NJ - 1:
                        gate_up(k, p, j + 1)
                        spread(k, p, j)
                    if has_front and j == 2:
                        front(k + 1, 1 - p, 0)
                    if has_front and j == 4:
                        front(k + 1, 1 - p, 1)
                    down(k, p, j)
                if has_front:
                    front(k + 1, 1 - p, 2)

            in_pairs(pe, MCH, -1, body)

        @block.scalar
        def _(act):
            g_ok.give(act)
            cT_ok.give(act)

            def main(k, p, j):
                s = (p + j) % 2
                act.wait_ge(gu_ok.sem, gu_ok.at(k, j + 1))
                act.activation(sl[:, s], pg[:, s], ACT.Silu).then_inc(sl_ok.sem, 1)

            def front(k, p, part):
                if part == 0:
                    act.wait_ge(tp_n.sem, tp_n.at(k))
                    act.wait_ge(xn_st.sem, xn_st.at(k, -1))
                    act.activation(xnT[:, p], pf[:, 0], ACT.Copy).then_inc(xnT_ok.sem, 1)
                    act.wait_ge(tp_r.sem, tp_r.at(k))
                    act.wait_ge(xr_st.sem, xr_st.at(k, 0))
                    act.activation(xrT[:], pf[:, 1], ACT.Copy).then_inc(xrT_ok.sem, 1)
                elif part == 1:
                    act.wait_ge(logits.sem, logits.at(k))
                    act.wait_ge(c3_ok.sem, c3_ok.at(k, 0))
                    act.activation(th[:], pf[:, 0, 0:MQ * E_ALL], ACT.Tanh, scale=0.5).then_inc(th_ok.sem, 1)
                else:
                    act.wait_ge(c_tp.sem, c_tp.at(k))
                    act.activation(cT[:, p], pf[0:96, 1], ACT.Copy).then_inc(cT_ok.sem, 1)

            def body(k, p, kk):
                has_front = kk is None or kk + 1 < MCH
                if kk is not None and kk < 0:
                    for part in range(3):
                        front(k + 1, 1 - p, part)
                    return
                for j in range(NJ):
                    main(k, p, j)
                    if has_front and j == 3:
                        front(k + 1, 1 - p, 0)
                    if has_front and j == 5:
                        front(k + 1, 1 - p, 1)
                if has_front:
                    front(k + 1, 1 - p, 2)
                act.wait_ge(down_ok.sem, down_ok.at(k, NJ))
                act.wait_ge(g_st.sem, g_st.at(k, -1))
                act.activation(g_out[:, p], py[:], ACT.Silu).then_inc(g_ok.sem, 1)

            in_pairs(act, MCH, -1, body)

        @block.vector
        def _(v):
            x_used.give(v)
            c3_ok.give(v)
            hb_ok.give(v)
            hid_ok.give(v)
            v.sem_inc(down_ok.sem, 2)
            v.memset(c3[:], 0.0).then_inc(consts, 1)
            v.memset(restart[:], 1.0).then_inc(dch, 1)
            for i in range(GROUPS):
                v.memset(ahead[:].rearrange("p (q g) -> p q g", g=GROUPS)[:, :, i], float(i)).then_inc(dch, 1)
            v.wait_ge(dch, 5)
            v.memset(restart[:].rearrange("p (q e) -> p q e", e=E_ALL)[:, :, 0], 0.0).then_inc(consts, 1)
            v.memset(zero[:], 0.0).then_inc(zeroed, 1)
            v.wait_ge(zeroed, 1)
            v.memset(cmp[:], 0.0).then_inc(consts, 1)
            v.wait_ge(consts, 4)
            v.wait_ge(w_load, 16 * NW)
            link_base = 5

            def main(k, p, j):
                s = (p + j) % 2
                v.wait_ge(sl_ok.sem, sl_ok.at(k, j + 1))
                if j < NJ - 1:
                    v.tensor_tensor(hb[:, s], sl[:, s], pu[:, s], ALU.mult).then_inc(hb_ok.sem, 1)
                    v.wait_ge(hb_ok.sem, hb_ok.at(k, j + 1))
                    v.wait_ge(cb_ok.sem, cb_ok.at(k, j + 1))
                    v.wait_ge(down_ok.sem, down_ok.at(k, j - 1))
                    v.tensor_tensor(hid[:, s], hb[:, s], pc[:], ALU.mult).then_inc(hid_ok.sem, 1)
                else:
                    v.wait_ge(down_ok.sem, down_ok.at(k, j - 1))
                    v.tensor_tensor(hid[:, s], sl[:, s], pu[:, s], ALU.mult).then_inc(hb_ok.sem, 1)
                    v.wait_ge(hb_ok.sem, hb_ok.at(k, NJ))
                    v.sem_inc(hid_ok.sem, 1)

            def front(k, p, parts, step):
                def link(ins):
                    step[0] += 1
                    ins.then_inc(dch, 1)
                    v.wait_ge(dch, k * DCH + (link_base + step[0]))

                def todo():
                    v.wait_ge(x_load.sem, x_load.at(k))
                    for q in range(MQ):
                        ins = v.bn_stats(stats[:, q], x_in[:, p, q])
                        if q < MQ - 1:
                            ins.then_inc(dch, 1)
                            step[0] += 1
                    link(ins)
                    v.sem_inc(spare, 1)
                    for q in range(MQ):
                        ins = v.bn_aggr(mv[:, q], stats[:, q])
                        if q < MQ - 1:
                            ins.then_inc(dch, 1)
                            step[0] += 1
                    link(ins)
                    v.sem_inc(moments.sem, 1)
                    yield
                    v.wait_ge(rstd_ok.sem, rstd_ok.at(k))
                    for q in range(MQ):
                        v.tensor_scalar(xn[:, q], x_in[:, p, q], mv[:, q, 0:1], rstd[:, 0, q:q + 1],
                                        ALU.subtract, ALU.mult).then_inc(dch, 1)
                        step[0] += 1
                        ins = v.tensor_scalar(xr[:, q], x_in[:, p, q], mv[:, q, 0:1], rstd[:, 1, q:q + 1],
                                              ALU.subtract, ALU.mult)
                        if q < MQ - 1:
                            ins.then_inc(dch, 1)
                            step[0] += 1
                    link(ins)
                    v.sem_inc(xn_ok.sem, 1)
                    v.sem_inc(x_used.sem, 1)
                    yield
                    v.wait_ge(th_ok.sem, th_ok.at(k))
                    link(v.tensor_scalar(r["sig"][:], th[:], 0.5, 0.5, ALU.mult, ALU.add))
                    link(v.tensor_tensor(r["sc"][:], r["sig"][:],
                                         e_bias[:].unsqueeze(1).broadcast_to([P, MQ, E_ALL]), ALU.add))
                    sc4 = r["sc"][:].rearrange("p q (g e) -> p (q g) e", e=4)
                    at = 0
                    for s in (1, 2, 3):
                        ins = v.tensor_tensor(pairs[:, :, at:at + 4 - s], sc4[:, :, 0:4 - s], sc4[:, :, s:4], ALU.add)
                        at += 4 - s
                        if s < 3:
                            ins.then_inc(dch, 1)
                            step[0] += 1
                    link(ins)
                    link(v.tensor_reduce(gs[:].rearrange("p q g -> p (q g)"), pairs[:], AX.X, ALU.max))
                    yield
                    wn = wins[:]
                    link(v.tensor_copy(wn, ahead[:].rearrange("p (q g) -> p q g", g=GROUPS)))
                    for s in (1, 2, 3):
                        n = GROUPS - s
                        link(v.tensor_tensor(cmp[:, :, 0:n], gs[:, :, 0:n], gs[:, :, s:GROUPS], ALU.is_ge))
                        link(v.tensor_tensor(wn[:, :, 0:n], wn[:, :, 0:n], cmp[:, :, 0:n], ALU.add))
                        link(v.tensor_tensor(wn[:, :, s:GROUPS], wn[:, :, s:GROUPS], cmp[:, :, 0:n], ALU.subtract))
                    link(v.tensor_scalar(wn, wn, float(GROUPS - TOPG) - 0.5, None, ALU.is_gt))
                    yield
                    link(v.tensor_tensor(r["msk"][:].rearrange("p q (g e) -> p (q g) e", e=4), sc4,
                                         wins[:].rearrange("p q g -> p (q g)").unsqueeze(2).broadcast_to(
                                             [P, MQ * GROUPS, 4]), ALU.mult))
                    v.sem_inc(spare, 1)
                    for q in range(MQ):
                        ins = v.max(top8[:, q], r["msk"][:, q])
                        if q < MQ - 1:
                            ins.then_inc(dch, 1)
                            step[0] += 1
                    link(ins)
                    fourth = top8[:, :, TOPK - 1:TOPK].broadcast_to([P, MQ, E_ALL])
                    link(v.tensor_tensor(r["gt"][:], r["msk"][:], fourth, ALU.is_gt))
                    link(v.tensor_tensor(r["eq"][:], r["msk"][:], fourth, ALU.is_equal))
                    link(v.tensor_reduce(room[:], r["gt"][:], AX.X, ALU.add))
                    link(v.tensor_scalar(room[:], room[:], -1.0, float(TOPK), ALU.mult, ALU.add))
                    link(v.tensor_tensor_scan(r["cum"][:].rearrange("p q e -> p (q e)"), restart[:],
                                              r["eq"][:].rearrange("p q e -> p (q e)"), 0.0, ALU.mult, ALU.add))
                    yield
                    link(v.tensor_tensor(r["cum"][:], r["cum"][:],
                                         room[:].unsqueeze(2).broadcast_to([P, MQ, E_ALL]), ALU.is_le))
                    link(v.tensor_tensor(r["sel"][:], r["cum"][:], r["eq"][:], ALU.mult))
                    link(v.tensor_tensor(r["sel"][:], r["sel"][:], r["gt"][:], ALU.add))
                    link(v.tensor_tensor(r["tw"][:], r["sel"][:], r["sig"][:], ALU.mult))
                    link(v.tensor_reduce(den[:], r["tw"][:], AX.X, ALU.add))
                    link(v.tensor_scalar(den[:], den[:], 1e-20, None, ALU.add))
                    link(v.reciprocal(den[:], den[:]))
                    link(v.scalar_tensor_tensor(r["c"][:], r["tw"][:], MOE_SCALE,
                                                den[:].unsqueeze(2).broadcast_to([P, MQ, E_ALL]), ALU.mult, ALU.mult))
                    yield
                    v.wait_ge(cT_ok.sem, cT_ok.at(k, 0))
                    link(v.tensor_copy(hi[:], r["c"][:]))
                    link(v.tensor_copy(c3[:, :, 0:16], hi[:]))
                    link(v.tensor_tensor(r["r1"][:], r["c"][:], c3[:, :, 0:16], ALU.subtract))
                    link(v.tensor_copy(hi[:], r["r1"][:]))
                    link(v.tensor_copy(c3[:, :, 32:48], hi[:]))
                    link(v.tensor_tensor(c3[:, :, 64:80], r["r1"][:], c3[:, :, 32:48], ALU.subtract))
                    v.sem_inc(c3_ok.sem, 1)
                    yield

                gen = todo()
                return gen

            def body(k, p, kk):
                has_front = kk is None or kk + 1 < MCH
                step = [0]
                gen = front(k + 1, 1 - p, None, step) if has_front else None
                if kk is not None and kk < 0:
                    for _ in gen:
                        pass
                    assert step[0] == DCH, step[0]
                    return
                for j in range(NJ):
                    main(k, p, j)
                    if has_front and j in (0, 1, 5, 6, 7, 8):
                        next(gen)
                if has_front:
                    for _ in gen:
                        pass
                    assert step[0] == DCH, step[0]

            in_pairs(v, MCH, -1, body)


def scan_phase(nc, io, scratch):
    R_DT, C_DT = (0.1 - 0.001) / 2, (0.1 + 0.001) / 2
    A_DT = 0.5 / (R_DT + 1e-8)
    NQ = ST // 64
    with ExitStack() as ctx:
        def sb(name, shape, dt=F32):
            return ctx.enter_context(nc.sbuf_tensor("s_" + name, shape, dt))

        def ps(name, shape, dt=F32):
            return ctx.enter_context(nc.psum_tensor("s_" + name, shape, dt))

        def cnt(name, per, credit=0, by=1):
            return Count(ctx, nc, "s_" + name, per, credit, by)

        def sem(name):
            return ctx.enter_context(nc.semaphore("s_" + name))

        h = sb("h", [P, 2, 2 * NS, ST])
        dA = sb("dA", [P, 2, 2 * NS, ST])
        conv_w = sb("conv_w", [P, 4, DI])
        gate_w = sb("gate_w", [P, DI])
        dt_w = sb("dt_w", [P, 2, DI])
        bc_w = sb("bc_w", [P, 2, 2 * NS])
        out_w = sb("out_w", [P, 2, D])
        pick = sb("pick", [96, NS], BF16)
        ident = sb("ident", [P, P])
        ident_b = sb("ident_b", [64, 64], BF16)
        ones = sb("ones", [P, P])
        cols = sb("cols", [P, 8])
        col2 = sb("col2", [P, 4])
        a16 = sb("a16", [P, 2 * NS])
        cst = sb("cst", [B, 2])
        xr = sb("xr", [P, HALO + ST])
        xg = sb("xg", [P, 4, ST])
        zg = sb("zg", [P, 4, ST])
        th = sb("th", [P, 2, ST])
        z = sb("z", [P, 2, ST])
        tg = sb("tg", [P, 2, ST])
        dt = sb("dt", [P, 2, 2, ST])
        dtx = sb("dtx", [P, 2, 2, ST])
        s3 = sb("s3", [64, NQ, 2, 96], BF16)
        rest = sb("rest", [64, NQ, 2, NS])
        bcT = sb("bcT", [96, 2, 2, ST], BF16)
        cT = sb("cT", [96, 2, ST], BF16)
        prod = sb("prod", [P, 2, 2, ST])
        xn = sb("xn", [P, ST])
        g = sb("g", [P, ST])
        tok = sb("tok", [P, 3, D])
        nrm = sb("nrm", [P, B])
        n2 = sb("n2", [B, 4])
        fac = sb("fac", [P, B])

        F = ps("F", [P, 2, 512])
        X = ps("X", [P, 3, 512])
        Y = ps("Y", [P, 2, 512])
        E = ps("E", [P, 512])
        Fb = F[:, 1, :].bitcast(BF16)

        w_load, consts, aset, vset, setup = (sem(n) for n in ("w_load", "consts", "aset", "vset", "setup"))
        xr_ld = cnt("xr_ld", 1, by=16)
        f_conv = cnt("f_conv", 2)
        a_conv = cnt("a_conv", 1)
        xc_ok = cnt("xc_ok", 1)
        f_gate = cnt("f_gate", 1)
        a_gate = cnt("a_gate", 1)
        gs_ok = cnt("gs_ok", 1, 1)
        f_dt = cnt("f_dt", 1)
        a_ln = cnt("a_ln", 1)
        v_ok = cnt("v_ok", 1)
        sp_ok = cnt("sp_ok", 1)
        a_dt = cnt("a_dt", 1)
        dt_ok = cnt("dt_ok", 1)
        f_bc = cnt("f_bc", 1)
        s3_ok = cnt("s3_ok", 1)
        f_t = cnt("f_t", 1, 1)
        bcT_ok = cnt("bcT_ok", 1)
        xg_st = cnt("xg_st", 1, 16, by=16)
        zg_ld = cnt("zg_ld", 1, by=16)
        xn_ld = cnt("xn_ld", 2, by=16)
        c_st = cnt("c_st", 1, 16, by=16)
        cT_ld = cnt("cT_ld", 1, by=16)
        b_ok = cnt("b_ok", NS)
        b_rd = cnt("b_rd", NS)
        c_ok = cnt("c_ok", NS)
        dA_ok = cnt("dA_ok", 4)
        a_th = cnt("a_th", 2 * NS)
        st0_ok = cnt("st0_ok", 1)
        fac_ok = cnt("fac_ok", 1)
        VST = 3 + 2 * (STEPS - 1)
        vst = cnt("vst", VST)
        sq_ok = cnt("sq_ok", 1)
        nr_ok = cnt("nr_ok", 1)
        n2_ps = cnt("n2_ps", 1)
        n2_ok = cnt("n2_ok", 1)
        n_fac = cnt("n_fac", 1)
        fac_ps = cnt("fac_ps", 1)
        PCH = 7 + 2 * (STEPS - 1)
        pch = cnt("pch", PCH)
        h_ok = cnt("h_ok", 1)
        prod_ok = cnt("prod_ok", NS)
        prod_rd = cnt("prod_rd", NS, 1)
        yy_ok = cnt("yy_ok", 1)
        o_ok = cnt("o_ok", 1, 1)
        sg_ok = cnt("sg_ok", 1)
        o_tp = cnt("o_tp", 1, 1)
        tok_ok = cnt("tok_ok", 1)
        tok_st = cnt("tok_st", 3, 48, by=16)
        vch = cnt("vch", 8)
        a_exp = cnt("a_exp", 2)
        NW = 15

        spare = sem("spare")

        stage = dA[:, 1].rearrange("p a b -> p (a b)")
        w_in, taps, a_log = stage[:, 0:2 * DI], stage[:, 512:1536], stage[:, 1536:1568]

        N_GATE, N_NORM, N_FAC, N_ROWS, N_CONV, N_DT, N_BC, N_TURN = 0, 0, 2, 4, 4, 8, 10, 12
        V_HOLD, V_GATE, V_XC, V_SP, V_SPLIT, V_DT = 3, 2, 6, 10, 11, 12

        def has_inner(kk):
            return kk is None or kk + 3 < NC

        def has_drive(kk):
            return kk is None or 0 <= kk + 2 < NC

        def has_steps(kk):
            return kk is None or 0 <= kk + 1 < NC

        def has_output(kk):
            return kk is None or 0 <= kk < NC

        def has_finish(kk):
            return kk is None or kk >= 1

        def turns(eng, body):
            in_pairs(eng, NC + 1, -3, body, loop_from=2, tail=4)

        block = ctx.enter_context(nc.Block())

        @block.sync
        def _(sp):
            loads = [(w_in, "w_in"), (taps, "taps"), (a_log, "a_log"), (dt_w[:], "dt_w"), (bc_w[:], "bc_w"),
                     (out_w[:], "out_w"), (pick[:], "pick"), (ident[:], "ident"), (ident_b[:], "ident_b"),
                     (cols[:, 0:2], "conv_b"), (cols[:, 2:4], "b_dt"), (cols[:, 4:6], "d_param"),
                     (cols[:, 6:7], "residual"), (cols[:, 7:8], "norm_w"), (ones[:], "ones")]
            assert len(loads) == NW
            for dst, src in loads:
                sp.dma_start(dst, io[src]).then_inc(w_load, 16)
            xg_st.give(sp)
            c_st.give(sp)
            tok_st.give(sp)

            def wait(c, value):
                sp.wait_ge(c.sem, value)
                sp.sem_inc(spare, 1)

            def load_x(kn):
                sp.dma_start(xr[:], scratch["xrT"][:, bass.ds(kn * ST, HALO + ST)]).then_inc(xr_ld.sem, 16)

            def body(k, p, kk):
                k1, k3 = k + 1, k + 3
                stored = k + 2 if kk is None else min(kk + 2, NC - 1)
                if kk == -3:
                    load_x(0)
                if has_steps(kk):
                    wait(c_st, c_st.at(stored))
                    if has_output(kk):
                        wait(c_ok, c_ok.at(k))
                    sp.dma_start(cT[:, 1 - p], scratch["cT"][bass.ds(k1 * 96, 96), :]).then_inc(cT_ld.sem, 16)
                if has_output(kk):
                    wait(xg_st, xg_st.at(stored))
                    wait(o_ok, o_ok.at(k, 0))
                    sp.dma_start(zg[:].rearrange("p a b -> p (a b)"),
                                 scratch["xg"][bass.ds(k * P, P), :]).then_inc(zg_ld.sem, 16)
                    wait(o_tp, o_tp.at(k, 0))
                    sp.dma_start(xn[:], scratch["xnT"][:, bass.ds(k * ST, ST)]).then_inc(xn_ld.sem, 16)
                    sp.dma_start(g[:], scratch["gT"][:, bass.ds(k * ST, ST)]).then_inc(xn_ld.sem, 16)
                if has_finish(kk):
                    wait(tok_ok, tok_ok.at(k - 1))
                    for q in range(3):
                        n = min(P, ST - q * P)
                        sp.dma_start(scratch["sg"][bass.ds((k - 1) * ST + q * P, n), :],
                                     tok[0:n, q]).then_inc(tok_st.sem, 16)
                if has_inner(kk):
                    if kk is None or kk + 4 < NC:
                        wait(f_conv, f_conv.at(k3, 2))
                        load_x(k + 4)
                    wait(xc_ok, xc_ok.at(k3))
                    sp.dma_start(scratch["xg"][bass.ds(k3 * P, P), :],
                                 xg[:].rearrange("p a b -> p (a b)")).then_inc(xg_st.sem, 16)
                    wait(bcT_ok, bcT_ok.at(k3))
                    sp.dma_start(scratch["cT"][bass.ds(k3 * 96, 96), :],
                                 bcT[:, 1 - p, 1]).then_inc(c_st.sem, 16)

            turns(sp, body)
            wait(tok_st, tok_st.at(NC - 1, 3))

        @block.gpsimd
        def _(pool):
            pool.memset(cst[:, 0:1], 0.5).then_inc(consts, 1)
            pool.memset(cst[:, 1:2], -1.0).then_inc(consts, 1)
            pool.wait_ge(consts, 5)

            def body(k, p, kk):
                if not has_steps(kk):
                    return
                k1, q = k + 1, 1 - p
                step = [0]

                def link(ins):
                    step[0] += 1
                    ins.then_inc(pch.sem, 1)
                    pool.wait_ge(pch.sem, pch.at(k1, step[0]))
                    if step[0] in (3, 5):
                        pool.sem_inc(spare, 1)

                def at(buf, par, s):
                    return buf[:, par, 0:JP, s * B:(s + 1) * B]

                pool.wait_ge(dA_ok.sem, dA_ok.at(k1, 4))
                pool.wait_ge(b_rd.sem, b_rd.at(k1, NS))
                link(pool.tensor_tensor(at(dA, q, 0), at(dA, q, 0), at(h, 1 - q, STEPS - 1), ALU.mult))
                link(pool.tensor_tensor(at(h, q, 0), at(h, q, 0), at(dA, q, 0), ALU.add))
                pool.sem_inc(st0_ok.sem, 1)
                pool.wait_ge(n2_ok.sem, n2_ok.at(k1))
                link(pool.tensor_tensor(n2[:, 1:2], n2[:, 0:1], cst[:, 0:1], ALU.pow))
                link(pool.tensor_scalar(n2[:, 2:3], n2[:, 1:2], 1e-8, None, ALU.add))
                link(pool.tensor_tensor(n2[:, 1:2], n2[:, 2:3], cst[:, 1:2], ALU.pow))
                link(pool.tensor_scalar(n2[:, 3:4], n2[:, 1:2], 20.0, 1.0, ALU.mult, ALU.min))
                pool.sem_inc(n_fac.sem, 1)
                pool.wait_ge(fac_ok.sem, fac_ok.at(k1))
                link(pool.tensor_tensor(at(h, q, 0), at(h, q, 0), fac[:].unsqueeze(1).broadcast_to([P, JP, B]),
                                        ALU.mult))
                for s in range(1, STEPS):
                    link(pool.tensor_tensor(at(dA, q, s), at(dA, q, s), at(h, q, s - 1), ALU.mult))
                    link(pool.tensor_tensor(at(h, q, s), at(h, q, s), at(dA, q, s), ALU.add))
                pool.sem_inc(h_ok.sem, 1)
                assert step[0] == PCH, step[0]

            turns(pool, body)

        @block.tensor
        def _(pe):
            f_t.give(pe)
            prod_rd.give(pe)
            o_ok.give(pe)
            o_tp.give(pe)
            pe.wait_ge(w_load, 16 * NW)
            pe.wait_ge(consts, 5)
            pe.wait_ge(setup, 5)

            def spread(bank, rows, n):
                return pe.matmul(X[:, bank, 0:ST], pick[:, n:n + 1].broadcast_to([96, P]), rows,
                                 start=True, stop=True)

            def spread_c(k, p, n, after):
                if n == 0:
                    pe.wait_ge(cT_ld.sem, cT_ld.at(k))
                if n >= 2:
                    pe.wait_ge(prod_ok.sem, prod_ok.at(k, n - 1))
                elif after:
                    pe.wait_ge(prod_ok.sem, prod_ok.at(k - 1, NS + n - 1))
                spread(n % 2, cT[:, p], n).then_inc(c_ok.sem, 1)

            def spread_b(k, p, n, after):
                if n == 0:
                    pe.wait_ge(bcT_ok.sem, bcT_ok.at(k))
                    if after:
                        pe.wait_ge(b_rd.sem, b_rd.at(k - 1, NS))
                else:
                    pe.wait_ge(b_rd.sem, b_rd.at(k, n))
                spread(2, bcT[:, p, 0], n).then_inc(b_ok.sem, 1)

            def body(k, p, kk):
                k1, k2, k3 = k + 1, k + 2, k + 3

                def gate():
                    pe.wait_ge(xr_ld.sem, xr_ld.at(k3))
                    if kk is None or kk > -3:
                        pe.wait_ge(bcT_ok.sem, bcT_ok.at(k2))
                    for c in range(2):
                        mm = pe.matmul(F[:, c, 0:ST], gate_w[:, c * P:(c + 1) * P], xr[:, HALO:HALO + ST],
                                       start=True, stop=True)
                    mm.then_inc(f_gate.sem, 1)

                def conv(c):
                    if c == 0:
                        pe.wait_ge(gs_ok.sem, gs_ok.at(k3))
                    for t in range(4):
                        mm = pe.matmul(F[:, c, 0:ST], conv_w[:, t, c * P:(c + 1) * P],
                                       xr[:, t * B:t * B + ST], start=(t == 0), stop=(t == 3))
                    mm.then_inc(f_conv.sem, 1)

                def step_width():
                    pe.wait_ge(xc_ok.sem, xc_ok.at(k3))
                    for c in range(2):
                        for i in range(2):
                            mm = pe.matmul(F[:, c, 0:ST], dt_w[:, i, c * P:(c + 1) * P], xg[:, i],
                                           start=(i == 0), stop=(i == 1))
                    mm.then_inc(f_dt.sem, 1)

                def b_c():
                    pe.wait_ge(v_ok.sem, v_ok.at(k3))
                    for q in range(NQ):
                        for i in range(2):
                            mm = pe.matmul(F[0:64, 0, q * 32:(q + 1) * 32], xg[:, i, q * 64:(q + 1) * 64],
                                           bc_w[:, i], start=(i == 0), stop=(i == 1))
                    mm.then_inc(f_bc.sem, 1)

                def turn_b_c():
                    pe.wait_ge(s3_ok.sem, s3_ok.at(k3))
                    pe.sem_inc(spare, 1)
                    for q in range(NQ):
                        for bc in range(2):
                            mm = pe.transpose(Fb[0:96, bc * ST + q * 64:bc * ST + (q + 1) * 64], s3[:, q, bc],
                                              ident_b[:])
                    mm.then_inc(f_t.sem, 1)

                def norms():
                    pe.wait_ge(nr_ok.sem, nr_ok.at(k1))
                    pe.matmul(E[0:B, 0:1], nrm[:], ones[:, 0:1], start=True, stop=True).then_inc(n2_ps.sem, 1)

                def factors():
                    pe.wait_ge(n_fac.sem, n_fac.at(k1))
                    pe.matmul(E[:, 0:B], n2[:, 3:4].broadcast_to([B, P]), ident[0:B, 0:B], start=True,
                              stop=True).then_inc(fac_ps.sem, 1)

                def token_rows():
                    pe.wait_ge(sg_ok.sem, sg_ok.at(k - 1))
                    if has_steps(kk):
                        pe.wait_ge(fac_ok.sem, fac_ok.at(k1))
                    for q in range(3):
                        n = min(P, ST - q * P)
                        mm = pe.transpose(E[0:n, q * P:(q + 1) * P], xn[:, q * P:q * P + n], ident[:])
                    mm.then_inc(o_tp.sem, 1)

                for n in range(NS):
                    if has_output(kk):
                        if n < NS - 1:
                            spread_c(k, p, n + 1, kk is None or kk >= 1)
                        pe.wait_ge(prod_ok.sem, prod_ok.at(k, n + 1))
                        for c in range(2):
                            mm = pe.matmul(Y[:, c, 0:ST], ident[:], prod[:, n % 2, c], start=(n == 0),
                                           stop=(n == NS - 1))
                        mm.then_inc(prod_rd.sem, 1)
                    if has_drive(kk) and n > 0:
                        spread_b(k2, p, n, False)
                    if has_steps(kk) and n == N_NORM:
                        norms()
                    if has_steps(kk) and n == N_FAC:
                        factors()
                    if has_finish(kk) and n == N_ROWS:
                        token_rows()
                    if has_inner(kk):
                        if n == N_GATE:
                            gate()
                        if n in (N_CONV, N_CONV + 1):
                            conv(n - N_CONV)
                        if n == N_DT:
                            step_width()
                        if n == N_BC:
                            b_c()
                        if n == N_TURN:
                            turn_b_c()
                if kk is None or 0 <= kk + 1 < NC:
                    spread_c(k1, 1 - p, 0, kk is None or kk >= 0)
                if kk is None or 0 <= kk + 3 < NC:
                    spread_b(k3, 1 - p, 0, kk is None or kk > -3)
                if has_output(kk):
                    if kk is None or kk >= 1:
                        pe.wait_ge(tok_ok.sem, tok_ok.at(k - 1))
                    pe.wait_ge(yy_ok.sem, yy_ok.at(k))
                    for i in range(2):
                        mm = pe.matmul(E[:, 0:ST], out_w[:, i], zg[:, i], start=(i == 0), stop=(i == 1))
                    mm.then_inc(o_ok.sem, 1)

            turns(pe, body)

        @block.scalar
        def _(act):
            act.wait_ge(w_load, 16 * NW)
            act.activation(a16[:], a_log, ACT.Tanh, scale=0.5 / (5.0 + 1e-8)).then_inc(aset, 1)
            act.activation(col2[:, 3:4], cols[:, 6:7], ACT.Tanh, scale=0.5).then_inc(aset, 1)
            act.wait_ge(aset, 2)
            act.activation(a16[:], a16[:], ACT.Exp, scale=10.0).then_inc(aset, 1)
            act.wait_ge(setup, 5)
            act.wait_ge(consts, 5)

            def body(k, p, kk):
                k1, k2, k3 = k + 1, k + 2, k + 3

                def decay_tanh(first, n):
                    if not has_drive(kk):
                        return
                    if first == 0:
                        act.wait_ge(dt_ok.sem, dt_ok.at(k2))
                        if has_output(kk):
                            act.wait_ge(h_ok.sem, h_ok.at(k))
                            act.wait_ge(vst.sem, vst.at(k, VST))
                    for j in range(first, first + n):
                        act.activation(dA[:, p, j], dt[:, p, j // NS], ACT.Tanh,
                                       scale=a16[:, j:j + 1]).then_inc(a_th.sem, 1)

                def decay_exp(i):
                    if not has_drive(kk):
                        return
                    act.wait_ge(a_th.sem, a_th.at(k2, 8 * i + 8))
                    act.activation(dA[:, p, 8 * i:8 * i + 8], dA[:, p, 8 * i:8 * i + 8], ACT.Exp,
                                   scale=16.0).then_inc(dA_ok.sem, 1)

                if has_steps(kk):
                    act.wait_ge(st0_ok.sem, st0_ok.at(k1))
                    act.wait_ge(vst.sem, vst.at(k1, 2))
                    act.activation(dA[:, 1 - p, :, 0:B], h[:, 1 - p, :, 0:B], ACT.Square).then_inc(sq_ok.sem, 1)
                decay_tanh(0, 4)
                if has_steps(kk):
                    act.wait_ge(n2_ps.sem, n2_ps.at(k1))
                    act.activation(n2[:, 0:1], E[0:B, 0:1], ACT.Copy).then_inc(n2_ok.sem, 1)
                if has_inner(kk):
                    act.wait_ge(f_gate.sem, f_gate.at(k3))
                    act.wait_ge(gs_ok.sem, gs_ok.at(k3, 0))
                    act.activation(tg[:], F[:, :, 0:ST], ACT.Tanh, scale=0.5).then_inc(a_gate.sem, 1)
                decay_tanh(4, 2)
                if has_steps(kk):
                    act.wait_ge(fac_ps.sem, fac_ps.at(k1))
                    act.activation(fac[:], E[:, 0:B], ACT.Copy).then_inc(fac_ok.sem, 1)
                decay_tanh(6, 6)
                if has_finish(kk):
                    act.wait_ge(o_tp.sem, o_tp.at(k - 1))
                    act.wait_ge(tok_st.sem, tok_st.at(k - 1, 0))
                    act.activation(tok[:, 0:2], E[:, 0:2 * D], ACT.Copy)
                    act.activation(tok[0:64, 2], E[0:64, 2 * D:3 * D], ACT.Copy).then_inc(tok_ok.sem, 1)
                decay_tanh(12, 4)
                decay_exp(0)
                if has_inner(kk):
                    act.wait_ge(f_conv.sem, f_conv.at(k3, 2))
                    if kk is None or kk > -3:
                        act.wait_ge(dt_ok.sem, dt_ok.at(k2))
                    for c in range(2):
                        act.activation(th[:, c], F[:, c, 0:ST], ACT.Tanh, bias=col2[:, c:c + 1], scale=0.5)
                    act.activation(z[:, 0], F[:, 0, 0:ST], ACT.Identity, bias=col2[:, 0:1], scale=0.5)
                    act.activation(z[:, 1], F[:, 1, 0:ST], ACT.Identity, bias=col2[:, 1:2],
                                   scale=0.5).then_inc(a_conv.sem, 1)
                decay_tanh(16, 8)
                decay_exp(1)
                if has_inner(kk):
                    act.wait_ge(f_dt.sem, f_dt.at(k3))
                    act.activation(z[:, 0], F[:, 0, 0:ST], ACT.Identity, bias=cols[:, 2:3])
                    act.activation(z[:, 1], F[:, 1, 0:ST], ACT.Identity, bias=cols[:, 3:4]).then_inc(v_ok.sem, 1)
                    act.wait_ge(v_ok.sem, v_ok.at(k3))
                    act.activation(th[:], z[:], ACT.Abs).then_inc(a_exp.sem, 1)
                    act.wait_ge(a_exp.sem, a_exp.at(k3, 1))
                    act.activation(th[:], th[:], ACT.Exp, scale=-1.0).then_inc(a_exp.sem, 1)
                    act.wait_ge(a_exp.sem, a_exp.at(k3, 2))
                    act.activation(th[:], th[:], ACT.Ln, bias=1.0).then_inc(a_ln.sem, 1)
                decay_tanh(24, 8)
                if has_inner(kk):
                    act.wait_ge(sp_ok.sem, sp_ok.at(k3))
                    act.activation(th[:], z[:], ACT.Tanh, bias=col2[:, 2:3], scale=A_DT).then_inc(a_dt.sem, 1)
                decay_exp(2)
                if has_inner(kk):
                    act.wait_ge(f_t.sem, f_t.at(k3))
                    if kk is None or kk + 1 >= 0:
                        act.wait_ge(b_ok.sem, b_ok.at(k1, NS))
                        act.wait_ge(c_st.sem, c_st.at(k2))
                    act.activation(bcT[:, 1 - p].rearrange("p a b -> p (a b)"), Fb[0:96, 0:2 * ST],
                                   ACT.Copy).then_inc(bcT_ok.sem, 1)
                decay_exp(3)

            turns(act, body)

        @block.vector
        def _(v):
            gs_ok.give(v)
            v.memset(s3[:], 0.0).then_inc(consts, 1)
            v.memset(h[:, 1, :, (STEPS - 1) * B:], 0.0).then_inc(consts, 1)
            v.memset(col2[:, 2:3], -C_DT * A_DT).then_inc(consts, 1)
            v.wait_ge(w_load, 16 * NW)
            v.tensor_scalar(col2[:, 0:2], cols[:, 0:2], 0.5, None, ALU.mult).then_inc(setup, 1)
            v.tensor_scalar(w_in, w_in, cols[:, 7:8], None, ALU.mult).then_inc(vset, 1)
            v.wait_ge(vset, 1)
            v.tensor_tensor(conv_w[:], taps.rearrange("p (t c) -> p t c", t=4),
                            w_in[:, 0:DI].unsqueeze(1).broadcast_to([P, 4, DI]), ALU.mult).then_inc(setup, 1)
            v.tensor_copy(gate_w[:], w_in[:, DI:2 * DI]).then_inc(setup, 1)
            v.wait_ge(aset, 3)
            v.tensor_scalar(a16[:], a16[:], -1.0 / 16, None, ALU.mult).then_inc(setup, 1)
            v.tensor_scalar(col2[:, 3:4], col2[:, 3:4], 0.125, 0.125, ALU.mult, ALU.add).then_inc(setup, 1)
            v.wait_ge(setup, 5)
            v.wait_ge(consts, 5)

            def body(k, p, kk):
                k1, k2, k3, q = k + 1, k + 2, k + 3, 1 - p
                step = [0]

                def link(ins):
                    step[0] += 1
                    ins.then_inc(vch.sem, 1)
                    v.wait_ge(vch.sem, vch.at(k3, step[0]))

                def advance(s, half):
                    a, now = dA[:, q, JP:, s * B:(s + 1) * B], h[:, q, JP:, s * B:(s + 1) * B]
                    n = 2 * s + (s > 0) + half
                    if n or kk is None or kk >= 0:
                        v.wait_ge(vst.sem, vst.at(k1, n))
                    if half:
                        ins = v.tensor_tensor(now, now, a, ALU.add)
                    else:
                        before = h[:, q, JP:, (s - 1) * B:s * B] if s else h[:, p, JP:, (STEPS - 1) * B:]
                        ins = v.tensor_tensor(a, a, before, ALU.mult)
                    ins.then_inc(vst.sem, 1)

                halves = iter([(s, half) for s in range(1, STEPS) for half in range(2)])

                def next_halves(n):
                    for _ in range(n if has_steps(kk) else 0):
                        s = next(halves, None)
                        if s:
                            advance(*s)

                def product(n):
                    if not has_output(kk):
                        return
                    v.wait_ge(c_ok.sem, c_ok.at(k, n + 1))
                    if n == 0:
                        v.wait_ge(h_ok.sem, h_ok.at(k))
                        v.wait_ge(vst.sem, vst.at(k, VST))
                    v.wait_ge(prod_rd.sem, prod_rd.at(k, n - 1))
                    v.tensor_tensor(prod[:, n % 2], h[:, p].rearrange("p (c n) t -> p c n t", c=2)[:, :, n],
                                    X[:, n % 2, 0:ST].unsqueeze(1).broadcast_to([P, 2, ST]),
                                    ALU.mult).then_inc(prod_ok.sem, 1)

                def drive(n):
                    if not has_drive(kk):
                        return
                    if n == 0:
                        v.wait_ge(dt_ok.sem, dt_ok.at(k2))
                    v.wait_ge(b_ok.sem, b_ok.at(k2, n + 1))
                    if n == 0 and has_steps(kk):
                        v.wait_ge(st0_ok.sem, st0_ok.at(k1))
                    if has_output(kk):
                        v.wait_ge(prod_ok.sem, prod_ok.at(k, n + 1))
                    v.tensor_tensor(h[:, p].rearrange("p (c n) t -> p c n t", c=2)[:, :, n], dtx[:, p],
                                    X[:, 2, 0:ST].unsqueeze(1).broadcast_to([P, 2, ST]),
                                    ALU.mult).then_inc(b_rd.sem, 1)

                if has_steps(kk):
                    v.wait_ge(dA_ok.sem, dA_ok.at(k1, 4))
                    advance(0, 0)
                    advance(0, 1)
                product(0)
                for n in range(NS):
                    if n == 0 and has_finish(kk):
                        v.wait_ge(o_ok.sem, o_ok.at(k - 1))
                        v.wait_ge(xn_ld.sem, xn_ld.at(k - 1, 2))
                        link(v.scalar_tensor_tensor(xn[:], E[:, 0:ST], col2[:, 3:4], xn[:], ALU.mult, ALU.add))
                        v.tensor_tensor(xn[:], xn[:], g[:], ALU.mult).then_inc(sg_ok.sem, 1)
                    if n < NS - 1:
                        product(n + 1)
                    if has_steps(kk) and n == 0:
                        v.wait_ge(sq_ok.sem, sq_ok.at(k1))
                        v.tensor_reduce(nrm[:], dA[:, q, :, 0:B].rearrange("p j b -> p b j"), AX.X,
                                        ALU.add).then_inc(nr_ok.sem, 1)
                    drive(n)
                    if has_steps(kk) and n == V_HOLD:
                        v.wait_ge(fac_ok.sem, fac_ok.at(k1))
                        v.tensor_tensor(h[:, q, JP:, 0:B], h[:, q, JP:, 0:B], fac[:].unsqueeze(1).broadcast_to(
                            [P, 2 * NS - JP, B]), ALU.mult).then_inc(vst.sem, 1)
                    if n > V_HOLD:
                        next_halves(1 + (n % 2 or n > NS - 4))
                    if has_inner(kk):
                        if n == V_GATE:
                            v.wait_ge(a_gate.sem, a_gate.at(k3))
                            v.wait_ge(xg_st.sem, xg_st.at(k3, 0))
                            v.scalar_tensor_tensor(xg[:, 2:4], tg[:], 1.0, F[:, :, 0:ST], ALU.add,
                                                   ALU.mult).then_inc(gs_ok.sem, 1)
                        if n == V_XC:
                            v.wait_ge(a_conv.sem, a_conv.at(k3))
                            v.scalar_tensor_tensor(xg[:, 0:2], th[:], 1.0, z[:], ALU.add,
                                                   ALU.mult).then_inc(xc_ok.sem, 1)
                        if n == V_SP:
                            v.wait_ge(a_ln.sem, a_ln.at(k3))
                            v.scalar_tensor_tensor(z[:], z[:], 0.0, th[:], ALU.max, ALU.add).then_inc(sp_ok.sem, 1)
                        if n == V_DT:
                            v.wait_ge(a_dt.sem, a_dt.at(k3))
                            link(v.tensor_scalar(dt[:, q], th[:], 2 * R_DT, C_DT, ALU.mult, ALU.add))
                            v.tensor_tensor(dtx[:, q], dt[:, q], xg[:, 0:2], ALU.mult).then_inc(dt_ok.sem, 1)
                        if n == V_SPLIT:
                            src = F[0:64, 0, 0:NQ * 2 * NS].rearrange("p (q c n) -> p q c n", q=NQ, c=2)
                            v.wait_ge(f_bc.sem, f_bc.at(k3))
                            v.wait_ge(f_t.sem, f_t.at(k3, 0))
                            link(v.tensor_copy(s3[:, :, :, 0:NS], src))
                            link(v.tensor_tensor(rest[:], src, s3[:, :, :, 0:NS], ALU.subtract))
                            link(v.tensor_copy(s3[:, :, :, 32:32 + NS], rest[:]))
                            link(v.tensor_tensor(rest[:], rest[:], s3[:, :, :, 32:32 + NS], ALU.subtract))
                            v.tensor_copy(s3[:, :, :, 64:64 + NS], rest[:]).then_inc(s3_ok.sem, 1)
                next_halves(2 * STEPS)
                if has_output(kk):
                    v.wait_ge(zg_ld.sem, zg_ld.at(k))
                    v.wait_ge(prod_rd.sem, prod_rd.at(k, NS))
                    link(v.scalar_tensor_tensor(zg[:, 0], zg[:, 0], cols[:, 4:5], Y[:, 0, 0:ST], ALU.mult, ALU.add))
                    link(v.scalar_tensor_tensor(zg[:, 1], zg[:, 1], cols[:, 5:6], Y[:, 1, 0:ST], ALU.mult, ALU.add))
                    v.tensor_tensor(zg[:, 0:2], zg[:, 0:2], zg[:, 2:4], ALU.mult).then_inc(yy_ok.sem, 1)
                for _ in range(8 - step[0]):
                    v.sem_inc(vch.sem, 1)

            turns(v, body)


def attention_phase(nc, io, scratch, out):
    SC = float(np.float32(1.0) / np.sqrt(np.float32(8.0)))
    CH = 32
    HC = 8
    HT = HC * CH
    G = 4
    with ExitStack() as ctx:
        def sb(name, shape, dt=F32):
            return ctx.enter_context(nc.sbuf_tensor("a_" + name, shape, dt))

        def ps(name, shape, dt=F32):
            return ctx.enter_context(nc.psum_tensor("a_" + name, shape, dt))

        def cnt(name, per, credit=0, by=1):
            return Count(ctx, nc, "a_" + name, per, credit, by)

        def sem(name):
            return ctx.enter_context(nc.semaphore("a_" + name))

        w = sb("w", [P, 8, D])
        wt = sb("wt", [P, D])
        tern = sb("tern", [P, 4])
        ident = sb("ident", [P, P])
        ones = sb("ones", [P, P])
        jmask = sb("jmask", [P, 4])
        vmask = sb("vmask", [P, 4])
        osum = sb("osum", [P, CH])
        bmask = sb("bmask", [P, CH])
        mhalf = sb("mhalf", [P, MQ])
        x_in = sb("x_in", [P, 2, MQ, D])
        sg_in = sb("sg_in", [P, 2, MQ, D])
        x1 = sb("x1", [P, 2, MQ, D])
        xn = sb("xn", [P, MQ, D])
        stats = sb("stats", [P, MQ, 6])
        mv = sb("mv", [P, MQ, 2])
        rstd = sb("rstd", [P, 2, MQ])
        xnT = sb("xnT", [P, 2, MT])
        qm = sb("qm", [P, 2 * HC, 4, CH])
        km = sb("km", [P, 2 * HC, G, CH])
        x4 = sb("x4", [P, 2 * HC, 4, CH])
        vb = sb("vb", [P, 2, HC * G, CH])
        mx = sb("mx", [P, G * HC])
        e = sb("e", [P, 2, HC, G, CH])
        eT = sb("eT", [P, 2, HC, G, CH])
        rden = sb("rden", [P, HT])
        ctxT = sb("ctxT", [P, 2, HT])
        ch = sb("ch", [P, 2, 2, HT])
        means = sb("means", [P, B * HC])
        gT = sb("gT", [P, B * HC])

        S = ps("S", [P, 2, HC, G * CH])
        V = ps("V", [P, HC, D])
        Vq, Vk = (V[:, 4 * i:4 * i + 4].rearrange("p c d -> p (c d)") for i in range(2))
        SL, RT = (S[:, i].rearrange("p (a b) d -> p a (b d)", a=2) for i in range(2))
        C = ps("C", [P, 2, HT])
        TB = ps("TB", [P, MT])

        w_load, power_ok, consts, wsum, wchain, spare = (
            sem(n) for n in ("w_load", "power_ok", "consts", "wsum", "wchain", "spare"))
        x_ld = cnt("x_ld", 3, by=16)
        x_rd = cnt("x_rd", 1, 2)
        x1_ok = cnt("x1_ok", 1)
        x1_st = cnt("x1_st", 1, 32, by=16)
        moments = cnt("moments", 1)
        rstd_ok = cnt("rstd_ok", 1)
        pchain = cnt("pchain", 1)
        xn_ok = cnt("xn_ok", 1)
        tp = cnt("tp", 1, 1)
        xnT_ok = cnt("xnT_ok", 1)
        xnT_st = cnt("xnT_st", 1, 32, by=16)
        x4_ok = cnt("x4_ok", 1)
        q_ps = cnt("q_ps", 1)
        qm_ok = cnt("qm_ok", 1)
        k_ps = cnt("k_ps", 1)
        km_ok = cnt("km_ok", 1)
        v_ps = cnt("v_ps", 2)
        vb_ok = cnt("vb_ok", 2)
        s_ps = cnt("s_ps", 2)
        mx_ok = cnt("mx_ok", 2)
        sub_ok = cnt("sub_ok", 2, 2)
        ex_ok = cnt("ex_ok", 2)
        eT_ok = cnt("eT_ok", 2)
        av_ps = cnt("av_ps", 2, 2)
        rd_ok = cnt("rd_ok", 2)
        ctx_ok = cnt("ctx_ok", 2, 1)
        o_ps = cnt("o_ps", 2)
        ch_ok = cnt("ch_ok", 2, 1)
        sum_ok = sem("sum_ok")
        ch_st = cnt("ch_st", 1, 32, by=16)
        dch = cnt("dch", 1)
        means_ok, g_ok = sem("means_ok"), sem("g_ok")
        f_ld = Alternate(ctx, nc, "a_f_ld", 3)
        f_ps = cnt("f_ps", 1)
        f_sl = cnt("f_sl", 1)
        f_en = cnt("f_en", 1)
        f_pr = cnt("f_pr", 1)
        f_tp = cnt("f_tp", 1, 2)
        f_out = cnt("f_out", 1, 2)
        f_st = Alternate(ctx, nc, "a_f_st", 1, 16)

        loads = [(w[:], "attn_w"), (wt[:], "tern_w"), (ident[:], "ident"), (ones[:], "ones"), (jmask[:], "jmask"),
                 (vmask[:], "vmask"), (osum[:], "osum"), (bmask[:], "bmask")]
        NW = len(loads)
        x_bt = io["x_bt"]
        sg_bt = scratch["sg"].rearrange("(t b) d -> b t d", b=B)

        def has_front(kk):
            return kk is None or kk + 1 < MCH

        def has_main(kk):
            return kk is None or kk >= 0

        block = ctx.enter_context(nc.Block())

        @block.sync
        def _(sp):
            for dst, src in loads:
                sp.dma_start(dst, io[src]).then_inc(w_load, 16)
            for c in (x1_st, xnT_st, ch_st, f_st):
                c.give(sp)

            def wait(c, value):
                sp.wait_ge(c.sem, value)
                sp.sem_inc(spare, 1)

            def body(k, p, kk):
                k1, n = k + 1, 1 - p
                if has_front(kk):
                    wait(x_rd, x_rd.at(k1, -1))
                    sp.dma_start(x_in[:, n], x_bt[bass.ds(k1 * MT, MT), :].rearrange(
                        "(q p) d -> p q d", p=P)).then_inc(x_ld.sem, 16)
                    for b in range(2):
                        sp.dma_start(sg_in[:, n, 2 * b:2 * b + 2], sg_bt[bass.ds(k1 * 2 + b, 1), 0:L, :].rearrange(
                            "o (q p) d -> p (o q) d", p=P)).then_inc(x_ld.sem, 16)
                    wait(x1_ok, x1_ok.at(k1))
                    sp.dma_start(scratch["x1"][:, bass.ds(k1 * MT, MT)],
                                 x1[:, n].rearrange("p q d -> p (q d)")).then_inc(x1_st.sem, 16)
                    wait(xnT_ok, xnT_ok.at(k1))
                    sp.dma_start(scratch["xnT1"][:, bass.ds(k1 * MT, MT)], xnT[:, n]).then_inc(xnT_st.sem, 16)
                if has_main(kk):
                    wait(ch_ok, ch_ok.at(k, 2))
                    sp.dma_start(scratch["ch"][:, bass.ds(k * MT, MT)],
                                 ch[:, p].rearrange("p a b -> p (a b)")).then_inc(ch_st.sem, 16)

            in_pairs(sp, MCH, -1, body)
            for c in (x1_st, xnT_st, ch_st):
                sp.wait_ge(c.sem, c.at(MCH - 1))
            sp.wait_ge(means_ok, 1)

            def load(k, p):
                wait(f_out, f_out.at(k, -1))
                for dst, src in ((x_in[:, p].rearrange("p q d -> p (q d)"), "x1"), (xnT[:, p], "xnT1"),
                                 (ch[:, p].rearrange("p a b -> p (a b)"), "ch")):
                    sp.dma_start(dst, scratch[src][:, bass.ds(k * MT, MT)]).then_inc(f_ld.sems[p], 16)

            def last(k, p, kk):
                if kk is None or kk + 1 < MCH:
                    load(k + 1, 1 - p)
                wait(f_out, f_out.at(k))
                sp.dma_start(out[bass.ds(k * MT, MT), :].rearrange("(q p) d -> p q d", p=P),
                             x1[:, p]).then_inc(f_st.sems[p], 16)

            load(0, 0)
            in_pairs(sp, MCH, 0, last)
            for p in range(2):
                sp.wait_ge(f_st.sems[p], f_st.at(MCH - 2 + p, p))

        @block.gpsimd
        def _(pool):
            pool.memset(mhalf[:], -0.5).then_inc(power_ok, 1)
            pool.memset(km[:], 0.0).then_inc(power_ok, 1)
            pool.wait_ge(power_ok, 2)

            def body(k, p, kk):
                if has_front(kk):
                    k1 = k + 1
                    pool.wait_ge(moments.sem, moments.at(k1))
                    pool.sem_inc(spare, 1)
                    pool.tensor_scalar(rstd[:, 1], mv[:, :, 1], 1e-5, None, ALU.add).then_inc(pchain.sem, 1)
                    pool.wait_ge(pchain.sem, pchain.at(k1))
                    pool.tensor_tensor(rstd[:, 0], rstd[:, 1], mhalf[:], ALU.pow).then_inc(rstd_ok.sem, 1)
                    pool.wait_ge(xnT_ok.sem, xnT_ok.at(k1))
                    pool.sem_inc(spare, 1)
                    if has_main(kk):
                        pool.wait_ge(v_ps.sem, v_ps.at(k, 2))
                        pool.sem_inc(spare, 1)
                    pool.tensor_copy(x4[:], xnT[:, 1 - p].rearrange("p (c q) -> p c q", q=CH).unsqueeze(2).broadcast_to(
                        [P, 2 * HC, 4, CH])).then_inc(x4_ok.sem, 1)

            in_pairs(pool, MCH, -1, body)
            pool.wait_ge(means_ok, 1)
            pool.tensor_copy(x4[:, 0:HC], means[:].rearrange("p (c q) -> p c q", q=CH).unsqueeze(2).broadcast_to(
                [P, HC, 4, CH])).then_inc(x4_ok.sem, 1)

        @block.tensor
        def _(pe):
            tp.give(pe)
            av_ps.give(pe)
            f_tp.give(pe)
            pe.wait_ge(w_load, 16 * NW)

            def values_scores(k, hf, wv):
                if hf:
                    pe.wait_ge(vb_ok.sem, vb_ok.at(k, 1))
                pe.wait_ge(qm_ok.sem, qm_ok.at(k))
                pe.wait_ge(km_ok.sem, km_ok.at(k))
                pe.wait_ge(x4_ok.sem, x4_ok.at(k))
                for c in range(HC):
                    mm = pe.matmul(V[:, c], x4[:, hf * HC + c].rearrange("p j q -> p (j q)"), wv,
                                   start=True, stop=True)
                mm.then_inc(v_ps.sem, 1)
                pe.wait_ge(sub_ok.sem, sub_ok.at(k - 1, hf + 1))
                for c in range(HC):
                    mm = pe.matmul(S[:, hf, c], qm[:, hf * HC + c].rearrange("p j q -> p (j q)"),
                                   km[:, hf * HC + c].rearrange("p g q -> p (g q)"), start=True, stop=True)
                mm.then_inc(s_ps.sem, 1)

            def contexts(k, hf):
                pe.wait_ge(eT_ok.sem, eT_ok.at(k, hf + 1))
                pe.wait_ge(vb_ok.sem, vb_ok.at(k, hf + 1))
                pe.wait_ge(ctx_ok.sem, ctx_ok.at(k, hf))
                for g in range(G):
                    a = slice(32 * g, 32 * g + 32)
                    pe.matmul(C[a, 1].rearrange("p (c q) -> p c q", q=CH), osum[:], eT[:, hf, :, g], start=True, stop=True)
                for c in range(HC):
                    for g in range(G):
                        a = slice(32 * g, 32 * g + 32)
                        mm = pe.matmul(C[a, 0, c * CH:(c + 1) * CH], vb[:, hf, c * G + g], eT[:, hf, c, g],
                                       start=True, stop=True)
                mm.then_inc(av_ps.sem, 1)

            def project(k, hf, wo):
                pe.wait_ge(ctx_ok.sem, ctx_ok.at(k, hf + 1))
                pe.matmul(TB[:, 0:HT], wo, ctxT[:, hf], start=True, stop=True).then_inc(o_ps.sem, 1)

            def body(k, p, kk):
                k1, n = k + 1, 1 - p
                if has_main(kk):
                    values_scores(k, 1, w[:, 2])
                if has_front(kk):
                    pe.wait_ge(xn_ok.sem, xn_ok.at(k1))
                    if has_main(kk):
                        pe.wait_ge(ch_ok.sem, ch_ok.at(k, 0))
                    for q in range(MQ):
                        mm = pe.transpose(TB[:, q * P:(q + 1) * P], xn[:, q], ident[:])
                    mm.then_inc(tp.sem, 1)
                if has_main(kk):
                    contexts(k, 0)
                if has_front(kk):
                    pe.wait_ge(xnT_ok.sem, xnT_ok.at(k1))
                    if has_main(kk):
                        pe.wait_ge(vb_ok.sem, vb_ok.at(k, 2))
                    pe.matmul(Vq, w[:, 0], xnT[:, n], start=True, stop=True).then_inc(q_ps.sem, 1)
                    pe.matmul(Vk, w[:, 1], xnT[:, n], start=True, stop=True).then_inc(k_ps.sem, 1)
                if has_main(kk):
                    if not has_front(kk):
                        pe.wait_ge(ch_ok.sem, ch_ok.at(k, 0))
                    project(k, 0, w[:, 3])
                    contexts(k, 1)
                if has_front(kk):
                    values_scores(k1, 0, w[:, 2])
                if has_main(kk):
                    pe.wait_ge(ch_ok.sem, ch_ok.at(k, 1))
                    project(k, 1, w[:, 3])

            in_pairs(pe, MCH, -1, body)

            K = MCH
            pe.wait_ge(means_ok, 1)
            pe.matmul(Vq[:, 0:HT], w[:, 4], means[:], start=True, stop=True).then_inc(q_ps.sem, 1)
            pe.matmul(Vk[:, 0:HT], w[:, 5], means[:], start=True, stop=True).then_inc(k_ps.sem, 1)
            values_scores(K, 0, w[:, 6])
            contexts(K, 0)
            project(K, 0, w[:, 7])
            pe.wait_ge(consts, 1)
            pe.wait_ge(g_ok, 1)
            pe.matmul(TB[:, HT:HT + 1], ones[:], tern[:, 0:1], start=True, stop=True).then_inc(wsum, 1)

            pe.wait_ge(consts, 2)

            def last(k, p, kk):
                pe.wait_ge(f_ld.sems[p], f_ld.at(k, p, 3))
                pe.matmul(SL[:, p], wt[:], xnT[:, p], start=True, stop=True).then_inc(f_ps.sem, 1)
                pe.wait_ge(f_pr.sem, f_pr.at(k))
                for q in range(MQ):
                    mm = pe.transpose(RT[:, p, q * P:(q + 1) * P],
                                      ch[:, p].rearrange("p a b -> p (a b)")[:, q * P:(q + 1) * P], ident[:])
                mm.then_inc(f_tp.sem, 1)

            in_pairs(pe, MCH, 0, last)

        @block.scalar
        def _(act):
            act.wait_ge(w_load, 16 * NW)
            act.wait_ge(power_ok, 2)

            def values(k, hf):
                act.wait_ge(v_ps.sem, v_ps.at(k, hf + 1))
                act.wait_ge(av_ps.sem, av_ps.at(k, hf - 1))
                for j in range(4):
                    ins = act.activation(vb[:, hf, :, 8 * j:8 * j + 8],
                                         V[:].rearrange("p c (g j e) -> p (c g) j e", g=G, j=4)[:, :, j],
                                         ACT.Copy, scale=vmask[:, j:j + 1])
                ins.then_inc(vb_ok.sem, 1)

            def exponentials(k, hf):
                act.wait_ge(sub_ok.sem, sub_ok.at(k, hf + 1))
                act.activation(e[:, hf], e[:, hf], ACT.Exp, scale=SC).then_inc(ex_ok.sem, 1)

            def queries_keys(k1, nc_):
                act.wait_ge(q_ps.sem, q_ps.at(k1))
                for j in range(4):
                    ins = act.activation(qm[:, 0:nc_, j], Vq[:, 0:nc_ * CH].rearrange("p (c q) -> p c q", q=CH),
                                         ACT.Copy, scale=jmask[:, j:j + 1])
                ins.then_inc(qm_ok.sem, 1)
                act.wait_ge(k_ps.sem, k_ps.at(k1))
                for g in range(G):
                    a = slice(32 * g, 32 * g + 32)
                    ins = act.activation(km[a, 0:nc_, g], Vk[a, 0:nc_ * CH].rearrange("p (c q) -> p c q", q=CH),
                                         ACT.Copy)
                ins.then_inc(km_ok.sem, 1)

            def body(k, p, kk):
                if has_main(kk):
                    exponentials(k, 0)
                    values(k, 1)
                if has_front(kk):
                    k1 = k + 1
                    act.wait_ge(tp.sem, tp.at(k1))
                    act.wait_ge(xnT_st.sem, xnT_st.at(k1, -1))
                    act.activation(xnT[:, 1 - p], TB[:], ACT.Copy).then_inc(xnT_ok.sem, 1)
                if has_main(kk):
                    exponentials(k, 1)
                if has_front(kk):
                    queries_keys(k1, 2 * HC)
                    values(k1, 0)

            in_pairs(act, MCH, -1, body)
            queries_keys(MCH, HC)
            values(MCH, 0)
            exponentials(MCH, 0)

            def last(k, p, kk):
                act.wait_ge(f_ps.sem, f_ps.at(k))
                act.activation(sg_in[:, p].rearrange("p q d -> p (q d)"), SL[:, p], ACT.Silu).then_inc(f_sl.sem, 1)

            in_pairs(act, MCH, 0, last)

        @block.vector
        def _(v):
            for c in (x_rd, sub_ok, ctx_ok, ch_ok, f_out):
                c.give(v)
            v.wait_ge(w_load, 16 * NW)
            v.tensor_reduce(tern[:, 0:1], wt[:], AX.X, ALU.add, apply_absolute_value=True).then_inc(consts, 1)

            def softmax_in(k, hf, masked=False):
                src = S[:, hf].rearrange("p c (g q) -> p c g q", q=CH)
                v.wait_ge(s_ps.sem, s_ps.at(k, hf + 1))
                if masked:
                    for g in range(G):
                        v.tensor_tensor(e[:, hf, :, g], src[:, :, g], bmask[:].unsqueeze(1).broadcast_to([P, HC, CH]),
                                        ALU.add).then_inc(wchain, 1)
                    v.wait_ge(wchain, 4)
                    src = e[:, hf]
                v.tensor_reduce(mx[:].rearrange("p (c g) -> p c g", g=G), src, AX.X, ALU.max).then_inc(mx_ok.sem, 1)
                v.wait_ge(mx_ok.sem, mx_ok.at(k, hf + 1))
                v.tensor_tensor(e[:, hf], src, mx[:].rearrange("p (c g) -> p c g", g=G).unsqueeze(3).broadcast_to(
                    [P, HC, G, CH]), ALU.subtract).then_inc(sub_ok.sem, 1)

            def turn(k, hf):
                v.wait_ge(ex_ok.sem, ex_ok.at(k, hf + 1))
                v.wait_ge(av_ps.sem, av_ps.at(k, hf - 1))
                v.transpose(eT[:, hf].rearrange("p c g q -> p (c g q)"),
                            e[:, hf].rearrange("p c g q -> p (c g q)")).then_inc(eT_ok.sem, 1)

            def normalise(k, hf):
                v.wait_ge(av_ps.sem, av_ps.at(k, hf + 1))
                v.reciprocal(rden[:], C[:, 1]).then_inc(rd_ok.sem, 1)
                v.wait_ge(rd_ok.sem, rd_ok.at(k, hf + 1))
                v.tensor_tensor(ctxT[:, hf], C[:, 0], rden[:], ALU.mult).then_inc(ctx_ok.sem, 1)

            def residual(k, p, hf):
                v.wait_ge(o_ps.sem, o_ps.at(k, hf + 1))
                v.wait_ge(ch_st.sem, ch_st.at(k, -1))
                v.tensor_tensor(ch[:, p, hf], TB[:, 0:HT], xnT[:, p, hf * HT:(hf + 1) * HT],
                                ALU.add).then_inc(ch_ok.sem, 1)
                v.wait_ge(ch_ok.sem, ch_ok.at(k, hf + 1))
                v.sem_inc(spare, 1)
                v.tensor_reduce(means[:, bass.ds(k * (2 * HC) + hf * HC, HC)],
                                ch[:, p, hf].rearrange("p (c q) -> p c q", q=CH), AX.X, ALU.add).then_inc(sum_ok, 1)

            def front_sum(k1, n):
                v.wait_ge(x_ld.sem, x_ld.at(k1, 3))
                v.wait_ge(x1_st.sem, x1_st.at(k1, -1))
                v.tensor_tensor(x1[:, n], x_in[:, n], sg_in[:, n], ALU.add).then_inc(x1_ok.sem, 1)
                v.wait_ge(x1_ok.sem, x1_ok.at(k1))
                v.sem_inc(x_rd.sem, 1)
                for q in range(MQ):
                    ins = v.bn_stats(stats[:, q], x1[:, n, q])
                ins.then_inc(dch.sem, 1)
                v.wait_ge(dch.sem, dch.at(k1, 1))
                v.sem_inc(spare, 1)
                for q in range(MQ):
                    ins = v.bn_aggr(mv[:, q], stats[:, q])
                ins.then_inc(moments.sem, 1)

            def front_norm(k1, n):
                v.wait_ge(rstd_ok.sem, rstd_ok.at(k1))
                v.wait_ge(tp.sem, tp.at(k1, 0))
                for q in range(MQ):
                    ins = v.tensor_scalar(xn[:, q], x1[:, n, q], mv[:, q, 0:1], rstd[:, 0, q:q + 1],
                                          ALU.subtract, ALU.mult)
                ins.then_inc(xn_ok.sem, 1)

            def body(k, p, kk):
                k1, n = k + 1, 1 - p
                if has_front(kk):
                    front_sum(k1, n)
                if has_main(kk):
                    softmax_in(k, 0)
                if has_front(kk):
                    front_norm(k1, n)
                if has_main(kk):
                    turn(k, 0)
                    softmax_in(k, 1)
                    turn(k, 1)
                    normalise(k, 0)
                    residual(k, p, 0)
                    normalise(k, 1)
                    residual(k, p, 1)

            in_pairs(v, MCH, -1, body)
            K = MCH
            v.wait_ge(sum_ok, 2 * MCH)
            v.tensor_scalar(means[:], means[:], 1.0 / CH, None, ALU.mult).then_inc(means_ok, 1)
            softmax_in(K, 0, masked=True)
            turn(K, 0)
            normalise(K, 0)
            v.wait_ge(o_ps.sem, o_ps.at(K, 1))
            v.tensor_tensor(gT[:], TB[:, 0:HT], means[:], ALU.add).then_inc(g_ok, 1)
            v.wait_ge(wsum, 1)
            v.tensor_scalar(tern[:, 1:2], TB[:, HT:HT + 1], 1.0 / (D * D), 1e-5, ALU.mult, ALU.max).then_inc(wchain, 1)
            v.wait_ge(wchain, 5)
            v.reciprocal(tern[:, 2:3], tern[:, 1:2]).then_inc(wchain, 1)
            v.wait_ge(wchain, 6)
            v.tensor_scalar(wt[:], wt[:], tern[:, 2:3], 1.0, ALU.mult, ALU.min).then_inc(wchain, 1)
            v.wait_ge(wchain, 7)
            v.tensor_scalar(wt[:], wt[:], -1.0, 12582912.0, ALU.max, ALU.add).then_inc(wchain, 1)
            v.wait_ge(wchain, 8)
            v.tensor_scalar(wt[:], wt[:], 12582912.0, tern[:, 1:2], ALU.subtract, ALU.mult).then_inc(consts, 1)
            v.wait_ge(g_ok, 1)

            def last(k, p, kk):
                chp = ch[:, p].rearrange("p a (c q) -> p (a c) q", q=CH)
                v.wait_ge(f_ld.sems[p], f_ld.at(k, p, 3))
                v.tensor_tensor(chp, chp, gT[:, bass.ds(k * 2 * HC, 2 * HC)].unsqueeze(2).broadcast_to(
                    [P, 2 * HC, CH]), ALU.add).then_inc(f_en.sem, 1)
                v.wait_ge(f_sl.sem, f_sl.at(k))
                v.wait_ge(f_en.sem, f_en.at(k))
                v.tensor_tensor(chp, chp, sg_in[:, p].rearrange("p q (c t) -> p (q c) t", t=CH),
                                ALU.mult).then_inc(f_pr.sem, 1)
                v.wait_ge(f_tp.sem, f_tp.at(k))
                v.wait_ge(f_st.sems[p], f_st.at(k, p, 0))
                v.tensor_tensor(x1[:, p].rearrange("p q d -> p (q d)"), RT[:, p],
                                x_in[:, p].rearrange("p q d -> p (q d)"), ALU.add).then_inc(f_out.sem, 1)

            in_pairs(v, MCH, 0, last)


def host_arrays(i):
    c = np.ascontiguousarray
    x = i["L0_attn_x"]
    out = {"x_tm": c(x.transpose(1, 0, 2).reshape(T, D)), "ident": np.eye(P, dtype=np.float32)}
    for n, a, s in (("gate_w", "L0_ffn_gate_w", "L0_ffn_sh_gate_w"), ("up_w", "L0_ffn_up_w", "L0_ffn_sh_up_w")):
        out[n] = c(np.concatenate([i[a].reshape(-1, D), i[s]], 0).T)
    down = np.concatenate([i["L0_ffn_down_w"].transpose(0, 2, 1).reshape(-1, D), i["L0_ffn_sh_down_w"].T], 0)
    out["down_w"] = c(down.reshape(NJ, P, D).transpose(1, 0, 2))
    out["router_w"] = c(i["L0_ffn_router_weight"].T)
    out["e_bias"] = c(np.broadcast_to(i["L0_ffn_e_bias"], (P, E_ALL)))
    w = lambda n: i["L0_attn_" + n]
    halves = lambda a: c(a.reshape(2, P, -1).transpose(1, 0, 2))
    out["w_in"] = c(w("W_in").T)
    out["taps"] = c(np.broadcast_to(w("conv_w")[:, 0].T.reshape(1, -1), (P, 4 * DI)))
    out["a_log"] = c(halves(w("A_log")).reshape(P, -1))
    out["dt_w"], out["out_w"] = halves(w("W_dt").T), halves(w("W_out").T)
    out["bc_w"] = halves(np.concatenate([w("W_B"), w("W_C")], 0).T)
    for n, a in (("conv_b", "conv_b"), ("b_dt", "b_dt"), ("d_param", "D_param")):
        out[n] = c(w(a).reshape(2, P).T)
    out["residual"] = c(np.broadcast_to(w("residual_scale").reshape(1, 1), (P, 1)))
    out["x_bt"] = c(x.reshape(T, D))
    out["attn_w"] = c(np.stack([i["L1_attn_W" + n + s] for s in ("_l", "_g") for n in "qkvo"], 1))
    out["tern_w"] = c(i["L1_ffn_weight"].T)
    out["norm_w"] = c(w("norm_w").reshape(P, 1))
    return out


def constants():
    bf16 = mybir.dt.np(BF16)
    sel = np.zeros((96, 8 * P), bf16)
    for a in range(3):
        for e in range(E_ALL):
            sel[32 * a + e, (e // 2) * P + (e % 2) * 64:(e // 2) * P + (e % 2) * 64 + 64] = 1
    pick = np.zeros((96, NS), bf16)
    for a in range(3):
        pick[32 * a:32 * a + NS] = np.eye(NS)
    row, head = np.arange(P), np.arange(4)
    bmask = np.where(row[:, None] % 32 // 8 == np.arange(32) // 8, 0.0, -1e30)
    return {"jmask": (row[:, None] // 8 % 4 == head).astype(np.float32),
            "vmask": (row[:, None] // 32 == head).astype(np.float32),
            "osum": (row[:, None] // 32 == np.arange(32) // 8).astype(np.float32),
            "bmask": bmask.astype(np.float32), "moe_sel": sel, "pick": pick, "ident_b": np.eye(64).astype(bf16),
            "ones": np.ones((P, P), np.float32)}


def program(nc, io, scratch, out):
    expert_phase(nc, io, scratch)
    scan_phase(nc, io, scratch)
    attention_phase(nc, io, scratch, out)


SCRATCH = (("xnT", (P, TP)), ("xrT", (P, HALO + TP)), ("gT", (P, TP)), ("xg", (NC * P, 4 * ST)), ("cT", (NC * 96, ST), BF16), ("sg", (TP, D)),
           ("x1", (P, T)), ("xnT1", (P, T)), ("ch", (P, T)))


def kernel(**inputs):
    import concourse.bacc as bacc
    from concourse.bass_utils import run_bass_kernel_spmd

    arrays = {**host_arrays({k: np.asarray(v) for k, v in inputs.items()}), **constants()}
    nc = bacc.Bacc("TRN2", target_bir_lowering=False, num_devices=1, dynamic_dma_scratch_size=1024)
    io = {n: nc.dram_tensor("in_" + n, a.shape, mybir.dt.from_np(a.dtype), kind="ExternalInput").ap()
          for n, a in arrays.items()}
    scratch = {n: nc.dram_tensor(n, s, *(t or (F32,)), kind="Internal").ap() for n, s, *t in SCRATCH}
    out = nc.dram_tensor("out", (T, D), F32, kind="ExternalOutput").ap()
    program(nc, io, scratch, out)
    r = run_bass_kernel_spmd(nc, [{"in_" + n: a for n, a in arrays.items()}], core_ids=[0])
    return r.results[0]["out"].reshape(B, L, D)
```

```python
import numpy as np
from contextlib import ExitStack

import concourse.bass as bass
from concourse import mybir

F32 = mybir.dt.float32
BF16 = mybir.dt.bfloat16
ALU = mybir.AluOpType
ACT = mybir.ActivationFunctionType
AX = mybir.AxisListType

P = 128
B, L, D = 32, 256, 128
T = B * L
DI = 256
NS = 16
E_ALL, TOPK = 16, 4
GROUPS, TOPG = 4, 2
MOE_SCALE = 2.5

MT = 512
MCH = T // MT
MQ = MT // P
NJ = 9
JP = 23
STEPS = 10
NC = -(-L // STEPS)
ST = STEPS * B
TP = NC * ST
HALO = 3 * B


class Count:

    def __init__(self, ctx, nc, name, per, credit=0, by=1):
        self.sem, self.per, self.credit, self.by = ctx.enter_context(nc.semaphore(name)), per, credit, by

    def at(self, k, n=1):
        return k * (self.per * self.by) + (self.credit + n * self.by)

    def give(self, eng):
        eng.sem_inc(self.sem, self.credit)


class Alternate:

    def __init__(self, ctx, nc, name, per, credit=0):
        self.sems = [ctx.enter_context(nc.semaphore(f"{name}_{p}")) for p in range(2)]
        self.half, self.credit = per * 8, credit

    def at(self, k, p, n=1):
        return k * self.half + (self.credit - p * self.half + n * 16)

    def give(self, eng):
        for s in self.sems:
            eng.sem_inc(s, self.credit)


def in_pairs(eng, n, first, body, loop_from=0, tail=2):
    for k in range(first, loop_from):
        body(k, k % 2, k)
    loops = (n - tail - loop_from) // 2
    with eng.Fori(0, loops) as i:
        body(i * 2 + loop_from, 0, None)
        body(i * 2 + (loop_from + 1), 1, None)
    for k in range(loop_from + 2 * loops, n):
        body(k, k % 2, k)


def expert_phase(nc, io, scratch):
    with ExitStack() as ctx:
        def sb(name, shape, dt=F32):
            return ctx.enter_context(nc.sbuf_tensor("m_" + name, shape, dt))

        def ps(name, shape, dt=F32):
            return ctx.enter_context(nc.psum_tensor("m_" + name, shape, dt))

        def cnt(name, per, credit=0, by=1):
            return Count(ctx, nc, "m_" + name, per, credit, by)

        gate_w = sb("gate_w", [P, NJ * P])
        up_w = sb("up_w", [P, NJ * P])
        down_w = sb("down_w", [P, NJ, D])
        router_w = sb("router_w", [P, E_ALL])
        e_bias = sb("e_bias", [P, E_ALL])
        sel = sb("sel", [96, 8 * P], BF16)
        ident = sb("ident", [P, P])
        ahead = sb("ahead", [P, E_ALL])
        restart = sb("restart", [P, MQ * E_ALL])
        mhalf = sb("mhalf", [P, MQ])
        x_in = sb("x_in", [P, 2, MQ, D])
        xn = sb("xn", [P, MQ, D])
        xr = sb("xr", [P, MQ, D])
        stats = sb("stats", [P, MQ, 6])
        mv = sb("mv", [P, MQ, 2])
        pt = sb("pt", [P, 4, MQ])
        rstd = sb("rstd", [P, 2, MQ])
        xnT = sb("xnT", [P, 2, MT])
        xrT = sb("xrT", [P, MT])
        th = sb("th", [P, MQ, E_ALL])
        r = {n: sb("r_" + n, [P, MQ, E_ALL]) for n in
             ("sig", "sc", "msk", "gt", "eq", "cum", "sel", "tw", "c", "r1")}
        pairs = sb("pairs", [P, MQ * GROUPS, 6])
        gs = sb("gs", [P, MQ, GROUPS])
        wins = sb("wins", [P, MQ, GROUPS])
        cmp = sb("cmp", [P, MQ, GROUPS])
        top8 = sb("top8", [P, MQ, 8])
        room = sb("room", [P, MQ])
        den = sb("den", [P, MQ])
        hi = sb("hi", [P, MQ, E_ALL], BF16)
        c3 = sb("c3", [P, MQ, 96])
        cT = sb("cT", [96, 2, MT], BF16)
        sl = sb("sl", [P, 2, MT])
        hb = sb("hb", [P, 2, MT])
        hid = sb("hid", [P, 2, MT])
        g_out = sb("g_out", [P, 2, MT])
        zero = sb("zero", [P, P])

        pg = ps("pg", [P, 2, MT])
        pu = ps("pu", [P, 2, MT])
        pc = ps("pc", [P, MT])
        py = ps("py", [P, MT])
        pf = ps("pf", [P, 2, MT])

        w_load = ctx.enter_context(nc.semaphore("m_w_load"))
        front_load = ctx.enter_context(nc.semaphore("m_front_load"))
        consts = ctx.enter_context(nc.semaphore("m_consts"))
        spare = ctx.enter_context(nc.semaphore("m_spare"))
        zeroed = ctx.enter_context(nc.semaphore("m_zeroed"))
        pads = ctx.enter_context(nc.semaphore("m_pads"))
        x_load = Alternate(ctx, nc, "m_x_load", 1)
        x_used = cnt("x_used", 1, 2)
        moments = cnt("moments", 1)
        rstd_ok = cnt("rstd_ok", 1)
        pchain = cnt("pchain", 7)
        xn_ok = cnt("xn_ok", 1)
        tp_n = cnt("tp_n", 1, 1)
        tp_r = cnt("tp_r", 1, 1)
        xnT_ok = cnt("xnT_ok", 1)
        xrT_ok = cnt("xrT_ok", 1)
        logits = cnt("logits", 1)
        th_ok = cnt("th_ok", 1)
        c3_ok = cnt("c3_ok", 1, 1)
        c_tp = cnt("c_tp", 1)
        cT_ok = cnt("cT_ok", 1, 1)
        xn_st = cnt("xn_st", 1, 32, by=16)
        xr_st = cnt("xr_st", 1, 16, by=16)
        gu_ok = cnt("gu_ok", NJ)
        sl_ok = cnt("sl_ok", NJ)
        hb_ok = cnt("hb_ok", NJ, 2)
        cb_ok = cnt("cb_ok", NJ - 1)
        hid_ok = cnt("hid_ok", NJ, 2)
        down_ok = cnt("down_ok", NJ, 2)
        g_ok = cnt("g_ok", 1, 1)
        g_st = cnt("g_st", 1, 32, by=16)
        dch = ctx.enter_context(nc.semaphore("m_dve_chain"))
        stats_ok = cnt("stats_ok", 1)
        DCH = 41
        NW = 4

        def has_norms(kk):
            return kk is None or kk + 2 < MCH

        def has_routing(kk):
            return kk is None or 0 <= kk + 1 < MCH

        def has_experts(kk):
            return kk is None or kk >= 0

        def turns(eng, body):
            in_pairs(eng, MCH, -2, body, tail=3)

        block = ctx.enter_context(nc.Block())

        @block.sync
        def _(sp):
            def load(kn, slot):
                sp.dma_start(x_in[:, slot], io["x_tm"][bass.ds(kn * MT, MT), :].rearrange(
                    "(q p) d -> p q d", p=P)).then_inc(x_load.sems[slot], 16)

            load(0, 0)
            for dst, src in ((ident, "ident"), (router_w, "router_w"), (e_bias, "e_bias")):
                sp.dma_start(dst[:], io[src]).then_inc(front_load, 16)
            for dst, src in ((gate_w, "gate_w"), (up_w, "up_w"), (sel, "moe_sel"), (down_w, "down_w")):
                sp.dma_start(dst[:], io[src]).then_inc(w_load, 16)
            xn_st.give(sp)
            xr_st.give(sp)
            g_st.give(sp)
            sp.wait_ge(zeroed, 1)
            sp.dma_start(scratch["xrT"][:, 0:HALO], zero[:, 0:HALO]).then_inc(pads, 16)
            for name, at in (("xrT", HALO + T), ("xnT", T), ("gT", T)):
                sp.dma_start(scratch[name][:, at:at + TP - T], zero[:, 0:TP - T]).then_inc(pads, 16)

            def wait(c, value):
                sp.wait_ge(c.sem, value)
                sp.sem_inc(spare, 1)

            def body(k, p, kk):
                if kk is None or kk + 3 < MCH:
                    wait(x_used, x_used.at(k + 2, 0))
                    load(k + 3, 1 - p)
                if has_experts(kk):
                    wait(g_ok, g_ok.at(k))
                    sp.dma_start(scratch["gT"][:, bass.ds(k * MT, MT)], g_out[:, p]).then_inc(g_st.sem, 16)
                if has_norms(kk):
                    wait(xnT_ok, xnT_ok.at(k + 2))
                    sp.dma_start(scratch["xnT"][:, bass.ds((k + 2) * MT, MT)], xnT[:, p]).then_inc(xn_st.sem, 16)
                    wait(xrT_ok, xrT_ok.at(k + 2))
                    sp.dma_start(scratch["xrT"][:, bass.ds((k + 2) * MT + HALO, MT)], xrT[:]).then_inc(xr_st.sem, 16)

            turns(sp, body)
            sp.wait_ge(pads, 64)
            sp.wait_ge(xn_st.sem, xn_st.at(MCH - 1))
            sp.sem_inc(spare, 1)
            sp.wait_ge(xr_st.sem, xr_st.at(MCH - 1))
            sp.sem_inc(spare, 1)
            sp.wait_ge(g_st.sem, g_st.at(MCH - 1))
            sp.sem_inc(spare, 1)

        @block.gpsimd
        def _(pool):
            pool.memset(mhalf[:], -0.5).then_inc(consts, 1)
            pool.wait_ge(consts, 4)

            def body(k, p, kk):
                if not has_norms(kk):
                    return
                k1 = k + 2
                step = [0]

                def link(ins):
                    step[0] += 1
                    ins.then_inc(pchain.sem, 1)
                    pool.wait_ge(pchain.sem, pchain.at(k1, step[0]))
                    if step[0] == 4:
                        pool.sem_inc(spare, 1)

                pool.wait_ge(moments.sem, moments.at(k1))
                pool.sem_inc(spare, 1)
                link(pool.tensor_scalar(pt[:, 0], mv[:, :, 1], 1e-5, None, ALU.add))
                link(pool.tensor_tensor(rstd[:, 0], pt[:, 0], mhalf[:], ALU.pow))
                link(pool.tensor_tensor(pt[:, 1], rstd[:, 0], rstd[:, 0], ALU.mult))
                link(pool.tensor_tensor(pt[:, 2], pt[:, 1], mv[:, :, 1], ALU.mult))
                link(pool.tensor_scalar(pt[:, 3], pt[:, 2], 1e-6, None, ALU.add))
                link(pool.tensor_tensor(pt[:, 1], pt[:, 3], mhalf[:], ALU.pow))
                link(pool.tensor_tensor(rstd[:, 1], pt[:, 1], rstd[:, 0], ALU.mult))
                pool.sem_inc(rstd_ok.sem, 1)

            turns(pool, body)

        @block.tensor
        def _(pe):
            tp_n.give(pe)
            tp_r.give(pe)
            pe.wait_ge(front_load, 16 * 3)
            pe.wait_ge(consts, 4)

            def gate_up(k, p, j):
                s = (p + j) % 2
                pe.wait_ge(hb_ok.sem, hb_ok.at(k, j - 1))
                pe.matmul(pg[:, s], gate_w[:, j * P:(j + 1) * P], xnT[:, p], start=True, stop=True)
                pe.matmul(pu[:, s], up_w[:, j * P:(j + 1) * P], xnT[:, p], start=True,
                          stop=True).then_inc(gu_ok.sem, 1)

            def spread(k, p, j):
                if j == 0:
                    pe.wait_ge(cT_ok.sem, cT_ok.at(k))
                pe.wait_ge(hid_ok.sem, hid_ok.at(k, j if j else -1))
                pe.matmul(pc[:], sel[:, j * P:(j + 1) * P], cT[:, p], start=True, stop=True).then_inc(cb_ok.sem, 1)

            def down(k, p, j):
                s = (p + j) % 2
                pe.wait_ge(hid_ok.sem, hid_ok.at(k, j + 1))
                if j == 0:
                    pe.wait_ge(g_ok.sem, g_ok.at(k, 0))
                pe.matmul(py[:], down_w[:, j], hid[:, s], start=(j == 0), stop=(j == NJ - 1)).then_inc(down_ok.sem, 1)

            def logits_of(k, p):
                pe.wait_ge(xnT_ok.sem, xnT_ok.at(k))
                for q in range(MQ):
                    mm = pe.matmul(pf[:, 0, q * E_ALL:(q + 1) * E_ALL], xnT[:, p, q * P:(q + 1) * P],
                                   router_w[:], start=True, stop=True)
                mm.then_inc(logits.sem, 1)

            def turn_c(k):
                pe.wait_ge(c3_ok.sem, c3_ok.at(k))
                pe.wait_ge(xrT_ok.sem, xrT_ok.at(k))
                for q in range(MQ):
                    mm = pe.transpose(pf[0:96, 1, q * P:(q + 1) * P], c3[:, q], ident[:])
                mm.then_inc(c_tp.sem, 1)

            def turn_xn(k, kk):
                pe.wait_ge(xn_ok.sem, xn_ok.at(k))
                if has_routing(kk):
                    pe.wait_ge(th_ok.sem, th_ok.at(k - 1))
                for q in range(MQ):
                    mm = pe.transpose(pf[:, 0, q * P:(q + 1) * P], xn[:, q], ident[:])
                mm.then_inc(tp_n.sem, 1)

            def turn_xr(k, kk):
                if has_routing(kk):
                    pe.wait_ge(cT_ok.sem, cT_ok.at(k - 1))
                for q in range(MQ):
                    mm = pe.transpose(pf[:, 1, q * P:(q + 1) * P], xr[:, q], ident[:])
                mm.then_inc(tp_r.sem, 1)

            def body(k, p, kk):
                if has_routing(kk):
                    logits_of(k + 1, 1 - p)
                if has_experts(kk):
                    for j in range(NJ - 1):
                        gate_up(k, p, j + 1)
                        spread(k, p, j)
                        if j:
                            down(k, p, j - 1)
                if has_routing(kk):
                    if kk == -1:
                        pe.wait_ge(w_load, 16 * NW)
                    gate_up(k + 1, 1 - p, 0)
                if has_experts(kk):
                    down(k, p, NJ - 2)
                if has_routing(kk):
                    turn_c(k + 1)
                if has_norms(kk):
                    turn_xn(k + 2, kk)
                if has_experts(kk):
                    down(k, p, NJ - 1)
                if has_norms(kk):
                    turn_xr(k + 2, kk)

            turns(pe, body)

        @block.scalar
        def _(act):
            g_ok.give(act)
            cT_ok.give(act)

            def main(k, p, j):
                s = (p + j) % 2
                act.wait_ge(gu_ok.sem, gu_ok.at(k, j + 1))
                act.activation(sl[:, s], pg[:, s], ACT.Silu).then_inc(sl_ok.sem, 1)

            def body(k, p, kk):
                if has_routing(kk):
                    act.wait_ge(logits.sem, logits.at(k + 1))
                    act.wait_ge(c3_ok.sem, c3_ok.at(k + 1, 0))
                    act.activation(th[:], pf[:, 0, 0:MQ * E_ALL], ACT.Tanh, scale=0.5).then_inc(th_ok.sem, 1)
                if has_experts(kk):
                    for j in range(1, NJ):
                        main(k, p, j)
                if has_routing(kk):
                    main(k + 1, 1 - p, 0)
                    act.wait_ge(c_tp.sem, c_tp.at(k + 1))
                    act.activation(cT[:, 1 - p], pf[0:96, 1], ACT.Copy).then_inc(cT_ok.sem, 1)
                if has_norms(kk):
                    act.wait_ge(tp_n.sem, tp_n.at(k + 2))
                    act.wait_ge(xn_st.sem, xn_st.at(k + 2, 0))
                    act.activation(xnT[:, p], pf[:, 0], ACT.Copy).then_inc(xnT_ok.sem, 1)
                if has_experts(kk):
                    act.wait_ge(down_ok.sem, down_ok.at(k, NJ))
                    act.wait_ge(g_st.sem, g_st.at(k, 0))
                    act.activation(g_out[:, p], py[:], ACT.Silu).then_inc(g_ok.sem, 1)
                if has_norms(kk):
                    act.wait_ge(tp_r.sem, tp_r.at(k + 2))
                    act.wait_ge(xr_st.sem, xr_st.at(k + 2, 0))
                    act.activation(xrT[:], pf[:, 1], ACT.Copy).then_inc(xrT_ok.sem, 1)

            turns(act, body)

        @block.vector
        def _(v):
            x_used.give(v)
            c3_ok.give(v)
            hb_ok.give(v)
            hid_ok.give(v)
            v.sem_inc(down_ok.sem, 2)
            v.memset(c3[:], 0.0).then_inc(consts, 1)
            v.memset(restart[:], 1.0).then_inc(dch, 1)
            for i in range(GROUPS):
                v.memset(ahead[:].rearrange("p (q g) -> p q g", g=GROUPS)[:, :, i], float(i)).then_inc(dch, 1)
            v.wait_ge(dch, 5)
            v.memset(restart[:].rearrange("p (q e) -> p q e", e=E_ALL)[:, :, 0], 0.0).then_inc(consts, 1)
            v.memset(zero[:], 0.0).then_inc(zeroed, 1)
            v.wait_ge(zeroed, 1)
            v.memset(cmp[:], 0.0).then_inc(consts, 1)
            v.wait_ge(consts, 4)
            v.wait_ge(front_load, 16 * 3)
            LINKS_0 = 5

            def multiplied(k, p, j):
                v.wait_ge(sl_ok.sem, sl_ok.at(k, j + 1))
                s = (p + j) % 2
                if j == NJ - 1:
                    v.wait_ge(down_ok.sem, down_ok.at(k, j - 1))
                v.tensor_tensor((hb if j < NJ - 1 else hid)[:, s], sl[:, s], pu[:, s], ALU.mult).then_inc(hb_ok.sem, 1)

            def weighted(k, p, j):
                s = (p + j) % 2
                v.wait_ge(hb_ok.sem, hb_ok.at(k, j + 1))
                if j < NJ - 1:
                    v.wait_ge(cb_ok.sem, cb_ok.at(k, j + 1))
                    v.wait_ge(down_ok.sem, down_ok.at(k, j - 1))
                    v.tensor_tensor(hid[:, s], hb[:, s], pc[:], ALU.mult).then_inc(hid_ok.sem, 1)
                else:
                    v.sem_inc(hid_ok.sem, 1)

            def moments_of(k, p):
                v.wait_ge(x_load.sems[p], x_load.at(k, p))
                for q in range(MQ):
                    ins = v.bn_stats(stats[:, q], x_in[:, p, q])
                ins.then_inc(stats_ok.sem, 1)
                v.wait_ge(stats_ok.sem, stats_ok.at(k))
                v.sem_inc(spare, 1)
                for q in range(MQ):
                    ins = v.bn_aggr(mv[:, q], stats[:, q])
                ins.then_inc(moments.sem, 1)

            def norms_of(k, p):
                v.wait_ge(rstd_ok.sem, rstd_ok.at(k))
                v.wait_ge(tp_n.sem, tp_n.at(k, 0))
                v.wait_ge(tp_r.sem, tp_r.at(k, 0))
                for q in range(MQ):
                    v.tensor_scalar(xn[:, q], x_in[:, p, q], mv[:, q, 0:1], rstd[:, 0, q:q + 1],
                                    ALU.subtract, ALU.mult)
                    ins = v.tensor_scalar(xr[:, q], x_in[:, p, q], mv[:, q, 0:1], rstd[:, 1, q:q + 1],
                                          ALU.subtract, ALU.mult)
                ins.then_inc(xn_ok.sem, 1)
                v.wait_ge(xn_ok.sem, xn_ok.at(k))
                v.sem_inc(x_used.sem, 1)

            def routing(k, step):
                def link(ins):
                    step[0] += 1
                    ins.then_inc(dch, 1)
                    return ins

                v.wait_ge(th_ok.sem, th_ok.at(k))
                yield link(v.tensor_scalar(r["sig"][:], th[:], 0.5, 0.5, ALU.mult, ALU.add))
                yield link(v.tensor_tensor(r["sc"][:], r["sig"][:],
                                     e_bias[:].unsqueeze(1).broadcast_to([P, MQ, E_ALL]), ALU.add))
                sc4 = r["sc"][:].rearrange("p q (g e) -> p (q g) e", e=4)
                at = 0
                for s in (1, 2, 3):
                    ins = v.tensor_tensor(pairs[:, :, at:at + 4 - s], sc4[:, :, 0:4 - s], sc4[:, :, s:4], ALU.add)
                    at += 4 - s
                    if s < 3:
                        ins.then_inc(dch, 1)
                        step[0] += 1
                yield link(ins)
                yield link(v.tensor_reduce(gs[:].rearrange("p q g -> p (q g)"), pairs[:], AX.X, ALU.max))
                wn = wins[:]
                yield link(v.tensor_copy(wn, ahead[:].rearrange("p (q g) -> p q g", g=GROUPS)))
                for s in (1, 2, 3):
                    n = GROUPS - s
                    yield link(v.tensor_tensor(cmp[:, :, 0:n], gs[:, :, 0:n], gs[:, :, s:GROUPS], ALU.is_ge))
                    yield link(v.tensor_tensor(wn[:, :, 0:n], wn[:, :, 0:n], cmp[:, :, 0:n], ALU.add))
                    yield link(v.tensor_tensor(wn[:, :, s:GROUPS], wn[:, :, s:GROUPS], cmp[:, :, 0:n], ALU.subtract))
                yield link(v.tensor_scalar(wn, wn, float(GROUPS - TOPG) - 0.5, None, ALU.is_gt))
                yield link(v.tensor_tensor(r["msk"][:].rearrange("p q (g e) -> p (q g) e", e=4), sc4,
                                     wins[:].rearrange("p q g -> p (q g)").unsqueeze(2).broadcast_to(
                                         [P, MQ * GROUPS, 4]), ALU.mult))
                v.sem_inc(spare, 1)
                for q in range(MQ):
                    ins = v.max(top8[:, q], r["msk"][:, q])
                    if q < MQ - 1:
                        ins.then_inc(dch, 1)
                        step[0] += 1
                yield link(ins)
                fourth = top8[:, :, TOPK - 1:TOPK].broadcast_to([P, MQ, E_ALL])
                yield link(v.tensor_tensor(r["gt"][:], r["msk"][:], fourth, ALU.is_gt))
                yield link(v.tensor_tensor(r["eq"][:], r["msk"][:], fourth, ALU.is_equal))
                yield link(v.tensor_reduce(room[:], r["gt"][:], AX.X, ALU.add))
                yield link(v.tensor_scalar(room[:], room[:], -1.0, float(TOPK), ALU.mult, ALU.add))
                yield link(v.tensor_tensor_scan(r["cum"][:].rearrange("p q e -> p (q e)"), restart[:],
                                          r["eq"][:].rearrange("p q e -> p (q e)"), 0.0, ALU.mult, ALU.add))
                yield link(v.tensor_tensor(r["cum"][:], r["cum"][:],
                                     room[:].unsqueeze(2).broadcast_to([P, MQ, E_ALL]), ALU.is_le))
                yield link(v.tensor_tensor(r["sel"][:], r["cum"][:], r["eq"][:], ALU.mult))
                yield link(v.tensor_tensor(r["sel"][:], r["sel"][:], r["gt"][:], ALU.add))
                yield link(v.tensor_tensor(r["tw"][:], r["sel"][:], r["sig"][:], ALU.mult))
                yield link(v.tensor_reduce(den[:], r["tw"][:], AX.X, ALU.add))
                yield link(v.tensor_scalar(den[:], den[:], 1e-20, None, ALU.add))
                yield link(v.reciprocal(den[:], den[:]))
                yield link(v.scalar_tensor_tensor(r["c"][:], r["tw"][:], MOE_SCALE,
                                            den[:].unsqueeze(2).broadcast_to([P, MQ, E_ALL]), ALU.mult, ALU.mult))
                v.wait_ge(cT_ok.sem, cT_ok.at(k, 0))
                yield link(v.tensor_copy(hi[:], r["c"][:]))
                yield link(v.tensor_copy(c3[:, :, 0:16], hi[:]))
                yield link(v.tensor_tensor(r["r1"][:], r["c"][:], c3[:, :, 0:16], ALU.subtract))
                yield link(v.tensor_copy(hi[:], r["r1"][:]))
                yield link(v.tensor_copy(c3[:, :, 32:48], hi[:]))
                yield link(v.tensor_tensor(c3[:, :, 64:80], r["r1"][:], c3[:, :, 32:48], ALU.subtract))
                v.sem_inc(c3_ok.sem, 1)

            def body(k, p, kk):
                step, ended = [0], []
                links = routing(k + 1, step)

                def route(n):
                    for _ in range(n):
                        if has_routing(kk) and not ended:
                            if step[0]:
                                v.wait_ge(dch, (k + 1) * DCH + (LINKS_0 + step[0]))
                            if next(links, None) is None:
                                ended.append(True)

                if has_norms(kk):
                    moments_of(k + 2, p)
                if has_experts(kk):
                    weighted(k, p, 0)
                for j in range(1, NJ):
                    if has_experts(kk):
                        multiplied(k, p, j)
                        route(3)
                        weighted(k, p, j)
                        if j < NJ - 1:
                            route(3)
                    if has_norms(kk) and j == 4:
                        norms_of(k + 2, p)
                route(DCH + 1)
                if has_routing(kk):
                    assert step[0] == DCH, step[0]
                    multiplied(k + 1, 1 - p, 0)

            turns(v, body)


def scan_phase(nc, io, scratch):
    R_DT, C_DT = (0.1 - 0.001) / 2, (0.1 + 0.001) / 2
    A_DT = 0.5 / (R_DT + 1e-8)
    NQ = ST // 64
    JH = 12
    with ExitStack() as ctx:
        def sb(name, shape, dt=F32):
            return ctx.enter_context(nc.sbuf_tensor("s_" + name, shape, dt))

        def ps(name, shape, dt=F32):
            return ctx.enter_context(nc.psum_tensor("s_" + name, shape, dt))

        def cnt(name, per, credit=0, by=1):
            return Count(ctx, nc, "s_" + name, per, credit, by)

        def sem(name):
            return ctx.enter_context(nc.semaphore("s_" + name))

        h = sb("h", [P, 2, 2 * NS, ST])
        dA = sb("dA", [P, 2, 2 * NS, ST])
        conv_w = sb("conv_w", [P, 4, DI])
        gate_w = sb("gate_w", [P, DI])
        dt_w = sb("dt_w", [P, 2, DI])
        bc_w = sb("bc_w", [P, 2, 2 * NS])
        out_w = sb("out_w", [P, 2, D])
        pick = sb("pick", [96, NS], BF16)
        ident = sb("ident", [P, P])
        ident_b = sb("ident_b", [64, 64], BF16)
        ones = sb("ones", [P, P])
        cols = sb("cols", [P, 8])
        col2 = sb("col2", [P, 5])
        a16 = sb("a16", [P, 2 * NS])
        cst = sb("cst", [B, 2])
        xr = sb("xr", [P, HALO + ST])
        xg = sb("xg", [P, 4, ST])
        zg = sb("zg", [P, 4, ST])
        th = sb("th", [P, 2, ST])
        z = sb("z", [P, 2, ST])
        tg = sb("tg", [P, 2, ST])
        dt = sb("dt", [P, 2, 2, ST])
        dtx = sb("dtx", [P, 2, 2, ST])
        s3 = sb("s3", [64, NQ, 2, 96], BF16)
        rest = sb("rest", [64, NQ, 2, NS])
        bcT = sb("bcT", [96, 2, 2, ST], BF16)
        cT = sb("cT", [96, 2, ST], BF16)
        prod = sb("prod", [P, 2, 2, ST])
        xn = sb("xn", [P, ST])
        g = sb("g", [P, ST])
        tok = sb("tok", [P, 3, D])
        nrm = sb("nrm", [P, 2, B])
        n2 = sb("n2", [B, 4])
        fac = sb("fac", [P, B])

        F = ps("F", [P, 2, 512])
        X = ps("X", [P, 3, 512])
        Y = ps("Y", [P, 2, 512])
        E = ps("E", [P, 512])
        Fb = F[:, 1, :].bitcast(BF16)

        w_load, consts, aset, vset, setup = (sem(n) for n in ("w_load", "consts", "aset", "vset", "setup"))
        xr_ld = cnt("xr_ld", 1, by=16)
        f_conv = cnt("f_conv", 1)
        a_conv = cnt("a_conv", 1)
        xc_ok = cnt("xc_ok", 1)
        f_gate = cnt("f_gate", 1)
        a_gate = cnt("a_gate", 1)
        gs_ok = cnt("gs_ok", 1, 1)
        f_dt = cnt("f_dt", 1)
        a_ln = cnt("a_ln", 1)
        v_ok = cnt("v_ok", 1)
        sp_ok = cnt("sp_ok", 1)
        a_dt = cnt("a_dt", 2)
        dt_ok = cnt("dt_ok", 1)
        f_bc = cnt("f_bc", 1)
        s3_ok = cnt("s3_ok", 1)
        f_t = cnt("f_t", 1, 1)
        bcT_ok = cnt("bcT_ok", 1)
        xg_st = cnt("xg_st", 1, 16, by=16)
        zg_ld = cnt("zg_ld", 1, by=16)
        xn_ld = cnt("xn_ld", 2, by=16)
        c_st = cnt("c_st", 1, 16, by=16)
        cT_ld = cnt("cT_ld", 1, by=16)
        b_ok = cnt("b_ok", NS)
        b_rd = cnt("b_rd", NS)
        c_ok = cnt("c_ok", NS)
        dA_ok = cnt("dA_ok", 4)
        a_th = cnt("a_th", 2 * NS)
        st0_ok = cnt("st0_ok", 2)
        fac_ok = cnt("fac_ok", 1)
        VST = 3 + 2 * (STEPS - 1)
        vst = cnt("vst", VST)
        sq_ok = cnt("sq_ok", 2)
        nr_ok = cnt("nr_ok", 2)
        n2_ps = cnt("n2_ps", 1)
        n2_ok = cnt("n2_ok", 1)
        n_fac = cnt("n_fac", 1)
        fac_ps = cnt("fac_ps", 1)
        PCH = 9 + 2 * (STEPS - 1)
        pch = cnt("pch", PCH)
        h_ok = cnt("h_ok", 1)
        prod_ok = cnt("prod_ok", NS)
        prod_rd = cnt("prod_rd", NS, 1)
        yy_ok = cnt("yy_ok", 1)
        o_ok = cnt("o_ok", 1, 1)
        sg_ok = cnt("sg_ok", 1)
        o_tp = cnt("o_tp", 1, 1)
        tok_ok = cnt("tok_ok", 1)
        tok_st = cnt("tok_st", 3, 48, by=16)
        vch = cnt("vch", 7)
        a_exp = cnt("a_exp", 2)
        NW = 15

        spare = sem("spare")

        stage = dA[:, 1].rearrange("p a b -> p (a b)")
        w_in, taps, a_log = stage[:, 0:2 * DI], stage[:, 512:1536], stage[:, 1536:1568]

        N_GATE, N_NORM, N_FAC, N_ROWS, N_CONV, N_DT, N_BC, N_TURN = 0, 1, 2, 3, 2, 7, 9, 11
        V_HOLD, V_GATE, V_XC, V_SP, V_SPLIT, V_DT = 3, 1, 6, 10, 10, 12

        def has_inner(kk):
            return kk is None or kk + 3 < NC

        def has_drive(kk):
            return kk is None or 0 <= kk + 2 < NC

        def has_steps(kk):
            return kk is None or 0 <= kk + 1 < NC

        def has_output(kk):
            return kk is None or 0 <= kk < NC

        def has_finish(kk):
            return kk is None or kk >= 1

        def turns(eng, body):
            in_pairs(eng, NC + 1, -3, body, loop_from=2, tail=4)

        block = ctx.enter_context(nc.Block())

        @block.sync
        def _(sp):
            loads = [(w_in, "w_in"), (taps, "taps"), (a_log, "a_log"), (dt_w[:], "dt_w"), (bc_w[:], "bc_w"),
                     (out_w[:], "out_w"), (pick[:], "pick"), (ident[:], "ident"), (ident_b[:], "ident_b"),
                     (cols[:, 0:2], "conv_b"), (cols[:, 2:4], "b_dt"), (cols[:, 4:6], "d_param"),
                     (cols[:, 6:7], "residual"), (cols[:, 7:8], "norm_w"), (ones[:], "ones")]
            assert len(loads) == NW
            for dst, src in loads:
                sp.dma_start(dst, io[src]).then_inc(w_load, 16)
            xg_st.give(sp)
            c_st.give(sp)
            tok_st.give(sp)

            def wait(c, value):
                sp.wait_ge(c.sem, value)
                sp.sem_inc(spare, 1)

            def load_x(kn):
                sp.dma_start(xr[:], scratch["xrT"][:, bass.ds(kn * ST, HALO + ST)]).then_inc(xr_ld.sem, 16)

            def body(k, p, kk):
                k1, k3 = k + 1, k + 3
                stored = k + 2 if kk is None else min(kk + 2, NC - 1)
                if kk == -3:
                    load_x(0)
                if has_steps(kk):
                    wait(c_st, c_st.at(stored))
                    if has_output(kk):
                        wait(c_ok, c_ok.at(k))
                    sp.dma_start(cT[:, 1 - p], scratch["cT"][bass.ds(k1 * 96, 96), :]).then_inc(cT_ld.sem, 16)
                if has_output(kk):
                    wait(xg_st, xg_st.at(stored))
                    wait(o_ok, o_ok.at(k, 0))
                    sp.dma_start(zg[:].rearrange("p a b -> p (a b)"),
                                 scratch["xg"][bass.ds(k * P, P), :]).then_inc(zg_ld.sem, 16)
                    wait(o_tp, o_tp.at(k, 0))
                    sp.dma_start(xn[:], scratch["xnT"][:, bass.ds(k * ST, ST)]).then_inc(xn_ld.sem, 16)
                    sp.dma_start(g[:], scratch["gT"][:, bass.ds(k * ST, ST)]).then_inc(xn_ld.sem, 16)
                if has_finish(kk):
                    wait(tok_ok, tok_ok.at(k - 1))
                    for q in range(3):
                        n = min(P, ST - q * P)
                        sp.dma_start(scratch["sg"][bass.ds((k - 1) * ST + q * P, n), :],
                                     tok[0:n, q]).then_inc(tok_st.sem, 16)
                if has_inner(kk):
                    if kk is None or kk + 4 < NC:
                        wait(f_conv, f_conv.at(k3))
                        load_x(k + 4)
                    wait(xc_ok, xc_ok.at(k3))
                    sp.dma_start(scratch["xg"][bass.ds(k3 * P, P), :],
                                 xg[:].rearrange("p a b -> p (a b)")).then_inc(xg_st.sem, 16)
                    wait(bcT_ok, bcT_ok.at(k3))
                    sp.dma_start(scratch["cT"][bass.ds(k3 * 96, 96), :],
                                 bcT[:, 1 - p, 1]).then_inc(c_st.sem, 16)

            turns(sp, body)
            wait(tok_st, tok_st.at(NC - 1, 3))

        @block.gpsimd
        def _(pool):
            pool.memset(cst[:, 0:1], 0.5).then_inc(consts, 1)
            pool.memset(cst[:, 1:2], -1.0).then_inc(consts, 1)
            pool.wait_ge(consts, 6)

            def body(k, p, kk):
                if not has_steps(kk):
                    return
                k1, q = k + 1, 1 - p
                step = [0]

                def link(ins):
                    step[0] += 1
                    ins.then_inc(pch.sem, 1)
                    pool.wait_ge(pch.sem, pch.at(k1, step[0]))
                    if step[0] in (5, 7):
                        pool.sem_inc(spare, 1)

                def at(buf, par, s):
                    return buf[:, par, 0:JP, s * B:(s + 1) * B]

                pool.wait_ge(dA_ok.sem, dA_ok.at(k1, 4))
                pool.wait_ge(b_rd.sem, b_rd.at(k1, NS))
                for js in (slice(JH, JP), slice(0, JH)):
                    a, now = dA[:, q, js, 0:B], h[:, q, js, 0:B]
                    link(pool.tensor_tensor(a, a, h[:, 1 - q, js, (STEPS - 1) * B:], ALU.mult))
                    link(pool.tensor_tensor(now, now, a, ALU.add))
                    pool.sem_inc(st0_ok.sem, 1)
                pool.wait_ge(n2_ok.sem, n2_ok.at(k1))
                link(pool.tensor_tensor(n2[:, 1:2], n2[:, 0:1], cst[:, 0:1], ALU.pow))
                link(pool.tensor_scalar(n2[:, 2:3], n2[:, 1:2], 1e-8, None, ALU.add))
                link(pool.tensor_tensor(n2[:, 1:2], n2[:, 2:3], cst[:, 1:2], ALU.pow))
                link(pool.tensor_scalar(n2[:, 3:4], n2[:, 1:2], 20.0, 1.0, ALU.mult, ALU.min))
                pool.sem_inc(n_fac.sem, 1)
                pool.wait_ge(fac_ok.sem, fac_ok.at(k1))
                link(pool.tensor_tensor(at(h, q, 0), at(h, q, 0), fac[:].unsqueeze(1).broadcast_to([P, JP, B]),
                                        ALU.mult))
                for s in range(1, STEPS):
                    link(pool.tensor_tensor(at(dA, q, s), at(dA, q, s), at(h, q, s - 1), ALU.mult))
                    link(pool.tensor_tensor(at(h, q, s), at(h, q, s), at(dA, q, s), ALU.add))
                pool.sem_inc(h_ok.sem, 1)
                assert step[0] == PCH, step[0]

            turns(pool, body)

        @block.tensor
        def _(pe):
            f_t.give(pe)
            prod_rd.give(pe)
            o_ok.give(pe)
            o_tp.give(pe)
            pe.wait_ge(w_load, 16 * NW)
            pe.wait_ge(consts, 6)
            pe.wait_ge(setup, 5)

            def spread(bank, rows, n):
                return pe.matmul(X[:, bank, 0:ST], pick[:, n:n + 1].broadcast_to([96, P]), rows,
                                 start=True, stop=True)

            def spread_c(k, p, n, after):
                if n == 0:
                    pe.wait_ge(cT_ld.sem, cT_ld.at(k))
                if n >= 2:
                    pe.wait_ge(prod_ok.sem, prod_ok.at(k, n - 1))
                elif after:
                    pe.wait_ge(prod_ok.sem, prod_ok.at(k - 1, NS + n - 1))
                spread(n % 2, cT[:, p], n).then_inc(c_ok.sem, 1)

            def spread_b(k, p, n, after):
                if n == 0:
                    pe.wait_ge(bcT_ok.sem, bcT_ok.at(k))
                    if after:
                        pe.wait_ge(b_rd.sem, b_rd.at(k - 1, NS))
                else:
                    pe.wait_ge(b_rd.sem, b_rd.at(k, n))
                spread(2, bcT[:, p, 0], n).then_inc(b_ok.sem, 1)

            def body(k, p, kk):
                k1, k2, k3 = k + 1, k + 2, k + 3

                def gate():
                    pe.wait_ge(xr_ld.sem, xr_ld.at(k3))
                    if kk is None or kk > -3:
                        pe.wait_ge(bcT_ok.sem, bcT_ok.at(k2))
                    for c in range(2):
                        mm = pe.matmul(F[:, c, 0:ST], gate_w[:, c * P:(c + 1) * P], xr[:, HALO:HALO + ST],
                                       start=True, stop=True)
                    mm.then_inc(f_gate.sem, 1)

                def conv(part):
                    if part == 0:
                        pe.wait_ge(gs_ok.sem, gs_ok.at(k3))
                    c = part // 2
                    for t in range(2 * (part % 2), 2 * (part % 2) + 2):
                        mm = pe.matmul(F[:, c, 0:ST], conv_w[:, t, c * P:(c + 1) * P],
                                       xr[:, t * B:t * B + ST], start=(t == 0), stop=(t == 3))
                    if part == 3:
                        mm.then_inc(f_conv.sem, 1)

                def step_width(c):
                    if c == 0:
                        pe.wait_ge(xc_ok.sem, xc_ok.at(k3))
                    for i in range(2):
                        mm = pe.matmul(F[:, c, 0:ST], dt_w[:, i, c * P:(c + 1) * P], xg[:, i],
                                       start=(i == 0), stop=(i == 1))
                    if c == 1:
                        mm.then_inc(f_dt.sem, 1)

                def b_c():
                    pe.wait_ge(v_ok.sem, v_ok.at(k3))
                    for q in range(NQ):
                        for i in range(2):
                            mm = pe.matmul(F[0:64, 0, q * 32:(q + 1) * 32], xg[:, i, q * 64:(q + 1) * 64],
                                           bc_w[:, i], start=(i == 0), stop=(i == 1))
                    mm.then_inc(f_bc.sem, 1)

                def turn_b_c():
                    pe.wait_ge(s3_ok.sem, s3_ok.at(k3))
                    pe.sem_inc(spare, 1)
                    for q in range(NQ):
                        for bc in range(2):
                            mm = pe.transpose(Fb[0:96, bc * ST + q * 64:bc * ST + (q + 1) * 64], s3[:, q, bc],
                                              ident_b[:])
                    mm.then_inc(f_t.sem, 1)

                def norms():
                    for i in range(2):
                        pe.wait_ge(nr_ok.sem, nr_ok.at(k1, i + 1))
                        mm = pe.matmul(E[0:B, 0:1], nrm[:, i], ones[:, 0:1], start=(i == 0), stop=(i == 1))
                    mm.then_inc(n2_ps.sem, 1)

                def factors():
                    pe.wait_ge(n_fac.sem, n_fac.at(k1))
                    pe.matmul(E[:, 0:B], n2[:, 3:4].broadcast_to([B, P]), ident[0:B, 0:B], start=True,
                              stop=True).then_inc(fac_ps.sem, 1)

                def token_rows():
                    pe.wait_ge(sg_ok.sem, sg_ok.at(k - 1))
                    if has_steps(kk):
                        pe.wait_ge(fac_ok.sem, fac_ok.at(k1))
                    for q in range(3):
                        n = min(P, ST - q * P)
                        mm = pe.transpose(E[0:n, q * P:(q + 1) * P], xn[:, q * P:q * P + n], ident[:])
                    mm.then_inc(o_tp.sem, 1)

                for n in range(NS):
                    if has_output(kk):
                        if n < NS - 1:
                            spread_c(k, p, n + 1, kk is None or kk >= 1)
                        pe.wait_ge(prod_ok.sem, prod_ok.at(k, n + 1))
                        for c in range(2):
                            mm = pe.matmul(Y[:, c, 0:ST], ident[:], prod[:, n % 2, c], start=(n == 0),
                                           stop=(n == NS - 1))
                        mm.then_inc(prod_rd.sem, 1)
                    if has_drive(kk) and n > 0:
                        spread_b(k2, p, n, False)
                    if has_steps(kk) and n == N_NORM:
                        norms()
                    if has_steps(kk) and n == N_FAC:
                        factors()
                    if has_finish(kk) and n == N_ROWS:
                        token_rows()
                    if has_inner(kk):
                        if n == N_GATE:
                            gate()
                        if N_CONV <= n < N_CONV + 4:
                            conv(n - N_CONV)
                        if N_DT <= n < N_DT + 2:
                            step_width(n - N_DT)
                        if n == N_BC:
                            b_c()
                        if n == N_TURN:
                            turn_b_c()
                if kk is None or 0 <= kk + 1 < NC:
                    spread_c(k1, 1 - p, 0, kk is None or kk >= 0)
                if kk is None or 0 <= kk + 3 < NC:
                    spread_b(k3, 1 - p, 0, kk is None or kk > -3)
                if has_output(kk):
                    if kk is None or kk >= 1:
                        pe.wait_ge(tok_ok.sem, tok_ok.at(k - 1))
                    pe.wait_ge(yy_ok.sem, yy_ok.at(k))
                    for i in range(2):
                        mm = pe.matmul(E[:, 0:ST], out_w[:, i], zg[:, i], start=(i == 0), stop=(i == 1))
                    mm.then_inc(o_ok.sem, 1)

            turns(pe, body)

        @block.scalar
        def _(act):
            act.wait_ge(w_load, 16 * NW)
            act.activation(a16[:], a_log, ACT.Tanh, scale=0.5 / (5.0 + 1e-8)).then_inc(aset, 1)
            act.activation(col2[:, 3:4], cols[:, 6:7], ACT.Tanh, scale=0.5).then_inc(aset, 1)
            act.wait_ge(aset, 2)
            act.activation(a16[:], a16[:], ACT.Exp, scale=10.0).then_inc(aset, 1)
            act.wait_ge(setup, 5)
            act.wait_ge(consts, 6)

            def body(k, p, kk):
                k1, k2, k3 = k + 1, k + 2, k + 3

                def decay_tanh(first, n):
                    if not has_drive(kk):
                        return
                    if first == 0:
                        act.wait_ge(dt_ok.sem, dt_ok.at(k2))
                        if has_output(kk):
                            act.wait_ge(h_ok.sem, h_ok.at(k))
                            act.wait_ge(vst.sem, vst.at(k, VST))
                    for j in range(first, first + n):
                        act.activation(dA[:, p, j], dt[:, p, j // NS], ACT.Tanh,
                                       scale=a16[:, j:j + 1]).then_inc(a_th.sem, 1)

                def decay_exp(i):
                    if not has_drive(kk):
                        return
                    act.wait_ge(a_th.sem, a_th.at(k2, 8 * i + 8))
                    act.activation(dA[:, p, 8 * i:8 * i + 8], dA[:, p, 8 * i:8 * i + 8], ACT.Exp,
                                   scale=16.0).then_inc(dA_ok.sem, 1)

                if has_steps(kk):
                    act.wait_ge(vst.sem, vst.at(k1, 2))
                    for i, js in enumerate((slice(JH, 2 * NS), slice(0, JH))):
                        act.wait_ge(st0_ok.sem, st0_ok.at(k1, i + 1))
                        act.activation(dA[:, 1 - p, js, 0:B], h[:, 1 - p, js, 0:B], ACT.Square).then_inc(sq_ok.sem, 1)
                decay_tanh(0, 4)
                if has_steps(kk):
                    act.wait_ge(n2_ps.sem, n2_ps.at(k1))
                    act.activation(n2[:, 0:1], E[0:B, 0:1], ACT.Copy).then_inc(n2_ok.sem, 1)
                if has_inner(kk):
                    act.wait_ge(f_gate.sem, f_gate.at(k3))
                    act.wait_ge(gs_ok.sem, gs_ok.at(k3, 0))
                    act.activation(tg[:], F[:, :, 0:ST], ACT.Tanh, scale=0.5).then_inc(a_gate.sem, 1)
                decay_tanh(4, 2)
                if has_steps(kk):
                    act.wait_ge(fac_ps.sem, fac_ps.at(k1))
                    act.activation(fac[:], E[:, 0:B], ACT.Copy).then_inc(fac_ok.sem, 1)
                decay_tanh(6, 6)
                if has_finish(kk):
                    act.wait_ge(o_tp.sem, o_tp.at(k - 1))
                    act.wait_ge(tok_st.sem, tok_st.at(k - 1, 0))
                    act.activation(tok[:, 0:2], E[:, 0:2 * D], ACT.Copy)
                    act.activation(tok[0:64, 2], E[0:64, 2 * D:3 * D], ACT.Copy).then_inc(tok_ok.sem, 1)
                decay_tanh(12, 4)
                decay_exp(0)
                if has_inner(kk):
                    act.wait_ge(f_conv.sem, f_conv.at(k3))
                    if kk is None or kk > -3:
                        act.wait_ge(dt_ok.sem, dt_ok.at(k2))
                    for c in range(2):
                        act.activation(th[:, c], F[:, c, 0:ST], ACT.Tanh, bias=col2[:, c:c + 1], scale=0.5)
                    act.activation(z[:, 0], F[:, 0, 0:ST], ACT.Identity, bias=col2[:, 0:1], scale=0.5)
                    act.activation(z[:, 1], F[:, 1, 0:ST], ACT.Identity, bias=col2[:, 1:2],
                                   scale=0.5).then_inc(a_conv.sem, 1)
                decay_tanh(16, 8)
                decay_exp(1)
                if has_inner(kk):
                    act.wait_ge(f_dt.sem, f_dt.at(k3))
                    act.activation(z[:, 0], F[:, 0, 0:ST], ACT.Identity, bias=cols[:, 2:3])
                    act.activation(z[:, 1], F[:, 1, 0:ST], ACT.Identity, bias=cols[:, 3:4]).then_inc(v_ok.sem, 1)
                    act.wait_ge(v_ok.sem, v_ok.at(k3))
                    act.activation(th[:], z[:], ACT.Abs).then_inc(a_exp.sem, 1)
                    act.wait_ge(a_exp.sem, a_exp.at(k3, 1))
                    act.activation(th[:], th[:], ACT.Exp, scale=-1.0).then_inc(a_exp.sem, 1)
                    act.wait_ge(a_exp.sem, a_exp.at(k3, 2))
                    act.activation(th[:], th[:], ACT.Ln, bias=1.0).then_inc(a_ln.sem, 1)
                decay_tanh(24, 8)
                if has_inner(kk):
                    act.wait_ge(sp_ok.sem, sp_ok.at(k3))
                    act.activation(th[:], z[:], ACT.Tanh, bias=col2[:, 2:3], scale=A_DT).then_inc(a_dt.sem, 1)
                    act.wait_ge(a_dt.sem, a_dt.at(k3, 1))
                    act.activation(dt[:, 1 - p], th[:], ACT.Identity, bias=col2[:, 4:5],
                                   scale=2 * R_DT).then_inc(a_dt.sem, 1)
                decay_exp(2)
                if has_inner(kk):
                    act.wait_ge(f_t.sem, f_t.at(k3))
                    if kk is None or kk + 1 >= 0:
                        act.wait_ge(b_ok.sem, b_ok.at(k1, NS))
                        act.wait_ge(c_st.sem, c_st.at(k2))
                    act.activation(bcT[:, 1 - p].rearrange("p a b -> p (a b)"), Fb[0:96, 0:2 * ST],
                                   ACT.Copy).then_inc(bcT_ok.sem, 1)
                decay_exp(3)

            turns(act, body)

        @block.vector
        def _(v):
            gs_ok.give(v)
            v.memset(s3[:], 0.0).then_inc(consts, 1)
            v.memset(h[:, 1, :, (STEPS - 1) * B:], 0.0).then_inc(consts, 1)
            v.memset(col2[:, 2:3], -C_DT * A_DT).then_inc(consts, 1)
            v.memset(col2[:, 4:5], C_DT).then_inc(consts, 1)
            v.wait_ge(w_load, 16 * NW)
            v.tensor_scalar(col2[:, 0:2], cols[:, 0:2], 0.5, None, ALU.mult).then_inc(setup, 1)
            v.tensor_scalar(w_in, w_in, cols[:, 7:8], None, ALU.mult).then_inc(vset, 1)
            v.wait_ge(vset, 1)
            v.tensor_tensor(conv_w[:], taps.rearrange("p (t c) -> p t c", t=4),
                            w_in[:, 0:DI].unsqueeze(1).broadcast_to([P, 4, DI]), ALU.mult).then_inc(setup, 1)
            v.tensor_copy(gate_w[:], w_in[:, DI:2 * DI]).then_inc(setup, 1)
            v.wait_ge(aset, 3)
            v.tensor_scalar(a16[:], a16[:], -1.0 / 16, None, ALU.mult).then_inc(setup, 1)
            v.tensor_scalar(col2[:, 3:4], col2[:, 3:4], 0.125, 0.125, ALU.mult, ALU.add).then_inc(setup, 1)
            v.wait_ge(setup, 5)
            v.wait_ge(consts, 6)

            def body(k, p, kk):
                k1, k2, k3, q = k + 1, k + 2, k + 3, 1 - p
                step = [0]

                def link(ins):
                    step[0] += 1
                    ins.then_inc(vch.sem, 1)
                    v.wait_ge(vch.sem, vch.at(k3, step[0]))

                def advance(s, half):
                    a, now = dA[:, q, JP:, s * B:(s + 1) * B], h[:, q, JP:, s * B:(s + 1) * B]
                    n = 2 * s + (s > 0) + half
                    if n or kk is None or kk >= 0:
                        v.wait_ge(vst.sem, vst.at(k1, n))
                    if half:
                        ins = v.tensor_tensor(now, now, a, ALU.add)
                    else:
                        before = h[:, q, JP:, (s - 1) * B:s * B] if s else h[:, p, JP:, (STEPS - 1) * B:]
                        ins = v.tensor_tensor(a, a, before, ALU.mult)
                    ins.then_inc(vst.sem, 1)

                halves = iter([(s, half) for s in range(1, STEPS) for half in range(2)])

                def next_halves(n):
                    for _ in range(n if has_steps(kk) else 0):
                        s = next(halves, None)
                        if s:
                            advance(*s)

                def product(n):
                    if not has_output(kk):
                        return
                    v.wait_ge(c_ok.sem, c_ok.at(k, n + 1))
                    if n == 0:
                        v.wait_ge(h_ok.sem, h_ok.at(k))
                        v.wait_ge(vst.sem, vst.at(k, VST))
                    v.wait_ge(prod_rd.sem, prod_rd.at(k, n - 1))
                    v.tensor_tensor(prod[:, n % 2], h[:, p].rearrange("p (c n) t -> p c n t", c=2)[:, :, n],
                                    X[:, n % 2, 0:ST].unsqueeze(1).broadcast_to([P, 2, ST]),
                                    ALU.mult).then_inc(prod_ok.sem, 1)

                def drive(n):
                    if not has_drive(kk):
                        return
                    if n == 0:
                        v.wait_ge(dt_ok.sem, dt_ok.at(k2))
                    v.wait_ge(b_ok.sem, b_ok.at(k2, n + 1))
                    if n == 0 and has_steps(kk):
                        v.wait_ge(st0_ok.sem, st0_ok.at(k1, 2))
                    if has_output(kk):
                        v.wait_ge(prod_ok.sem, prod_ok.at(k, n + 1))
                    v.tensor_tensor(h[:, p].rearrange("p (c n) t -> p c n t", c=2)[:, :, n], dtx[:, p],
                                    X[:, 2, 0:ST].unsqueeze(1).broadcast_to([P, 2, ST]),
                                    ALU.mult).then_inc(b_rd.sem, 1)

                if has_steps(kk):
                    v.wait_ge(dA_ok.sem, dA_ok.at(k1, 4))
                    advance(0, 0)
                    advance(0, 1)
                product(0)
                for n in range(NS):
                    if n == 0 and has_finish(kk):
                        v.wait_ge(o_ok.sem, o_ok.at(k - 1))
                        v.wait_ge(xn_ld.sem, xn_ld.at(k - 1, 2))
                        link(v.scalar_tensor_tensor(xn[:], E[:, 0:ST], col2[:, 3:4], xn[:], ALU.mult, ALU.add))
                        v.tensor_tensor(xn[:], xn[:], g[:], ALU.mult).then_inc(sg_ok.sem, 1)
                    if n < NS - 1:
                        product(n + 1)
                    if has_steps(kk) and n == 0:
                        for i, js in enumerate((slice(JH, 2 * NS), slice(0, JH))):
                            v.wait_ge(sq_ok.sem, sq_ok.at(k1, i + 1))
                            v.tensor_reduce(nrm[:, i], dA[:, q, js, 0:B].rearrange("p j b -> p b j"), AX.X,
                                            ALU.add).then_inc(nr_ok.sem, 1)
                    drive(n)
                    if has_steps(kk) and n == V_HOLD:
                        v.wait_ge(fac_ok.sem, fac_ok.at(k1))
                        v.tensor_tensor(h[:, q, JP:, 0:B], h[:, q, JP:, 0:B], fac[:].unsqueeze(1).broadcast_to(
                            [P, 2 * NS - JP, B]), ALU.mult).then_inc(vst.sem, 1)
                    if n > V_HOLD:
                        next_halves(1 + (n % 2 or n > NS - 4))
                    if has_inner(kk):
                        if n == V_GATE:
                            v.wait_ge(a_gate.sem, a_gate.at(k3))
                            v.wait_ge(xg_st.sem, xg_st.at(k3, 0))
                            v.scalar_tensor_tensor(xg[:, 2:4], tg[:], 1.0, F[:, :, 0:ST], ALU.add,
                                                   ALU.mult).then_inc(gs_ok.sem, 1)
                        if n == V_XC:
                            v.wait_ge(a_conv.sem, a_conv.at(k3))
                            v.scalar_tensor_tensor(xg[:, 0:2], th[:], 1.0, z[:], ALU.add,
                                                   ALU.mult).then_inc(xc_ok.sem, 1)
                        if n == V_SP:
                            v.wait_ge(a_ln.sem, a_ln.at(k3))
                            v.scalar_tensor_tensor(z[:], z[:], 0.0, th[:], ALU.max, ALU.add).then_inc(sp_ok.sem, 1)
                        if n == V_DT:
                            v.wait_ge(a_dt.sem, a_dt.at(k3, 2))
                            v.tensor_tensor(dtx[:, q], dt[:, q], xg[:, 0:2], ALU.mult).then_inc(dt_ok.sem, 1)
                        if n == V_SPLIT:
                            src = F[0:64, 0, 0:NQ * 2 * NS].rearrange("p (q c n) -> p q c n", q=NQ, c=2)
                            v.wait_ge(f_bc.sem, f_bc.at(k3))
                            v.wait_ge(f_t.sem, f_t.at(k3, 0))
                            link(v.tensor_copy(s3[:, :, :, 0:NS], src))
                            link(v.tensor_tensor(rest[:], src, s3[:, :, :, 0:NS], ALU.subtract))
                            link(v.tensor_copy(s3[:, :, :, 32:32 + NS], rest[:]))
                            link(v.tensor_tensor(rest[:], rest[:], s3[:, :, :, 32:32 + NS], ALU.subtract))
                            v.tensor_copy(s3[:, :, :, 64:64 + NS], rest[:]).then_inc(s3_ok.sem, 1)
                next_halves(2 * STEPS)
                if has_output(kk):
                    v.wait_ge(zg_ld.sem, zg_ld.at(k))
                    v.wait_ge(prod_rd.sem, prod_rd.at(k, NS))
                    link(v.scalar_tensor_tensor(zg[:, 0], zg[:, 0], cols[:, 4:5], Y[:, 0, 0:ST], ALU.mult, ALU.add))
                    link(v.scalar_tensor_tensor(zg[:, 1], zg[:, 1], cols[:, 5:6], Y[:, 1, 0:ST], ALU.mult, ALU.add))
                    v.tensor_tensor(zg[:, 0:2], zg[:, 0:2], zg[:, 2:4], ALU.mult).then_inc(yy_ok.sem, 1)
                for _ in range(7 - step[0]):
                    v.sem_inc(vch.sem, 1)

            turns(v, body)


def attention_phase(nc, io, scratch, out):
    SC = float(np.float32(1.0) / np.sqrt(np.float32(8.0)))
    CH = 32
    HC = 8
    HT = HC * CH
    G = 4
    with ExitStack() as ctx:
        def sb(name, shape, dt=F32):
            return ctx.enter_context(nc.sbuf_tensor("a_" + name, shape, dt))

        def ps(name, shape, dt=F32):
            return ctx.enter_context(nc.psum_tensor("a_" + name, shape, dt))

        def cnt(name, per, credit=0, by=1):
            return Count(ctx, nc, "a_" + name, per, credit, by)

        def sem(name):
            return ctx.enter_context(nc.semaphore("a_" + name))

        w = sb("w", [P, 8, D])
        wt = sb("wt", [P, D])
        tern = sb("tern", [P, 4])
        ident = sb("ident", [P, P])
        ones = sb("ones", [P, P])
        jmask = sb("jmask", [P, 4])
        vmask = sb("vmask", [P, 4])
        osum = sb("osum", [P, CH])
        bmask = sb("bmask", [P, CH])
        mhalf = sb("mhalf", [P, MQ])
        x_in = sb("x_in", [P, 2, MQ, D])
        sg_in = sb("sg_in", [P, 2, MQ, D])
        x1 = sb("x1", [P, T // P, D])
        xn = sb("xn", [P, MQ, D])
        stats = sb("stats", [P, MQ, 6])
        mv = sb("mv", [P, MQ, 2])
        rstd = sb("rstd", [P, 2, MQ])
        xnT = sb("xnT", [P, T])
        qm = sb("qm", [P, 2 * HC, 4, CH])
        km = sb("km", [P, 2 * HC, G, CH])
        x4 = sb("x4", [P, 2 * HC, 4, CH])
        vb = sb("vb", [P, 2, HC * G, CH])
        mx = sb("mx", [P, G * HC])
        e = sb("e", [P, 2, HC, G, CH])
        eT = sb("eT", [P, 2, HC, G, CH])
        rden = sb("rden", [P, HT])
        ctxT = sb("ctxT", [P, 2, HT])
        ch = sb("ch", [P, T])
        sl = sb("sl", [P, 2, MT])
        gated = sb("gated", [P, 2, MT])
        o_out = sb("o_out", [P, 2, MQ, D])
        means = sb("means", [P, B * HC])
        gT = sb("gT", [P, B * HC])

        S = ps("S", [P, 2, HC, G * CH])
        V = ps("V", [P, HC, D])
        Vq, Vk = (V[:, 4 * i:4 * i + 4].rearrange("p c d -> p (c d)") for i in range(2))
        SL, RT = (S[:, i].rearrange("p (a b) d -> p a (b d)", a=2) for i in range(2))
        C = ps("C", [P, 2, HT])
        TB = ps("TB", [P, MT])

        w_load, power_ok, consts, wsum, wchain, spare = (
            sem(n) for n in ("w_load", "power_ok", "consts", "wsum", "wchain", "spare"))
        x_ld = Alternate(ctx, nc, "a_x_ld", 3)
        x_rd = cnt("x_rd", 1, 2)
        x1_ok = cnt("x1_ok", 1)
        moments = cnt("moments", 1)
        rstd_ok = cnt("rstd_ok", 1)
        pchain = cnt("pchain", 1)
        xn_ok = cnt("xn_ok", 1)
        tp = cnt("tp", 1, 1)
        xnT_ok = cnt("xnT_ok", 1)
        x4_ok = cnt("x4_ok", 1)
        q_ps = cnt("q_ps", 1)
        qm_ok = cnt("qm_ok", 1)
        k_ps = cnt("k_ps", 1)
        km_ok = cnt("km_ok", 1)
        v_ps = cnt("v_ps", 2)
        vb_ok = cnt("vb_ok", 2)
        s_ps = cnt("s_ps", 2)
        mx_ok = cnt("mx_ok", 2)
        sub_ok = cnt("sub_ok", 2, 2)
        ex_ok = cnt("ex_ok", 2)
        eT_ok = cnt("eT_ok", 2)
        av_ps = cnt("av_ps", 2, 2)
        rd_ok = cnt("rd_ok", 2)
        ctx_ok = cnt("ctx_ok", 2, 1)
        o_ps = cnt("o_ps", 2)
        ch_ok = cnt("ch_ok", 2, 1)
        sum_ok = sem("sum_ok")
        dch = cnt("dch", 1)
        means_ok, g_ok = sem("means_ok"), sem("g_ok")
        f_ps = cnt("f_ps", 1)
        f_sl = cnt("f_sl", 1)
        f_en = cnt("f_en", 1)
        f_pr = cnt("f_pr", 1, 1)
        f_tp = cnt("f_tp", 1, 2)
        f_out = cnt("f_out", 1, 2)
        f_st = Alternate(ctx, nc, "a_f_st", 1, 16)

        loads = [(w[:], "attn_w"), (wt[:], "tern_w"), (ident[:], "ident"), (ones[:], "ones"), (jmask[:], "jmask"),
                 (vmask[:], "vmask"), (osum[:], "osum"), (bmask[:], "bmask")]
        NW = len(loads)
        x_bt = io["x_bt"]
        sg_bt = scratch["sg"].rearrange("(t b) d -> b t d", b=B)

        def half_of(buf, k, hf):
            return buf[:, bass.ds(k * MT + hf * HT, HT)]

        def chunk_of(buf, k):
            return buf[:, bass.ds(k * MT, MT)]

        def tile_of(k, q, n=1):
            return x1[:, bass.ds(k * MQ + q, n)]

        def has_sum(kk):
            return kk is None or kk + 2 < MCH

        def has_front(kk):
            return kk is None or 0 <= kk + 1 < MCH

        def has_main(kk):
            return kk is None or kk >= 0

        block = ctx.enter_context(nc.Block())

        @block.sync
        def _(sp):
            f_st.give(sp)

            def wait(c, value):
                sp.wait_ge(c.sem, value)
                sp.sem_inc(spare, 1)

            def load(k, p):
                sp.dma_start(x_in[:, p], x_bt[bass.ds(k * MT, MT), :].rearrange(
                    "(q p) d -> p q d", p=P)).then_inc(x_ld.sems[p], 16)
                for b in range(2):
                    sp.dma_start(sg_in[:, p, 2 * b:2 * b + 2], sg_bt[bass.ds(k * 2 + b, 1), 0:L, :].rearrange(
                        "o (q p) d -> p (o q) d", p=P)).then_inc(x_ld.sems[p], 16)

            load(0, 0)
            for dst, src in loads:
                sp.dma_start(dst, io[src]).then_inc(w_load, 16)

            def body(k, p, kk):
                if kk is None or kk + 3 < MCH:
                    wait(x_rd, x_rd.at(k + 3, -1))
                    load(k + 3, 1 - p)

            in_pairs(sp, MCH, -2, body, tail=3)

            def last(k, p, kk):
                wait(f_out, f_out.at(k))
                sp.dma_start(out[bass.ds(k * MT, MT), :].rearrange("(q p) d -> p q d", p=P),
                             o_out[:, p]).then_inc(f_st.sems[p], 16)

            in_pairs(sp, MCH, 0, last)
            for p in range(2):
                sp.wait_ge(f_st.sems[p], f_st.at(MCH - 2 + p, p))

        @block.gpsimd
        def _(pool):
            pool.memset(mhalf[:], -0.5).then_inc(power_ok, 1)
            pool.memset(km[:], 0.0).then_inc(power_ok, 1)
            pool.wait_ge(power_ok, 2)
            x_rd.give(pool)

            def body(k, p, kk):
                k1, k2 = k + 1, k + 2
                if has_sum(kk):
                    pool.wait_ge(x_ld.sems[p], x_ld.at(k2, p, 3))
                    pool.tensor_tensor(tile_of(k2, 0, MQ), x_in[:, p], sg_in[:, p], ALU.add).then_inc(x1_ok.sem, 1)
                    pool.wait_ge(x1_ok.sem, x1_ok.at(k2))
                    pool.sem_inc(x_rd.sem, 1)
                if has_front(kk):
                    pool.wait_ge(xnT_ok.sem, xnT_ok.at(k1))
                    pool.sem_inc(spare, 1)
                    if has_main(kk):
                        pool.wait_ge(v_ps.sem, v_ps.at(k, 2))
                        pool.sem_inc(spare, 1)
                    pool.tensor_copy(x4[:], chunk_of(xnT, k1).rearrange("p (c q) -> p c q", q=CH).unsqueeze(
                        2).broadcast_to([P, 2 * HC, 4, CH])).then_inc(x4_ok.sem, 1)
                if has_sum(kk):
                    pool.wait_ge(moments.sem, moments.at(k2))
                    if has_front(kk):
                        pool.wait_ge(xn_ok.sem, xn_ok.at(k1))
                    pool.sem_inc(spare, 1)
                    pool.tensor_scalar(rstd[:, 1], mv[:, :, 1], 1e-5, None, ALU.add).then_inc(pchain.sem, 1)
                    pool.wait_ge(pchain.sem, pchain.at(k2))
                    pool.tensor_tensor(rstd[:, 0], rstd[:, 1], mhalf[:], ALU.pow).then_inc(rstd_ok.sem, 1)

            in_pairs(pool, MCH, -2, body, tail=3)
            pool.wait_ge(means_ok, 1)
            pool.tensor_copy(x4[:, 0:HC], means[:].rearrange("p (c q) -> p c q", q=CH).unsqueeze(2).broadcast_to(
                [P, HC, 4, CH])).then_inc(x4_ok.sem, 1)

        @block.tensor
        def _(pe):
            tp.give(pe)
            av_ps.give(pe)
            f_tp.give(pe)
            pe.wait_ge(w_load, 16 * NW)

            def values_scores(k, hf, wv):
                if hf:
                    pe.wait_ge(vb_ok.sem, vb_ok.at(k, 1))
                pe.wait_ge(qm_ok.sem, qm_ok.at(k))
                pe.wait_ge(km_ok.sem, km_ok.at(k))
                pe.wait_ge(x4_ok.sem, x4_ok.at(k))
                for c in range(HC):
                    mm = pe.matmul(V[:, c], x4[:, hf * HC + c].rearrange("p j q -> p (j q)"), wv,
                                   start=True, stop=True)
                mm.then_inc(v_ps.sem, 1)
                pe.wait_ge(sub_ok.sem, sub_ok.at(k - 1, hf + 1))
                for c in range(HC):
                    mm = pe.matmul(S[:, hf, c], qm[:, hf * HC + c].rearrange("p j q -> p (j q)"),
                                   km[:, hf * HC + c].rearrange("p g q -> p (g q)"), start=True, stop=True)
                mm.then_inc(s_ps.sem, 1)

            def contexts(k, hf):
                pe.wait_ge(eT_ok.sem, eT_ok.at(k, hf + 1))
                pe.wait_ge(vb_ok.sem, vb_ok.at(k, hf + 1))
                pe.wait_ge(ctx_ok.sem, ctx_ok.at(k, hf))
                for g in range(G):
                    a = slice(32 * g, 32 * g + 32)
                    pe.matmul(C[a, 1].rearrange("p (c q) -> p c q", q=CH), osum[:], eT[:, hf, :, g], start=True,
                              stop=True)
                for c in range(HC):
                    for g in range(G):
                        a = slice(32 * g, 32 * g + 32)
                        mm = pe.matmul(C[a, 0, c * CH:(c + 1) * CH], vb[:, hf, c * G + g], eT[:, hf, c, g],
                                       start=True, stop=True)
                mm.then_inc(av_ps.sem, 1)

            def project(k, hf, wo):
                pe.wait_ge(ctx_ok.sem, ctx_ok.at(k, hf + 1))
                pe.matmul(TB[:, 0:HT], wo, ctxT[:, hf], start=True, stop=True).then_inc(o_ps.sem, 1)

            def body(k, p, kk):
                k1, n = k + 1, 1 - p
                if has_main(kk):
                    values_scores(k, 1, w[:, 2])
                if has_front(kk):
                    pe.wait_ge(xn_ok.sem, xn_ok.at(k1))
                    if has_main(kk):
                        pe.wait_ge(ch_ok.sem, ch_ok.at(k, 0))
                    for q in range(MQ):
                        mm = pe.transpose(TB[:, q * P:(q + 1) * P], xn[:, q], ident[:])
                    mm.then_inc(tp.sem, 1)
                if has_main(kk):
                    contexts(k, 0)
                if has_front(kk):
                    pe.wait_ge(xnT_ok.sem, xnT_ok.at(k1))
                    if has_main(kk):
                        pe.wait_ge(vb_ok.sem, vb_ok.at(k, 2))
                    pe.matmul(Vq, w[:, 0], chunk_of(xnT, k1), start=True, stop=True).then_inc(q_ps.sem, 1)
                    pe.matmul(Vk, w[:, 1], chunk_of(xnT, k1), start=True, stop=True).then_inc(k_ps.sem, 1)
                if has_main(kk):
                    if not has_front(kk):
                        pe.wait_ge(ch_ok.sem, ch_ok.at(k, 0))
                    project(k, 0, w[:, 3])
                    contexts(k, 1)
                if has_front(kk):
                    values_scores(k1, 0, w[:, 2])
                if has_main(kk):
                    pe.wait_ge(ch_ok.sem, ch_ok.at(k, 1))
                    project(k, 1, w[:, 3])

            in_pairs(pe, MCH, -2, body, tail=3)

            K = MCH
            pe.wait_ge(means_ok, 1)
            pe.matmul(Vq[:, 0:HT], w[:, 4], means[:], start=True, stop=True).then_inc(q_ps.sem, 1)
            pe.matmul(Vk[:, 0:HT], w[:, 5], means[:], start=True, stop=True).then_inc(k_ps.sem, 1)
            pe.wait_ge(consts, 1)
            pe.wait_ge(ctx_ok.sem, ctx_ok.at(K, 0))
            pe.matmul(C[:, 0, 0:1], ones[:], tern[:, 0:1], start=True, stop=True).then_inc(wsum, 1)
            values_scores(K, 0, w[:, 6])
            pe.wait_ge(consts, 2)
            contexts(K, 0)
            project(K, 0, w[:, 7])
            pe.wait_ge(g_ok, 1)

            def ternary(k, p):
                pe.matmul(SL[:, p], wt[:], chunk_of(xnT, k), start=True, stop=True).then_inc(f_ps.sem, 1)

            ternary(0, 0)

            def last(k, p, kk):
                if kk is None or kk + 1 < MCH:
                    pe.wait_ge(f_pr.sem, f_pr.at(k - 1))
                    ternary(k + 1, 1 - p)
                pe.wait_ge(f_pr.sem, f_pr.at(k))
                pe.wait_ge(f_out.sem, f_out.at(k - 2))
                for q in range(MQ):
                    mm = pe.transpose(RT[:, p, q * P:(q + 1) * P], gated[:, p, q * P:(q + 1) * P], ident[:])
                mm.then_inc(f_tp.sem, 1)

            in_pairs(pe, MCH, 0, last)

        @block.scalar
        def _(act):
            act.wait_ge(w_load, 16 * NW)
            act.wait_ge(power_ok, 2)

            def values(k, hf):
                act.wait_ge(v_ps.sem, v_ps.at(k, hf + 1))
                act.wait_ge(av_ps.sem, av_ps.at(k, hf - 1))
                for j in range(4):
                    ins = act.activation(vb[:, hf, :, 8 * j:8 * j + 8],
                                         V[:].rearrange("p c (g j e) -> p (c g) j e", g=G, j=4)[:, :, j],
                                         ACT.Copy, scale=vmask[:, j:j + 1])
                ins.then_inc(vb_ok.sem, 1)

            def exponentials(k, hf):
                act.wait_ge(sub_ok.sem, sub_ok.at(k, hf + 1))
                act.activation(e[:, hf], e[:, hf], ACT.Exp, scale=SC).then_inc(ex_ok.sem, 1)

            def queries_keys(k1, nc_):
                act.wait_ge(q_ps.sem, q_ps.at(k1))
                for j in range(4):
                    ins = act.activation(qm[:, 0:nc_, j], Vq[:, 0:nc_ * CH].rearrange("p (c q) -> p c q", q=CH),
                                         ACT.Copy, scale=jmask[:, j:j + 1])
                ins.then_inc(qm_ok.sem, 1)
                act.wait_ge(k_ps.sem, k_ps.at(k1))
                for g in range(G):
                    a = slice(32 * g, 32 * g + 32)
                    ins = act.activation(km[a, 0:nc_, g], Vk[a, 0:nc_ * CH].rearrange("p (c q) -> p c q", q=CH),
                                         ACT.Copy)
                ins.then_inc(km_ok.sem, 1)

            def body(k, p, kk):
                if has_main(kk):
                    exponentials(k, 0)
                    values(k, 1)
                if has_front(kk):
                    k1 = k + 1
                    act.wait_ge(tp.sem, tp.at(k1))
                    act.activation(chunk_of(xnT, k1), TB[:], ACT.Copy).then_inc(xnT_ok.sem, 1)
                if has_main(kk):
                    exponentials(k, 1)
                if has_front(kk):
                    queries_keys(k1, 2 * HC)
                    values(k1, 0)

            in_pairs(act, MCH, -2, body, tail=3)
            queries_keys(MCH, HC)
            values(MCH, 0)
            exponentials(MCH, 0)

            def last(k, p, kk):
                act.wait_ge(f_ps.sem, f_ps.at(k))
                act.activation(sl[:, p], SL[:, p], ACT.Silu).then_inc(f_sl.sem, 1)

            in_pairs(act, MCH, 0, last)

        @block.vector
        def _(v):
            for c in (sub_ok, ctx_ok, ch_ok, f_out, f_pr):
                c.give(v)

            def softmax_in(k, hf, masked=False):
                src = S[:, hf].rearrange("p c (g q) -> p c g q", q=CH)
                v.wait_ge(s_ps.sem, s_ps.at(k, hf + 1))
                if masked:
                    for g in range(G):
                        v.tensor_tensor(e[:, hf, :, g], src[:, :, g], bmask[:].unsqueeze(1).broadcast_to([P, HC, CH]),
                                        ALU.add).then_inc(wchain, 1)
                    v.wait_ge(wchain, 8)
                    src = e[:, hf]
                v.tensor_reduce(mx[:].rearrange("p (c g) -> p c g", g=G), src, AX.X, ALU.max).then_inc(mx_ok.sem, 1)
                v.wait_ge(mx_ok.sem, mx_ok.at(k, hf + 1))
                v.tensor_tensor(e[:, hf], src, mx[:].rearrange("p (c g) -> p c g", g=G).unsqueeze(3).broadcast_to(
                    [P, HC, G, CH]), ALU.subtract).then_inc(sub_ok.sem, 1)

            def turn(k, hf):
                v.wait_ge(ex_ok.sem, ex_ok.at(k, hf + 1))
                v.wait_ge(av_ps.sem, av_ps.at(k, hf - 1))
                v.transpose(eT[:, hf].rearrange("p c g q -> p (c g q)"),
                            e[:, hf].rearrange("p c g q -> p (c g q)")).then_inc(eT_ok.sem, 1)

            def normalise(k, hf):
                v.wait_ge(av_ps.sem, av_ps.at(k, hf + 1))
                v.reciprocal(rden[:], C[:, 1]).then_inc(rd_ok.sem, 1)
                v.wait_ge(rd_ok.sem, rd_ok.at(k, hf + 1))
                v.tensor_tensor(ctxT[:, hf], C[:, 0], rden[:], ALU.mult).then_inc(ctx_ok.sem, 1)

            def residual(k, p, hf):
                v.wait_ge(o_ps.sem, o_ps.at(k, hf + 1))
                v.tensor_tensor(half_of(ch, k, hf), TB[:, 0:HT], half_of(xnT, k, hf), ALU.add).then_inc(ch_ok.sem, 1)
                v.wait_ge(ch_ok.sem, ch_ok.at(k, hf + 1))
                v.sem_inc(spare, 1)
                v.tensor_reduce(means[:, bass.ds(k * (2 * HC) + hf * HC, HC)],
                                half_of(ch, k, hf).rearrange("p (c q) -> p c q", q=CH), AX.X,
                                ALU.add).then_inc(sum_ok, 1)

            def front_moments(k1):
                v.wait_ge(x1_ok.sem, x1_ok.at(k1))
                for q in range(MQ):
                    ins = v.bn_stats(stats[:, q], tile_of(k1, q).rearrange("p a d -> p (a d)"))
                ins.then_inc(dch.sem, 1)
                v.wait_ge(dch.sem, dch.at(k1, 1))
                v.sem_inc(spare, 1)
                for q in range(MQ):
                    ins = v.bn_aggr(mv[:, q], stats[:, q])
                ins.then_inc(moments.sem, 1)

            def front_norm(k1, n):
                v.wait_ge(rstd_ok.sem, rstd_ok.at(k1))
                v.wait_ge(tp.sem, tp.at(k1, 0))
                for q in range(MQ):
                    ins = v.tensor_scalar(xn[:, q], tile_of(k1, q).rearrange("p a d -> p (a d)"), mv[:, q, 0:1],
                                          rstd[:, 0, q:q + 1], ALU.subtract, ALU.mult)
                ins.then_inc(xn_ok.sem, 1)

            def body(k, p, kk):
                k1, n = k + 1, 1 - p
                if has_front(kk):
                    front_norm(k1, n)
                if has_main(kk):
                    turn(k, 0)
                    softmax_in(k, 1)
                    normalise(k, 0)
                    turn(k, 1)
                    residual(k, p, 0)
                    normalise(k, 1)
                if has_sum(kk):
                    front_moments(k + 2)
                if has_front(kk):
                    softmax_in(k1, 0)
                if has_main(kk):
                    residual(k, p, 1)

            in_pairs(v, MCH, -2, body, tail=3)
            K = MCH
            v.wait_ge(w_load, 16 * NW)
            v.tensor_reduce(tern[:, 0:1], wt[:], AX.X, ALU.add, apply_absolute_value=True).then_inc(consts, 1)
            v.wait_ge(sum_ok, 2 * MCH)
            v.tensor_scalar(means[:], means[:], 1.0 / CH, None, ALU.mult).then_inc(means_ok, 1)
            v.wait_ge(wsum, 1)
            v.tensor_scalar(tern[:, 1:2], C[:, 0, 0:1], 1.0 / (D * D), 1e-5, ALU.mult, ALU.max).then_inc(wchain, 1)
            v.wait_ge(wchain, 1)
            v.reciprocal(tern[:, 2:3], tern[:, 1:2]).then_inc(wchain, 1)
            v.wait_ge(wchain, 2)
            v.tensor_scalar(wt[:], wt[:], tern[:, 2:3], 1.0, ALU.mult, ALU.min).then_inc(wchain, 1)
            v.wait_ge(wchain, 3)
            v.tensor_scalar(wt[:], wt[:], -1.0, 12582912.0, ALU.max, ALU.add).then_inc(wchain, 1)
            v.wait_ge(wchain, 4)
            v.tensor_scalar(wt[:], wt[:], 12582912.0, tern[:, 1:2], ALU.subtract, ALU.mult).then_inc(consts, 1)
            softmax_in(K, 0, masked=True)
            turn(K, 0)
            normalise(K, 0)
            v.wait_ge(o_ps.sem, o_ps.at(K, 1))
            v.tensor_tensor(gT[:], TB[:, 0:HT], means[:], ALU.add).then_inc(g_ok, 1)
            v.wait_ge(g_ok, 1)

            def enhance(k):
                chp = chunk_of(ch, k).rearrange("p (c q) -> p c q", q=CH)
                v.tensor_tensor(chp, chp, gT[:, bass.ds(k * 2 * HC, 2 * HC)].unsqueeze(2).broadcast_to(
                    [P, 2 * HC, CH]), ALU.add).then_inc(f_en.sem, 1)

            def final(k, p):
                v.wait_ge(f_tp.sem, f_tp.at(k))
                v.wait_ge(f_st.sems[p], f_st.at(k, p, 0))
                v.tensor_tensor(o_out[:, p].rearrange("p q d -> p (q d)"), RT[:, p],
                                tile_of(k, 0, MQ).rearrange("p q d -> p (q d)"), ALU.add).then_inc(f_out.sem, 1)

            enhance(0)

            def last(k, p, kk):
                v.wait_ge(f_sl.sem, f_sl.at(k))
                v.wait_ge(f_en.sem, f_en.at(k))
                v.wait_ge(f_tp.sem, f_tp.at(k - 2))
                v.tensor_tensor(gated[:, p], chunk_of(ch, k), sl[:, p], ALU.mult).then_inc(f_pr.sem, 1)
                if kk is None or kk >= 1:
                    final(k - 1, 1 - p)
                if kk is None or kk + 1 < MCH:
                    enhance(k + 1)

            in_pairs(v, MCH, 0, last, loop_from=2)
            final(MCH - 1, (MCH - 1) % 2)


def host_arrays(i):
    c = np.ascontiguousarray
    x = i["L0_attn_x"]
    out = {"x_tm": c(x.transpose(1, 0, 2).reshape(T, D)), "ident": np.eye(P, dtype=np.float32)}
    for n, a, s in (("gate_w", "L0_ffn_gate_w", "L0_ffn_sh_gate_w"), ("up_w", "L0_ffn_up_w", "L0_ffn_sh_up_w")):
        out[n] = c(np.concatenate([i[a].reshape(-1, D), i[s]], 0).T)
    down = np.concatenate([i["L0_ffn_down_w"].transpose(0, 2, 1).reshape(-1, D), i["L0_ffn_sh_down_w"].T], 0)
    out["down_w"] = c(down.reshape(NJ, P, D).transpose(1, 0, 2))
    out["router_w"] = c(i["L0_ffn_router_weight"].T)
    out["e_bias"] = c(np.broadcast_to(i["L0_ffn_e_bias"], (P, E_ALL)))
    w = lambda n: i["L0_attn_" + n]
    halves = lambda a: c(a.reshape(2, P, -1).transpose(1, 0, 2))
    out["w_in"] = c(w("W_in").T)
    out["taps"] = c(np.broadcast_to(w("conv_w")[:, 0].T.reshape(1, -1), (P, 4 * DI)))
    out["a_log"] = c(halves(w("A_log")).reshape(P, -1))
    out["dt_w"], out["out_w"] = halves(w("W_dt").T), halves(w("W_out").T)
    out["bc_w"] = halves(np.concatenate([w("W_B"), w("W_C")], 0).T)
    for n, a in (("conv_b", "conv_b"), ("b_dt", "b_dt"), ("d_param", "D_param")):
        out[n] = c(w(a).reshape(2, P).T)
    out["residual"] = c(np.broadcast_to(w("residual_scale").reshape(1, 1), (P, 1)))
    out["x_bt"] = c(x.reshape(T, D))
    out["attn_w"] = c(np.stack([i["L1_attn_W" + n + s] for s in ("_l", "_g") for n in "qkvo"], 1))
    out["tern_w"] = c(i["L1_ffn_weight"].T)
    out["norm_w"] = c(w("norm_w").reshape(P, 1))
    return out


def constants():
    bf16 = mybir.dt.np(BF16)
    sel = np.zeros((96, 8 * P), bf16)
    for a in range(3):
        for e in range(E_ALL):
            sel[32 * a + e, (e // 2) * P + (e % 2) * 64:(e // 2) * P + (e % 2) * 64 + 64] = 1
    pick = np.zeros((96, NS), bf16)
    for a in range(3):
        pick[32 * a:32 * a + NS] = np.eye(NS)
    row, head = np.arange(P), np.arange(4)
    bmask = np.where(row[:, None] % 32 // 8 == np.arange(32) // 8, 0.0, -1e30)
    return {"jmask": (row[:, None] // 8 % 4 == head).astype(np.float32),
            "vmask": (row[:, None] // 32 == head).astype(np.float32),
            "osum": (row[:, None] // 32 == np.arange(32) // 8).astype(np.float32),
            "bmask": bmask.astype(np.float32), "moe_sel": sel, "pick": pick, "ident_b": np.eye(64).astype(bf16),
            "ones": np.ones((P, P), np.float32)}


def program(nc, io, scratch, out):
    expert_phase(nc, io, scratch)
    scan_phase(nc, io, scratch)
    attention_phase(nc, io, scratch, out)


SCRATCH = (("xnT", (P, TP)), ("xrT", (P, HALO + TP)), ("gT", (P, TP)), ("xg", (NC * P, 4 * ST)),
           ("cT", (NC * 96, ST), BF16), ("sg", (TP, D)))


def kernel(**inputs):
    import concourse.bacc as bacc
    from concourse.bass_utils import run_bass_kernel_spmd

    arrays = {**host_arrays({k: np.asarray(v) for k, v in inputs.items()}), **constants()}
    nc = bacc.Bacc("TRN2", target_bir_lowering=False, num_devices=1, dynamic_dma_scratch_size=1024)
    io = {n: nc.dram_tensor("in_" + n, a.shape, mybir.dt.from_np(a.dtype), kind="ExternalInput").ap()
          for n, a in arrays.items()}
    scratch = {n: nc.dram_tensor(n, s, *(t or (F32,)), kind="Internal").ap() for n, s, *t in SCRATCH}
    out = nc.dram_tensor("out", (T, D), F32, kind="ExternalOutput").ap()
    program(nc, io, scratch, out)
    r = run_bass_kernel_spmd(nc, [{"in_" + n: a for n, a in arrays.items()}], core_ids=[0])
    return r.results[0]["out"].reshape(B, L, D)
```
